# Optimizing a Trainium2 kernel written in Bass

```python
import numpy as np
import jax
import jax.numpy as jnp

def _softmax(x, axis=-1):
    return jax.nn.softmax(x, axis=axis)

def _gelu(x):
    return jax.nn.gelu(x, approximate=True)

def _silu(x):
    return jax.nn.silu(x)

def _sigmoid(x):
    return jax.nn.sigmoid(x)

def _layernorm(x, axis=-1, eps=1e-05):
    m = jnp.mean(x, axis=axis, keepdims=True)
    v = jnp.var(x, axis=axis, keepdims=True)
    return (x - m) / jnp.sqrt(v + eps)

def _scatter_add(tgt, idx, src, axis=0):
    return tgt.at[idx].add(src)

def _segment_sum(src, seg, n):
    return jax.ops.segment_sum(src, seg, n)
kernel_name = 'mk_lm_tower_d2_tok_ids512_r4_b8dcfc'

def setup_inputs(seed: int=0):
    np.random.seed(seed)
    _w = jnp.asarray

    def _rec_inputs():
        import jax
        import jax.numpy as jnp
        _rk = jax.random.key(seed)
        x = jax.random.randint(jax.random.fold_in(_rk, 1), (2, 1024), 0, 64, jnp.int32)
        return x
    x = _rec_inputs()

    def _L0_tok_setup():
        import jax, jax.numpy as jnp
        import numpy as np
        NGRAM_SIZES = (2, 3, 4)
        HASH_VOCAB = 25000
        EMBED_DIM = 128
        BATCH, SEQ = (8, 1024)

        def _ngram_hash_ids(byte_sequence, n):
            L = byte_sequence.shape[1] - n + 1
            h = jnp.zeros((byte_sequence.shape[0], L), dtype=jnp.int64)
            for j in range(n):
                h = (h * 64 + byte_sequence[:, j:j + L]) % HASH_VOCAB
            return h

        def _ngram_embed(byte_sequence, table, n):
            B, S = byte_sequence.shape
            ids = _ngram_hash_ids(byte_sequence, n)
            emb = table[ids]
            out = jnp.zeros((B, S, table.shape[1]), dtype=table.dtype)
            c = n // 2
            return out.at[:, c:c + emb.shape[1]].set(emb)
        key = jax.random.key(seed)
        ks = jax.random.split(key, 6)
        return {'byte_sequence': jax.random.randint(ks[0], (BATCH, SEQ), 0, 64, dtype=jnp.int64), 'emb_2': jax.random.normal(ks[1], (HASH_VOCAB, EMBED_DIM), dtype=jnp.float32), 'emb_3': jax.random.normal(ks[2], (HASH_VOCAB, EMBED_DIM), dtype=jnp.float32), 'emb_4': jax.random.normal(ks[3], (HASH_VOCAB, EMBED_DIM), dtype=jnp.float32), 'proj_w': jax.random.normal(ks[4], (EMBED_DIM, len(NGRAM_SIZES) * EMBED_DIM), dtype=jnp.float32) * 0.02, 'proj_b': jax.random.normal(ks[5], (EMBED_DIM,), dtype=jnp.float32) * 0.02}
    _L0_tok_all = _L0_tok_setup()
    _L0_tok_in = {k: v for k, v in _L0_tok_all.items() if k in ('emb_2', 'emb_3', 'emb_4', 'proj_w', 'proj_b')}
    del _L0_tok_all

    def _L0_attn_setup():
        import jax, jax.numpy as jnp
        import numpy as np
        import math
        B, S, D, H = (8, 256, 128, 8)
        DH = D // H
        SCALE_BASE = 128

        def _xpos(x, downscale):
            s = x.shape[-2]
            d = x.shape[-1]
            half = d // 2
            sv = (jnp.arange(0, d, 2, dtype=jnp.float32) + 0.4 * d) / (1.4 * d)
            power = jnp.arange(s, dtype=jnp.float32) / SCALE_BASE
            scale = sv[None, :] ** power[:, None]
            inv_freq = 1.0 / 10000.0 ** (jnp.arange(half, dtype=jnp.float32) / half)
            ang = jnp.arange(s, dtype=jnp.float32)[:, None] * inv_freq[None, :]
            if downscale:
                scale = 1.0 / scale
            sin = jnp.repeat(jnp.sin(ang) * scale, 2, axis=-1)
            cos = jnp.repeat(jnp.cos(ang) * scale, 2, axis=-1)
            rot = jnp.stack((-x[..., 1::2], x[..., ::2]), axis=-1).reshape(x.shape)
            return x * cos + rot * sin
        key = jax.random.key(seed)
        ks = jax.random.split(key, 7)
        X = jax.random.normal(ks[0], (B, S, D), dtype=jnp.float32)
        W_Q = jax.random.normal(ks[1], (H, D, DH), dtype=jnp.float32) / D
        W_K = jax.random.normal(ks[2], (H, D, DH), dtype=jnp.float32) / D
        W_V = jax.random.normal(ks[3], (H, D, DH), dtype=jnp.float32) / D
        W_G = jax.random.normal(ks[4], (D, D), dtype=jnp.float32) / D
        W_O = jax.random.normal(ks[5], (D, D), dtype=jnp.float32) / D
        gn_weight = jnp.ones((D,), dtype=jnp.float32)
        gn_bias = jnp.zeros((D,), dtype=jnp.float32)
        return {'X': X, 'W_Q': W_Q, 'W_K': W_K, 'W_V': W_V, 'W_G': W_G, 'W_O': W_O, 'gn_weight': gn_weight, 'gn_bias': gn_bias}
    _L0_attn_all = _L0_attn_setup()
    _L0_attn_in = {k: v for k, v in _L0_attn_all.items() if k in ('W_Q', 'W_K', 'W_V', 'W_G', 'W_O', 'gn_weight', 'gn_bias')}
    del _L0_attn_all

    def _L0_ffn_setup():
        import jax, jax.numpy as jnp
        import numpy as np
        B, S, D, H, E = (4, 512, 128, 256, 8)
        key = jax.random.key(seed)
        ks = jax.random.split(key, 4)
        x = jax.random.normal(ks[0], (B, S, D), jnp.float32)
        Wr = jax.random.normal(ks[1], (E, D), jnp.float32) * 0.02
        br = jnp.zeros((E,), jnp.float32)
        W1 = jax.random.normal(ks[2], (E, D, H), jnp.float32) * 0.02
        b1 = jnp.zeros((E, H), jnp.float32)
        W2 = jax.random.normal(ks[3], (E, H, D), jnp.float32) * 0.02
        b2 = jnp.zeros((E, D), jnp.float32)
        return {'x': x, 'Wr': Wr, 'br': br, 'W1': W1, 'b1': b1, 'W2': W2, 'b2': b2}
    _L0_ffn_all = _L0_ffn_setup()
    _L0_ffn_in = {k: v for k, v in _L0_ffn_all.items() if k in ('Wr', 'br', 'W1', 'b1', 'W2', 'b2')}
    del _L0_ffn_all

    def _L1_attn_setup():
        import jax, jax.numpy as jnp
        import numpy as np
        import math
        D_MODEL = 128
        NUM_HEADS = 8
        B, S = (4, 256)
        key = jax.random.key(seed)
        ks = jax.random.split(key, 9)
        s = 1.0 / math.sqrt(D_MODEL)
        return {'x': jax.random.normal(ks[0], (B, S, D_MODEL), dtype=jnp.float32), 'Wq': jax.random.normal(ks[1], (NUM_HEADS, D_MODEL, D_MODEL), dtype=jnp.float32) * s, 'bq': jax.random.normal(ks[2], (NUM_HEADS, D_MODEL), dtype=jnp.float32) * s, 'Wk': jax.random.normal(ks[3], (NUM_HEADS, D_MODEL, D_MODEL), dtype=jnp.float32) * s, 'bk': jax.random.normal(ks[4], (NUM_HEADS, D_MODEL), dtype=jnp.float32) * s, 'Wv': jax.random.normal(ks[5], (NUM_HEADS, D_MODEL, D_MODEL), dtype=jnp.float32) * s, 'bv': jax.random.normal(ks[6], (NUM_HEADS, D_MODEL), dtype=jnp.float32) * s, 'Wo': jax.random.normal(ks[7], (NUM_HEADS * D_MODEL, D_MODEL), dtype=jnp.float32) * (1.0 / math.sqrt(NUM_HEADS * D_MODEL))}
    _L1_attn_all = _L1_attn_setup()
    _L1_attn_in = {k: v for k, v in _L1_attn_all.items() if k in ('Wq', 'bq', 'Wk', 'bk', 'Wv', 'bv', 'Wo')}
    del _L1_attn_all

    def _L1_ffn_setup():
        import jax, jax.numpy as jnp
        import numpy as np
        G, H, DQK, DV, L, D_IN = (8, 16, 128, 128, 100, 128)
        FF = D_IN
        LSW = 1.0

        def _l2norm(x, d):
            n = jnp.maximum(jnp.linalg.norm(x, axis=-1, keepdims=True), 1e-12)
            return x / n * d ** 0.5
        key = jax.random.key(seed)
        ks = jax.random.split(key, 16)
        s = 0.02
        inp = {'x': jax.random.normal(ks[0], (4, 512, D_IN), dtype=jnp.float32), 'gamma_norm': jnp.ones((D_IN,), jnp.float32), 'Wq_w': jax.random.normal(ks[1], (D_IN, G * H * DQK), jnp.float32) * s, 'Wq_b': jnp.zeros((G * H * DQK,), jnp.float32), 'Wkv_w': jax.random.normal(ks[2], (D_IN, G * (DQK + DV)), jnp.float32) * s, 'Wkv_b': jnp.zeros((G * (DQK + DV),), jnp.float32), 'aw1_w': jax.random.normal(ks[3], (G * DQK, L), jnp.float32) * s, 'aw1_b': jnp.zeros((L,), jnp.float32), 'aw2_w': jax.random.normal(ks[4], (L, L), jnp.float32) * s, 'aw2_b': jnp.zeros((L,), jnp.float32), 'wz_g1': jnp.ones((G * H * DV,), jnp.float32), 'wz_w1': jax.random.normal(ks[5], (G * H * DV, 2 * FF), jnp.float32) * s, 'wz_b1': jnp.zeros((2 * FF,), jnp.float32), 'wz_g2': jnp.ones((2 * FF,), jnp.float32), 'wz_w2': jax.random.normal(ks[6], (2 * FF, FF), jnp.float32) * s, 'wz_b2': jnp.zeros((FF,), jnp.float32)}
        return inp
    _L1_ffn_all = _L1_ffn_setup()
    _L1_ffn_in = {k: v for k, v in _L1_ffn_all.items() if k in ('gamma_norm', 'Wq_w', 'Wq_b', 'Wkv_w', 'Wkv_b', 'aw1_w', 'aw1_b', 'aw2_w', 'aw2_b', 'wz_g1', 'wz_w1', 'wz_b1', 'wz_g2', 'wz_w2', 'wz_b2')}
    del _L1_ffn_all
    return {'x': x, 'L0_tok_emb_2': _L0_tok_in['emb_2'], 'L0_tok_emb_3': _L0_tok_in['emb_3'], 'L0_tok_emb_4': _L0_tok_in['emb_4'], 'L0_tok_proj_w': _L0_tok_in['proj_w'], 'L0_tok_proj_b': _L0_tok_in['proj_b'], 'L0_attn_W_Q': _L0_attn_in['W_Q'], 'L0_attn_W_K': _L0_attn_in['W_K'], 'L0_attn_W_V': _L0_attn_in['W_V'], 'L0_attn_W_G': _L0_attn_in['W_G'], 'L0_attn_W_O': _L0_attn_in['W_O'], 'L0_attn_gn_weight': _L0_attn_in['gn_weight'], 'L0_attn_gn_bias': _L0_attn_in['gn_bias'], 'L0_ffn_Wr': _L0_ffn_in['Wr'], 'L0_ffn_br': _L0_ffn_in['br'], 'L0_ffn_W1': _L0_ffn_in['W1'], 'L0_ffn_b1': _L0_ffn_in['b1'], 'L0_ffn_W2': _L0_ffn_in['W2'], 'L0_ffn_b2': _L0_ffn_in['b2'], 'L1_attn_Wq': _L1_attn_in['Wq'], 'L1_attn_bq': _L1_attn_in['bq'], 'L1_attn_Wk': _L1_attn_in['Wk'], 'L1_attn_bk': _L1_attn_in['bk'], 'L1_attn_Wv': _L1_attn_in['Wv'], 'L1_attn_bv': _L1_attn_in['bv'], 'L1_attn_Wo': _L1_attn_in['Wo'], 'L1_ffn_gamma_norm': _L1_ffn_in['gamma_norm'], 'L1_ffn_Wq_w': _L1_ffn_in['Wq_w'], 'L1_ffn_Wq_b': _L1_ffn_in['Wq_b'], 'L1_ffn_Wkv_w': _L1_ffn_in['Wkv_w'], 'L1_ffn_Wkv_b': _L1_ffn_in['Wkv_b'], 'L1_ffn_aw1_w': _L1_ffn_in['aw1_w'], 'L1_ffn_aw1_b': _L1_ffn_in['aw1_b'], 'L1_ffn_aw2_w': _L1_ffn_in['aw2_w'], 'L1_ffn_aw2_b': _L1_ffn_in['aw2_b'], 'L1_ffn_wz_g1': _L1_ffn_in['wz_g1'], 'L1_ffn_wz_w1': _L1_ffn_in['wz_w1'], 'L1_ffn_wz_b1': _L1_ffn_in['wz_b1'], 'L1_ffn_wz_g2': _L1_ffn_in['wz_g2'], 'L1_ffn_wz_w2': _L1_ffn_in['wz_w2'], 'L1_ffn_wz_b2': _L1_ffn_in['wz_b2']}

def reference(x, L0_tok_emb_2, L0_tok_emb_3, L0_tok_emb_4, L0_tok_proj_w, L0_tok_proj_b, L0_attn_W_Q, L0_attn_W_K, L0_attn_W_V, L0_attn_W_G, L0_attn_W_O, L0_attn_gn_weight, L0_attn_gn_bias, L0_ffn_Wr, L0_ffn_br, L0_ffn_W1, L0_ffn_b1, L0_ffn_W2, L0_ffn_b2, L1_attn_Wq, L1_attn_bq, L1_attn_Wk, L1_attn_bk, L1_attn_Wv, L1_attn_bv, L1_attn_Wo, L1_ffn_gamma_norm, L1_ffn_Wq_w, L1_ffn_Wq_b, L1_ffn_Wkv_w, L1_ffn_Wkv_b, L1_ffn_aw1_w, L1_ffn_aw1_b, L1_ffn_aw2_w, L1_ffn_aw2_b, L1_ffn_wz_g1, L1_ffn_wz_w1, L1_ffn_wz_b1, L1_ffn_wz_g2, L1_ffn_wz_w2, L1_ffn_wz_b2):
    import jax
    import jax.numpy as jnp

    def _L0_tok_ref(byte_sequence, emb_2, emb_3, emb_4, proj_w, proj_b):
        import jax, jax.numpy as jnp
        import numpy as np
        NGRAM_SIZES = (2, 3, 4)
        HASH_VOCAB = 25000
        EMBED_DIM = 128
        BATCH, SEQ = (8, 1024)

        def _ngram_hash_ids(byte_sequence, n):
            L = byte_sequence.shape[1] - n + 1
            h = jnp.zeros((byte_sequence.shape[0], L), dtype=jnp.int64)
            for j in range(n):
                h = (h * 64 + byte_sequence[:, j:j + L]) % HASH_VOCAB
            return h

        def _ngram_embed(byte_sequence, table, n):
            B, S = byte_sequence.shape
            ids = _ngram_hash_ids(byte_sequence, n)
            emb = table[ids]
            out = jnp.zeros((B, S, table.shape[1]), dtype=table.dtype)
            c = n // 2
            return out.at[:, c:c + emb.shape[1]].set(emb)
        tables = (emb_2, emb_3, emb_4)
        combined = jnp.concatenate([_ngram_embed(byte_sequence, t, n) for t, n in zip(tables, NGRAM_SIZES)], axis=-1)
        return jnp.einsum('bsk,dk->bsd', combined, proj_w) + proj_b

    def _L0_attn_ref(X, W_Q, W_K, W_V, W_G, W_O, gn_weight, gn_bias):
        import jax, jax.numpy as jnp
        import numpy as np
        import math
        B, S, D, H = (8, 256, 128, 8)
        DH = D // H
        SCALE_BASE = 128

        def _xpos(x, downscale):
            s = x.shape[-2]
            d = x.shape[-1]
            half = d // 2
            sv = (jnp.arange(0, d, 2, dtype=jnp.float32) + 0.4 * d) / (1.4 * d)
            power = jnp.arange(s, dtype=jnp.float32) / SCALE_BASE
            scale = sv[None, :] ** power[:, None]
            inv_freq = 1.0 / 10000.0 ** (jnp.arange(half, dtype=jnp.float32) / half)
            ang = jnp.arange(s, dtype=jnp.float32)[:, None] * inv_freq[None, :]
            if downscale:
                scale = 1.0 / scale
            sin = jnp.repeat(jnp.sin(ang) * scale, 2, axis=-1)
            cos = jnp.repeat(jnp.cos(ang) * scale, 2, axis=-1)
            rot = jnp.stack((-x[..., 1::2], x[..., ::2]), axis=-1).reshape(x.shape)
            return x * cos + rot * sin
        b, s, _ = X.shape
        gammas = 1.0 - jnp.exp(jnp.linspace(math.log(1.0 / 32), math.log(1.0 / 128), H)).astype(jnp.float32)
        n = jnp.arange(s)
        Dmat = gammas[:, None, None] ** jnp.abs(n[:, None] - n[None, :]).astype(jnp.float32)
        Q = _xpos(jnp.einsum('bsd,hde->bhse', X, W_Q), False)
        K = _xpos(jnp.einsum('bsd,hde->bhse', X, W_K), True)
        V = jnp.einsum('bsd,hde->bhse', X, W_V)
        scores = jnp.einsum('bhse,bhte->bhst', Q, K)
        p = jax.nn.softmax(scores, axis=-1) * Dmat[None]
        Y = jnp.einsum('bhst,bhte->bhse', p, V)
        Y = jnp.moveaxis(Y, 1, 2).reshape(b, s, H * DH)
        Yg = Y.reshape(-1, H, DH)
        mu = Yg.mean(axis=-1, keepdims=True)
        var = Yg.var(axis=-1, keepdims=True)
        Yn = ((Yg - mu) * jax.lax.rsqrt(var + 1e-05)).reshape(-1, H * DH)
        Yn = (Yn * gn_weight + gn_bias).reshape(b, s, H * DH)
        G = X @ W_G
        swish = G * jax.nn.sigmoid(G)
        return swish * Yn @ W_O

    def _L0_ffn_ref(x, Wr, br, W1, b1, W2, b2):
        import jax, jax.numpy as jnp
        import numpy as np
        B, S, D, H, E = (4, 512, 128, 256, 8)
        b, s, d = x.shape
        n = b * s
        e = Wr.shape[0]
        xf = x.reshape(n, d)
        logits = xf @ Wr.T + br
        probs = jax.nn.softmax(logits, axis=-1)
        top2_prob, top2_idx = jax.lax.top_k(probs, 2)
        comb = jnp.zeros((n, e), x.dtype).at[jnp.arange(n)[:, None], top2_idx].add(top2_prob)
        h = jax.nn.gelu(jnp.einsum('nd,edh->enh', xf, W1) + b1[:, None, :], approximate=False)
        o = jnp.einsum('enh,ehd->end', h, W2) + b2[:, None, :]
        y = jnp.einsum('ne,end->nd', comb, o)
        return y.reshape(b, s, d)

    def _L1_attn_ref(x, Wq, bq, Wk, bk, Wv, bv, Wo):
        import jax, jax.numpy as jnp
        import numpy as np
        import math
        D_MODEL = 128
        NUM_HEADS = 8
        B, S = (4, 256)
        q = jnp.einsum('bsd,hde->bhse', x, Wq) + bq[None, :, None, :]
        k = jnp.einsum('bsd,hde->bhse', x, Wk) + bk[None, :, None, :]
        v = jnp.einsum('bsd,hde->bhse', x, Wv) + bv[None, :, None, :]
        scores = jnp.einsum('bhqe,bhke->bhqk', q, k) / math.sqrt(D_MODEL)
        attn = jax.nn.softmax(scores, axis=-1)
        heads = jnp.einsum('bhqk,bhke->bhqe', attn, v)
        concat = heads.transpose(0, 2, 1, 3).reshape(heads.shape[0], heads.shape[2], -1)
        return concat @ Wo

    def _L1_ffn_ref(x, gamma_norm, Wq_w, Wq_b, Wkv_w, Wkv_b, aw1_w, aw1_b, aw2_w, aw2_b, wz_g1, wz_w1, wz_b1, wz_g2, wz_w2, wz_b2):
        import jax, jax.numpy as jnp
        import numpy as np
        G, H, DQK, DV, L, D_IN = (8, 16, 128, 128, 100, 128)
        FF = D_IN
        LSW = 1.0

        def _l2norm(x, d):
            n = jnp.maximum(jnp.linalg.norm(x, axis=-1, keepdims=True), 1e-12)
            return x / n * d ** 0.5
        b, s, d = x.shape
        xn = _l2norm(x, d) * gamma_norm
        q = (xn @ Wq_w + Wq_b).reshape(b, s, G, H, DQK)
        kv = xn @ Wkv_w + Wkv_b
        k, v = (kv[..., :G * DQK], kv[..., G * DQK:])
        w = jax.nn.silu(k @ aw1_w + aw1_b) @ aw2_w + aw2_b
        w1 = jax.nn.softmax(w, axis=-1) / s
        w2 = jax.nn.softmax(w, axis=-2) / L * LSW
        w = (w1 + w2) / (1.0 + LSW)
        kc = jnp.einsum('bsd,bsl->bld', k, w).reshape(b, L, G, DQK)
        vc = jnp.einsum('bsd,bsl->bld', v, w).reshape(b, L, G, DV)
        qk = jnp.einsum('bsghd,blgd->bghsl', q, kc) * (1.0 / DQK ** 0.5)
        att = jax.nn.softmax(qk, axis=-1)
        z = jnp.einsum('bghsl,blgd->bsghd', att, vc).reshape(b, s, G * H * DV)
        zn = _l2norm(z, G * H * DV) * wz_g1
        h1 = jax.nn.silu(zn @ wz_w1 + wz_b1)
        h1n = _l2norm(h1, 2 * FF) * wz_g2
        out = jax.nn.silu(h1n @ wz_w2 + wz_b2)
        return out
    h = _L0_tok_ref(x, L0_tok_emb_2, L0_tok_emb_3, L0_tok_emb_4, L0_tok_proj_w, L0_tok_proj_b)
    h = h + _L0_attn_ref(_layernorm(h, axis=-1), L0_attn_W_Q, L0_attn_W_K, L0_attn_W_V, L0_attn_W_G, L0_attn_W_O, L0_attn_gn_weight, L0_attn_gn_bias)
    h = h + _L0_ffn_ref(_layernorm(h, axis=-1), L0_ffn_Wr, L0_ffn_br, L0_ffn_W1, L0_ffn_b1, L0_ffn_W2, L0_ffn_b2)
    h = h + _L1_attn_ref(_layernorm(h, axis=-1), L1_attn_Wq, L1_attn_bq, L1_attn_Wk, L1_attn_bk, L1_attn_Wv, L1_attn_bv, L1_attn_Wo)
    h = h + _L1_ffn_ref(_layernorm(h, axis=-1), L1_ffn_gamma_norm, L1_ffn_Wq_w, L1_ffn_Wq_b, L1_ffn_Wkv_w, L1_ffn_Wkv_b, L1_ffn_aw1_w, L1_ffn_aw1_b, L1_ffn_aw2_w, L1_ffn_aw2_b, L1_ffn_wz_g1, L1_ffn_wz_w1, L1_ffn_wz_b1, L1_ffn_wz_g2, L1_ffn_wz_w2, L1_ffn_wz_b2)
    return h

_drawn_inputs = setup_inputs


def setup_inputs(seed=0):
    import zlib

    import numpy as np

    out = dict(_drawn_inputs(seed))
    spreads = {'L0_attn_gn_weight': (1.0, 0.6),
     'L0_attn_gn_bias': (0.0, 0.8),
     'L0_ffn_br': (0.0, 0.1),
     'L0_ffn_b1': (0.0, 0.438),
     'L0_ffn_b2': (0.0, 0.1),
     'L1_ffn_gamma_norm': (1.0, 0.2),
     'L1_ffn_Wq_b': (0.0, 2.0),
     'L1_ffn_Wkv_b': (0.0, 0.1),
     'L1_ffn_aw1_b': (0.0, 2.0),
     'L1_ffn_aw2_b': (0.0, 2.0),
     'L1_ffn_wz_g1': (1.0, 0.2),
     'L1_ffn_wz_b1': (0.0, 0.515),
     'L1_ffn_wz_g2': (1.0, 0.2),
     'L1_ffn_wz_b2': (0.0, 0.1)}
    factors = {'L0_attn_W_Q': 8.0,
     'L0_attn_W_K': 8.0,
     'L0_attn_W_V': 8.0,
     'L0_attn_W_G': 8.0,
     'L0_attn_W_O': 8.0,
     'L1_attn_bk': 200.0,
     'L1_ffn_Wq_w': 200.0,
     'L1_ffn_aw1_w': 64.0,
     'L1_ffn_aw2_w': 64.0,
     'L0_ffn_W1': 2.948,
     'L1_attn_bq': 2.744}
    for name, (base, spread) in spreads.items():
        noise = np.random.default_rng([zlib.crc32(name.encode()), seed]).standard_normal(out[name].shape)
        drawn = base * np.exp(spread * noise) if base else spread * noise
        out[name] = jnp.asarray(drawn.astype(out[name].dtype))
    for name, factor in factors.items():
        out[name] = (out[name] * factor).astype(out[name].dtype)
    return out
```

```python
from contextlib import ExitStack

import numpy as np

import concourse.bass as bass
from concourse import mybir

F32 = mybir.dt.float32
F32R = mybir.dt.float32r
PARTS = ((0, 0), (0, 1), (1, 0))
BF16 = mybir.dt.bfloat16
I32 = mybir.dt.int32
U32 = mybir.dt.uint32
ALU = mybir.AluOpType
ACT = mybir.ActivationFunctionType
AX = mybir.AxisListType

P = 128
B, S, D = 2, 1024, 128
NT = B * S // P
TB = S // P
BANK = 512
H = 8
DH = D // H
VOCAB = 25000
E, FH = 8, 256
G, GH = 8, 16
L = 100
QH = 4
NQ = G * GH // QH
FF2 = 2 * D
START = 1
SCORE_PARTS = ((0, 0), (0, 1), (1, 0), (1, 1), (0, 2), (2, 0), (1, 2), (2, 1))
DMA_SEMS = ("_in", "_loaded", "gathered", "stored")
GAMMAS = (1.0 - np.exp(np.linspace(np.log(1.0 / 32), np.log(1.0 / 128), H))).astype(np.float32)


class Chain:

    def __init__(self, eng, sem, base=0):
        self.eng, self.sem, self.base, self.n = eng, sem, base, 0

    def mark(self, ins):
        self.n += 1
        ins.then_inc(self.sem, 1)

    def then(self, ins):
        self.n += 1
        ins.then_inc(self.sem, 1)
        self.eng.wait_ge(self.sem, START + self.base + self.n)


class Core:

    def __init__(self, nc, ctx, tag):
        self.nc, self.ctx, self.tag, self.sems, self.primed = nc, ctx, tag, [], []

    def sb(self, name, shape, dt=F32):
        return self.ctx.enter_context(self.nc.sbuf_tensor(f"{self.tag}_{name}", shape, dt))

    def ps(self, name, shape):
        return self.ctx.enter_context(self.nc.psum_tensor(f"{self.tag}_{name}", shape, F32))

    def sem(self, name):
        if not self.sems:
            self.ctx.callback(self.clear)
        self.sems.append(self.nc.alloc_semaphore(f"{self.tag}_{name}"))
        if not name.rstrip("0123456789").endswith(DMA_SEMS):
            self.primed.append(self.sems[-1])
        return self.sems[-1]

    def start(self):
        engines = (self.nc.sync, self.nc.gpsimd, self.nc.vector, self.nc.tensor, self.nc.scalar)
        for n, sem in enumerate(self.primed):
            engines[n % len(engines)].sem_inc(sem, START)
        self.nc.all_engine_barrier()

    def clear(self):
        self.nc.clear_and_free_semaphores(self.sems)
        self.nc.all_engine_barrier()


class Norm:

    def __init__(self, core, h, ident, xT, psT, l2=None, xr=None):
        self.nc, self.h, self.ident, self.xT, self.psT, self.l2 = core.nc, h, ident, xT, psT, l2
        self.xr = xr
        self.xc = core.sb("xc", [P, NT, D])
        self.sq = core.sb("sq", [P, NT, D])
        self.stat = core.sb("stat", [P, 6, NT])
        self.eps = core.sb("eps", [P, 1])
        self.chain = core.sem("norm_chain")
        self.squares = core.sem("norm_squares")
        self.var_ready = core.sem("norm_var_ready")
        self.root = core.sem("norm_root")
        self.centred = core.sem("norm_centred")
        self.scaled = core.sem("norm_scaled")
        self.turned = core.sem("norm_turned")
        self.xT_ready = core.sem("norm_xT_ready")
        self.xr_ready = core.sem("norm_xr_ready")
        self.high = core.sem("norm_high")

    def vector(self, e):
        nc, c = self.nc, Chain(e, self.chain)
        tot, mean, var, root, inv = (self.stat[:, i, :] for i in range(5))
        wide = lambda a: a.unsqueeze(2).to_broadcast([P, NT, D])
        c.then(nc.vector.memset(self.eps[:], 1e-5))
        c.then(nc.vector.tensor_reduce(tot, self.h[:], AX.X, ALU.add))
        c.then(nc.vector.tensor_scalar(mean, tot, 1.0 / D, None, ALU.mult))
        nc.vector.tensor_tensor(self.xc[:], self.h[:], wide(mean), ALU.subtract).then_inc(self.centred, 1)
        e.wait_ge(self.squares, START + 1)
        nc.vector.tensor_reduce(var, self.sq[:], AX.X, ALU.add).then_inc(self.var_ready, 1)
        e.wait_ge(self.root, START + 1)
        c.then(nc.vector.reciprocal(inv, root))
        e.wait_ge(self.centred, START + 1)
        if self.l2 is None:
            nc.vector.tensor_tensor(self.xc[:], self.xc[:], wide(inv), ALU.mult).then_inc(self.scaled, 1)
            if self.xr is not None:
                for g in range(NT // 4):
                    cols = slice(g * BANK, (g + 1) * BANK)
                    e.wait_ge(self.high, START + g + 1)
                    e.wait_ge(self.xT_ready, START + g + 1)
                    nc.vector.tensor_tensor(self.xr[:, 1, cols], self.xT[:, cols], self.xr[:, 0, cols].bitcast(F32),
                                            ALU.subtract).then_inc(self.xr_ready, 1)
            return
        nc.vector.tensor_tensor(self.xc[:], self.xc[:], wide(inv), ALU.mult).then_inc(self.centred, 1)
        e.wait_ge(self.squares, START + 2)
        nc.vector.tensor_reduce(var, self.sq[:], AX.X, ALU.add).then_inc(self.var_ready, 1)
        e.wait_ge(self.root, START + 2)
        c.then(nc.vector.tensor_scalar(root, root, 1e-12, None, ALU.max))
        c.then(nc.vector.reciprocal(inv, root))
        c.then(nc.vector.tensor_scalar(inv, inv, float(D) ** 0.5, None, ALU.mult))
        e.wait_ge(self.centred, START + 2)
        nc.vector.tensor_tensor(self.xc[:], self.xc[:], wide(inv), ALU.mult).then_inc(self.scaled, 1)

    def scalar(self, e):
        nc = self.nc
        var, root = self.stat[:, 2, :], self.stat[:, 3, :]
        for n in range(1 if self.l2 is None else 2):
            e.wait_ge(self.centred, START + n + 1)
            nc.scalar.activation(self.sq[:], self.xc[:], ACT.Square).then_inc(self.squares, 1)
            e.wait_ge(self.var_ready, START + n + 1)
            if n == 0:
                nc.scalar.activation(root, var, ACT.Sqrt, bias=self.eps[:], scale=1.0 / D).then_inc(self.root, 1)
            else:
                nc.scalar.activation(root, var, ACT.Sqrt).then_inc(self.root, 1)
        for g in range(NT // 4):
            e.wait_ge(self.turned, START + g + 1)
            dst, src = self.xT[:, g * BANK:(g + 1) * BANK], self.psT[:, g % 2, :]
            if self.xr is not None:
                nc.scalar.copy(self.xr[:, 0, g * BANK:(g + 1) * BANK], src).then_inc(self.high, 1)
            if self.l2 is None:
                nc.scalar.copy(dst, src).then_inc(self.xT_ready, 1)
            else:
                nc.scalar.mul(dst, src, self.l2).then_inc(self.xT_ready, 1)

    def tensor(self, e):
        e.wait_ge(self.scaled, START + 1)
        for g in range(NT // 4):
            if g >= 2:
                e.wait_ge(self.xT_ready, START + g - 1)
            for k in range(4):
                mm = e.transpose(self.psT[:, g % 2, k * P:(k + 1) * P], self.xc[:, 4 * g + k, :], self.ident[:])
            mm.then_inc(self.turned, 1)


def embed(nc, io, keep):
    GT = 4
    with ExitStack() as ctx:
        m = Core(nc, ctx, "emb")
        tok_i = m.sb("tok_i", [P, 4, NT], I32)
        tok = m.sb("tok", [P, 4, NT])
        hash_f = m.sb("hash_f", [P, 3, NT])
        quot = m.sb("quot", [P, NT])
        quot_i = m.sb("quot_i", [P, NT], I32)
        fix = m.sb("fix", [P, NT])
        ids = m.sb("ids", [P, 3 * NT], U32)
        mask = m.sb("mask", [P, NT, 3])
        proj = m.sb("proj", [P, 3, D])
        bias = m.sb("bias", [P, D])
        rows = m.sb("rows", [P, NT, 3, D])
        rowsM = m.sb("rowsM", [P, 3, D])
        rowsT = m.sb("rowsT", [P, 3, D])
        ps_t = m.ps("ps_t", [P, 3 * D])
        ps_h = m.ps("ps_h", [P, D])
        tok_in, proj_in, ident_in = m.sem("tok_in"), m.sem("proj_in"), m.sem("ident_in")
        chain, ids_ready = m.sem("chain"), m.sem("ids_ready")
        gathered = [m.sem(f"gathered{g}") for g in range(NT // GT)]
        masked, turned, rows_ready, projected, h_ready = (
            m.sem(n) for n in ("masked", "turned", "rows_ready", "projected", "h_ready"))
        m.start()
        block = ctx.enter_context(nc.Block())

        @block.sync
        def _(e):
            e.dma_start(tok_i[:], io["tok"]).then_inc(tok_in, 16)
            e.dma_start(mask[:], io["tok_mask"]).then_inc(proj_in, 16)
            e.dma_start(keep["ident"][:], io["ident"]).then_inc(ident_in, 16)
            e.dma_start(proj[:], io["proj_wT"]).then_inc(proj_in, 16)
            e.dma_start(bias[:], io["proj_b"].partition_broadcast(P)).then_inc(proj_in, 16)

        @block.gpsimd
        def _(e):
            e.wait_ge(ids_ready, START + 1)
            for t in range(NT):
                for n in range(3):
                    nc.gpsimd.indirect_dma_start(
                        out=rows[:, t, n, :], out_offset=None, in_=io[f"emb_{n + 2}"],
                        in_offset=bass.IndirectOffsetOnAxis(ap=ids[:, n * NT + t:n * NT + t + 1], axis=0),
                    ).then_inc(gathered[t // GT], 16)

        @block.vector
        def _(e):
            c = Chain(e, chain)

            def push(dst, src, nxt):
                c.then(nc.vector.tensor_scalar(dst, src, 64.0, None, ALU.mult))
                c.then(nc.vector.tensor_tensor(dst, dst, nxt, ALU.add))
                c.then(nc.vector.tensor_scalar(quot_i[:], dst, 1.0 / VOCAB, None, ALU.mult))
                c.then(nc.vector.tensor_copy(quot[:], quot_i[:]))
                c.then(nc.vector.tensor_scalar(quot[:], quot[:], float(VOCAB), None, ALU.mult))
                c.then(nc.vector.tensor_tensor(dst, dst, quot[:], ALU.subtract))
                c.then(nc.vector.tensor_scalar(fix[:], dst, 0.0, float(VOCAB), ALU.is_lt, ALU.mult))
                c.then(nc.vector.tensor_tensor(dst, dst, fix[:], ALU.add))
                c.then(nc.vector.tensor_scalar(fix[:], dst, float(VOCAB), float(VOCAB), ALU.is_ge, ALU.mult))
                c.then(nc.vector.tensor_tensor(dst, dst, fix[:], ALU.subtract))

            e.wait_ge(tok_in, 16)
            c.then(nc.vector.tensor_copy(tok[:], tok_i[:]))
            push(hash_f[:, 0, :], tok[:, 1, :], tok[:, 2, :])
            push(hash_f[:, 1, :], hash_f[:, 0, :], tok[:, 3, :])
            push(hash_f[:, 2, :], tok[:, 0, :], tok[:, 1, :])
            push(hash_f[:, 2, :], hash_f[:, 2, :], tok[:, 2, :])
            push(hash_f[:, 2, :], hash_f[:, 2, :], tok[:, 3, :])
            nc.vector.tensor_copy(ids[:], hash_f[:].rearrange("p n t -> p (n t)")).then_inc(ids_ready, 1)
            e.wait_ge(proj_in, 48)
            for g in range(NT // GT):
                e.wait_ge(gathered[g], 16 * 3 * GT)
                with e.Fori(0, GT) as i:
                    t = i + g * GT
                    e.wait_ge(turned, START + t)
                    nc.vector.tensor_tensor(
                        rowsM[:], rows[:, g * GT:(g + 1) * GT][:, bass.ds(i, 1)].rearrange("p a n d -> p (a n) d"),
                        mask[:, bass.ds(t, 1), :].rearrange("p a n -> p (a n)").unsqueeze(2).to_broadcast([P, 3, D]),
                        ALU.mult).then_inc(masked, 1)
                    e.wait_ge(projected, START + t + 1)
                    nc.vector.tensor_tensor(keep["h"][:, bass.ds(t, 1), :].rearrange("p a d -> p (a d)"),
                                            ps_h[:], bias[:], ALU.add).then_inc(h_ready, 1)

        @block.tensor
        def _(e):
            e.wait_ge(ident_in, 16)
            e.wait_ge(proj_in, 48)
            with e.Fori(0, NT) as t:
                e.wait_ge(masked, START + t + 1)
                e.wait_ge(rows_ready, START + t)
                for n in range(3):
                    mm = e.transpose(ps_t[:, n * D:(n + 1) * D], rowsM[:, n, :], keep["ident"][:])
                mm.then_inc(turned, 1)
                e.wait_ge(rows_ready, START + t + 1)
                e.wait_ge(h_ready, START + t)
                for n in range(3):
                    mm = e.matmul(ps_h[:], rowsT[:, n, :], proj[:, n, :], start=(n == 0), stop=(n == 2))
                mm.then_inc(projected, 1)

        @block.scalar
        def _(e):
            with e.Fori(0, NT) as t:
                e.wait_ge(turned, START + t + 1)
                e.wait_ge(projected, START + t)
                nc.scalar.copy(rowsT[:].rearrange("p n d -> p (n d)"), ps_t[:]).then_inc(rows_ready, 1)


class Attention:

    def __init__(self, m, split):
        self.parts = PARTS if split else ((0, 0),)
        count = 2 if split else 1
        self.psS = m.ps("psS", [P, 2, 2, BANK])
        self.psT = m.ps("psT", [P, 2, BANK])
        self.psO = m.ps("psO", [P, 2, BANK])
        self.probs = m.sb("probs", [P, 3, S])
        self.probsT = m.sb("probsT", [P, count, TB, S], F32R if split else F32)
        self.negmax = m.sb("negmax", [P, TB])
        self.total = m.sb("total", [P, TB])
        self.scores_ready = m.sem("scores_ready")
        self.max_ready = m.sem("max_ready")
        self.probs_ready = m.sem("probs_ready")
        self.turned = m.sem("turned")
        self.high_ready = [m.sem(f"high_ready{q}") for q in range(2)]
        self.probsT_ready = [m.sem(f"probsT_ready{q}") for q in range(2)]
        self.heads_ready = m.sem("heads_ready")

    def score(self, e, n, i, products):
        e.wait_ge(self.probs_ready, START + n * TB + max(0, i - 1))
        for c in range(2):
            pairs = products(i, c)
            for j, (lhsT, rhs) in enumerate(pairs):
                mm = e.matmul(self.psS[:, i % 2, c, :], lhsT, rhs, start=(j == 0), stop=(j == len(pairs) - 1))
        mm.then_inc(self.scores_ready, 1)

    def turn(self, e, n, i, ident):
        e.wait_ge(self.probs_ready, START + n * TB + (i + 1))
        for half in range(2):
            e.wait_ge(self.probsT_ready[half], START + n * TB + i)
            for j in range(4):
                mm = e.transpose(self.psT[:, half, j * P:(j + 1) * P],
                                 self.probs[:, i % 3, (4 * half + j) * P:(4 * half + j + 1) * P], ident)
            mm.then_inc(self.turned, 1)

    def gather(self, e, v, c, t, start):
        last = len(self.parts) - 1
        for j, (v_part, p_part) in enumerate(self.parts):
            mm = e.matmul(self.psO[:, c, :], v[:, v_part, t, :], self.probsT[:, p_part, t, c * BANK:(c + 1) * BANK],
                          start=(start and t == 0 and j == 0), stop=(start and t == TB - 1 and j == last),
                          skip_group_check=not start)
        if t == TB - 1:
            mm.then_inc(self.heads_ready, 1)

    def rest(self, e, n, products, v, ident, start, psO_free, after_turn, among_gathers=None):
        for i in range(TB):
            if i + 2 < TB:
                self.score(e, n, i + 2, products)
            self.turn(e, n, i, ident)
            after_turn(i)
            if i >= 4:
                if i == 4:
                    for half in range(2):
                        e.wait_ge(self.probsT_ready[half], START + n * TB + 4)
                    psO_free()
                self.gather(e, v, 0, 2 * (i - 4), start)
                self.gather(e, v, 0, 2 * (i - 4) + 1, start)
        for half in range(2):
            e.wait_ge(self.probsT_ready[half], START + n * TB + TB)
        for t in range(TB):
            if t == TB // 2 and among_gathers is not None:
                among_gathers()
            self.gather(e, v, 1, t, start)

    def maxima(self, e, n, i, ahead=0):
        if i == 0:
            e.wait_ge(self.probs_ready, START + n * TB)
        e.wait_ge(self.scores_ready, START + n * TB + (ahead + i + 1))
        e.tensor_reduce(self.negmax[:, i:i + 1], self.psS[:, i % 2].rearrange("p a b -> p (a b)"),
                        AX.X, ALU.max, negate=True).then_inc(self.max_ready, 1)

    def exponentials(self, e, n, i, ahead=0):
        e.wait_ge(self.turned, START + n * 2 * TB + max(0, 2 * (i - 2)))
        e.wait_ge(self.max_ready, START + n * TB + (ahead + i + 1))
        e.activation(self.probs[:, i % 3, :], self.psS[:, i % 2].rearrange("p a b -> p (a b)"), ACT.Exp,
                     bias=self.negmax[:, i:i + 1],
                     accum_out=self.total[:, i:i + 1]).then_inc(self.probs_ready, 1)

    def turned_half(self, i, half):
        return ([self.probsT[:, part, 4 * half:4 * half + 4, i * P:(i + 1) * P] for part in range(len(self.parts[:2]))],
                self.psT[:, half, :].rearrange("p (j s) -> p j s", j=4))


def retention(nc, io, keep):
    h, ident, xT = keep["h"], keep["ident"], keep["xT"]
    with ExitStack() as ctx:
        m = Core(nc, ctx, "ret")
        at = Attention(m, split=False)
        norm = Norm(m, h, ident, xT, at.psT)
        wq, wqr, wk, wkr, wo = (m.sb(n, [P, D]) for n in ("wq", "wqr", "wk", "wkr", "wo"))
        wvg = m.sb("wvg", [P, 2 * D])
        heads_mask = m.sb("heads_mask", [P, H + 1])
        heads_row = m.sb("heads_row", [P, H, D])
        gn_w, gn_b = m.sb("gn_w", [P, D]), m.sb("gn_b", [P, D])
        log_gamma = m.sb("log_gamma", [P, H + 1])
        log_gamma_head = m.sb("log_gamma_head", [P, 1])
        xpos = m.sb("xpos", [P, 2, S])
        full = m.sb("full", [P, 4, BANK])
        qk_parts = m.sb("qk_parts", [P, 2, 3, B * S], BF16)
        pattern = m.sb("pattern", [P, 2 * 3, P])
        pick = m.sb("pick", [P, 2 * 3, P], BF16)
        q_head, k_head = m.sb("q_head", [P, S], BF16), m.sb("k_head", [P, S], BF16)
        vals = m.sb("vals", [P, NT, D])
        gate = m.sb("gate", [P, NT, D])
        v_head = m.sb("v_head", [P, 1, TB, D])
        dist = m.sb("dist", [P, 2 * TB - 1, P])
        decay = m.sb("decay", [P, 2 * TB - 1, P])
        heads = m.sb("heads", [P, S])
        zeros = m.sb("zeros", [P, P])
        yt = m.sb("yt", [P, TB, H, DH])
        totals = m.sb("totals", [P, B, H, TB])
        gs = m.sb("gs", [P, 4, TB, H])
        gn_eps = m.sb("gn_eps", [P, 1])
        names = ("log_gamma_ready weights_in consts_in xpos_q_in xpos_k_in chain pool_chain dist_ready proj_ready proj_used q_ready k_ready "
                 "xpos_free vg_ready vg_used head_ready v_head_ready decay_ready init_done heads_copied "
                 "part_made rest_made pick_ready q_picked k_picked q_kept k_kept y_turned y_ready gn_sq gn_var gn_root gated g_turned gT_ready out_ready totals_kept out_added dve_chain").split()
        s = {n: m.sem(n) for n in names}
        sq = norm.sq
        m.start()
        block = ctx.enter_context(nc.Block())
        units = lambda b, hh: hh + b * H

        @block.sync
        def _(e):
            for dst, src in ((wq, "WQ"), (wqr, "WQ_rot"), (wk, "WK"), (wkr, "WK_rot"), (wvg, "WVG"), (wo, "WO_0")):
                e.dma_start(dst[:], io[src]).then_inc(s["weights_in"], 16)
            e.dma_start(xpos[:], io["xpos_q"]).then_inc(s["xpos_q_in"], 16)
            e.dma_start(heads_mask[:], io["heads_mask"]).then_inc(s["consts_in"], 16)
            e.dma_start(pattern[:], io["pattern"]).then_inc(s["consts_in"], 16)
            e.dma_start(heads_row[:], io["heads_row"].partition_broadcast(P)).then_inc(s["consts_in"], 16)
            e.dma_start(log_gamma[:], io["log_gamma"].partition_broadcast(P)).then_inc(s["consts_in"], 16)
            e.dma_start(gn_w[:], io["gn_w"].partition_broadcast(P)).then_inc(s["consts_in"], 16)
            e.dma_start(gn_b[:], io["gn_b"].partition_broadcast(P)).then_inc(s["consts_in"], 16)
            e.wait_ge(s["q_ready"], START + 4)
            e.dma_start(xpos[:], io["xpos_k"]).then_inc(s["xpos_k_in"], 16)

        @block.gpsimd
        def _(e):
            c = Chain(e, s["pool_chain"])
            c.then(nc.gpsimd.iota(decay[:].bitcast(I32), [[P, 2 * TB - 1], [-1, P]], base=-(TB - 1) * P,
                                  channel_multiplier=1))
            c.then(nc.gpsimd.tensor_copy(dist[:], decay[:].bitcast(I32)))
            c.then(nc.gpsimd.tensor_scalar(decay[:], dist[:], -1.0, None, ALU.mult))
            nc.gpsimd.memset(zeros[:], 0.0).then_inc(s["dist_ready"], 1)
            for i in range(8):
                for part in range(2):
                    e.wait_ge(s["part_made"], START + 3 * i + part + 1)
                    nc.gpsimd.tensor_tensor(full[:, i % 4], full[:, i % 4], qk_parts[:, i // 4, part, i % 4 * BANK:(i % 4 + 1) * BANK],
                                            ALU.subtract).then_inc(s["rest_made"], 1)
            e.wait_ge(s["consts_in"], 96)

            def make_pick(hh):
                nc.gpsimd.tensor_tensor(pick[:].rearrange("p m r -> p (m r)"), pattern[:].rearrange("p m r -> p (m r)"),
                                        heads_mask[:, bass.ds(hh, 1)].to_broadcast([P, 6 * P]), ALU.mult).then_inc(s["pick_ready"], 1)
            for b in range(B):
                e.wait_ge(s["vg_used"], START + NT)
                if b > 0:
                    e.wait_ge(s["k_picked"], START + b * (H + 1))
                make_pick(0)
                with e.Fori(0, H) as hh:
                    n = units(b, hh)
                    e.wait_ge(at.heads_ready, START + 2 * n)
                    nc.gpsimd.tensor_tensor(v_head[:, 0], vals[:, b * TB:(b + 1) * TB, :],
                                            heads_row[:, bass.ds(hh, 1), :].to_broadcast([P, TB, D]),
                                            ALU.mult).then_inc(s["v_head_ready"], 1)
                    e.wait_ge(s["k_picked"], START + b * (H + 1) + hh + 1)
                    make_pick(hh + 1)

        @block.vector
        def _(e):
            e.wait_ge(s["dist_ready"], START + 1)
            c = Chain(e, s["dve_chain"])
            c.then(nc.vector.tensor_tensor(dist[:], dist[:], decay[:], ALU.max))
            c.then(nc.vector.memset(gn_eps[:], 1e-5))
            norm.vector(e)
            for n, (ready, tables) in enumerate((("q_ready", "xpos_q_in"), ("k_ready", "xpos_k_in"))):
                e.wait_ge(s[tables], 16)
                for ch in range(4):
                    i, dst, pos = 4 * n + ch, full[:, ch], slice(ch % 2 * BANK, (ch % 2 + 1) * BANK)
                    e.wait_ge(s["proj_ready"], START + i + 1)
                    if i >= 4:
                        e.wait_ge(s["part_made"], START + 3 * (i - 3))
                    c.then(nc.vector.tensor_tensor(dst, at.psS[:, i % 2, 0, :], xpos[:, 0, pos], ALU.mult))
                    nc.vector.tensor_tensor(heads[:, 0:BANK], at.psS[:, i % 2, 1, :], xpos[:, 1, pos],
                                            ALU.mult).then_inc(s["proj_used"], 1)
                    e.wait_ge(s["proj_used"], START + i + 1)
                    nc.vector.tensor_tensor(dst, dst, heads[:, 0:BANK], ALU.add).then_inc(s[ready], 1)
                    e.wait_ge(s[ready], START + ch + 1)
            e.wait_ge(s["consts_in"], 96)

            def choose_decay(hh, count):
                e.wait_ge(s["decay_ready"], START + count)
                e.tensor_scalar(log_gamma_head[:], log_gamma[:, bass.ds(hh, 1)], 1.0, None, ALU.mult).then_inc(
                    s["log_gamma_ready"], 1)

            def keep_keys(count, used):
                e.wait_ge(s["k_picked"], START + count)
                e.wait_ge(at.scores_ready, START + used)
                e.tensor_copy(k_head[:], at.psS[:, 1].rearrange("p a b -> p (a b)")).then_inc(s["k_kept"], 1)
            for b in range(B):
                choose_decay(0, b * (H + 1))
                keep_keys(b * (H + 1) + 1, b * (H * TB + 2))
                at.maxima(e, b * H, 0, ahead=2 * b)
                at.maxima(e, b * H, 1, ahead=2 * b)
                with e.Fori(0, H) as hh:
                    n = units(b, hh)
                    for i in range(TB):
                        if i + 2 < TB:
                            at.maxima(e, n, i + 2, ahead=2 * b)
                        if i == 0:
                            e.wait_ge(at.heads_ready, START + 2 * n)
                        for half in range(2):
                            (dst,), src = at.turned_half(i, half)
                            first = 4 * half - i + TB - 1
                            e.wait_ge(s["decay_ready"], START + b * (H + 1) + hh + 1)
                            e.wait_ge(at.turned, START + n * 2 * TB + (2 * i + half + 1))
                            e.tensor_tensor(dst, src, decay[:, first:first + 4, :], ALU.mult).then_inc(
                                at.probsT_ready[half], 1)
                    e.wait_ge(at.probs_ready, START + n * TB + TB)
                    e.tensor_copy(totals[:, b, bass.ds(hh, 1), :], at.total[:].unsqueeze(1)).then_inc(s["totals_kept"], 1)
                    choose_decay(hh + 1, b * (H + 1) + hh + 1)
                    keep_keys(b * (H + 1) + hh + 2, n * TB + (2 * b + TB))
                    at.maxima(e, n + 1, 0, ahead=2 * b)
                    at.maxima(e, n + 1, 1, ahead=2 * b)
                wide = lambda a: a.unsqueeze(3).to_broadcast([P, TB, H, DH])
                e.wait_ge(s["totals_kept"], START + (b + 1) * H)
                e.wait_ge(s["y_ready"], START + 2 * b + 2)
                c.then(e.reciprocal(gs[:, 0], totals[:, b].rearrange("p h t -> p t h")))
                c.then(e.tensor_tensor(yt[:], yt[:], wide(gs[:, 0]), ALU.mult))
                c.then(e.tensor_reduce(gs[:, 1], yt[:], AX.X, ALU.add))
                c.then(e.tensor_scalar(gs[:, 1], gs[:, 1], 1.0 / DH, None, ALU.mult))
                c.then(e.tensor_tensor(yt[:], yt[:], wide(gs[:, 1]), ALU.subtract))
                sq4 = sq[:, 0:TB, :].rearrange("p t (h e) -> p t h e", h=H)
                c.then(e.tensor_tensor(sq4, yt[:], yt[:], ALU.mult))
                e.tensor_reduce(gs[:, 2], sq4, AX.X, ALU.add).then_inc(s["gn_var"], 1)
                e.wait_ge(s["gn_root"], START + b + 1)
                c.then(e.reciprocal(gs[:, 0], gs[:, 3]))
                c.then(e.tensor_tensor(yt[:], yt[:], wide(gs[:, 0]), ALU.mult))
                y3 = yt[:].rearrange("p t h e -> p t (h e)")
                row = lambda a: a[:].unsqueeze(1).to_broadcast([P, TB, D])
                c.then(e.tensor_tensor(y3, y3, row(gn_w), ALU.mult))
                c.then(e.tensor_tensor(y3, y3, row(gn_b), ALU.add))
                e.tensor_tensor(y3, y3, gate[:, b * TB:(b + 1) * TB, :], ALU.mult).then_inc(s["gated"], 1)
                for half in range(2):
                    e.wait_ge(s["out_ready"], START + 2 * b + half + 1)
                    hv = h[:, b * TB + 4 * half:b * TB + 4 * half + 4, :]
                    e.tensor_tensor(hv, at.psO[:, half, :].rearrange("p (t d) -> p t d", t=4), hv,
                                    ALU.add).then_inc(s["out_added"], 1)

        @block.tensor
        def _(e):
            norm.tensor(e)
            e.wait_ge(s["weights_in"], 96)
            for n, (w, wr) in enumerate(((wq, wqr), (wk, wkr))):
                for ch in range(4):
                    i, cols = 4 * n + ch, slice(ch * BANK, (ch + 1) * BANK)
                    e.wait_ge(norm.xT_ready, START + ch + 1)
                    if i >= 2:
                        e.wait_ge(s["proj_used"], START + i - 1)
                    e.matmul(at.psS[:, i % 2, 0, :], w[:], xT[:, cols], start=True, stop=True)
                    e.matmul(at.psS[:, i % 2, 1, :], wr[:], xT[:, cols], start=True, stop=True).then_inc(s["proj_ready"], 1)
            for t in range(NT):
                if t >= 2:
                    e.wait_ge(s["vg_used"], START + t - 1)
                e.matmul(at.psO[:, t % 2, 0:2 * D], xT[:, t * P:(t + 1) * P], wvg[:], start=True,
                         stop=True).then_inc(s["vg_ready"], 1)
            e.wait_ge(s["proj_used"], START + 8)
            e.wait_ge(s["vg_used"], START + NT)
            e.wait_ge(s["dist_ready"], START + 1)

            def pick_head(which, b, picked):
                for c in range(2):
                    for part in range(3):
                        mm = e.matmul(at.psS[:, which, c, :], pick[:, 3 * which + part, :],
                                      qk_parts[:, which, part, b * S + c * BANK:b * S + (c + 1) * BANK],
                                      start=(part == 0), stop=(part == 2))
                mm.then_inc(picked, 1)

            def products(i, c):
                return [(q_head[:, i * P:(i + 1) * P], k_head[:, c * BANK:(c + 1) * BANK])]

            def first_scores(n, count):
                e.wait_ge(s["q_kept"], START + count)
                e.wait_ge(s["k_kept"], START + count)
                for i in range(2):
                    at.score(e, n, i, products)

            e.wait_ge(s["part_made"], START + 24)
            for b in range(B):
                e.wait_ge(s["pick_ready"], START + b * (H + 1) + 1)
                if b > 0:
                    e.wait_ge(at.max_ready, START + b * (H * TB + 2))
                pick_head(0, b, s["q_picked"])
                pick_head(1, b, s["k_picked"])
                first_scores(b * H, b * (H + 1) + 1)
                e.wait_ge(s["out_added"], START + 2 * b)
                for c in range(2):
                    e.matmul(at.psO[:, c, :], zeros[:], xT[:, 0:BANK], start=True, stop=False, skip_group_check=True)
                with e.Fori(0, H) as hh:
                    n = units(b, hh)

                    def next_head(i):
                        if i == TB - 2:
                            e.wait_ge(s["pick_ready"], START + b * (H + 1) + hh + 2)
                            pick_head(0, b, s["q_picked"])
                        if i == TB - 1:
                            pick_head(1, b, s["k_picked"])
                    at.rest(e, n, products, v_head, ident[:], start=False,
                            psO_free=lambda: e.wait_ge(s["v_head_ready"], START + n + 1), after_turn=next_head,
                            among_gathers=lambda: first_scores(n + 1, b * (H + 1) + hh + 2))
                for c in range(2):
                    e.matmul(at.psO[:, c, :], zeros[:], xT[:, 0:BANK], start=False, stop=True,
                             skip_group_check=True).then_inc(s["init_done"], 1)
                for half in range(2):
                    e.wait_ge(s["heads_copied"], START + 2 * b + half + 1)
                    for j in range(4):
                        t = 4 * half + j
                        mm = e.transpose(at.psT[:, half, j * P:(j + 1) * P], heads[:, t * P:(t + 1) * P], ident[:])
                    mm.then_inc(s["y_turned"], 1)
                e.wait_ge(s["gated"], START + b + 1)
                for half in range(2):
                    for j in range(4):
                        mm = e.transpose(at.psT[:, half, j * P:(j + 1) * P],
                                         yt[:, 4 * half + j].rearrange("p h e -> p (h e)"), ident[:])
                    mm.then_inc(s["g_turned"], 1)
                for half in range(2):
                    e.wait_ge(s["gT_ready"], START + 2 * b + half + 1)
                    for j in range(4):
                        t = 4 * half + j
                        mm = e.matmul(at.psO[:, half, j * P:(j + 1) * P], heads[:, t * P:(t + 1) * P], wo[:],
                                      start=True, stop=True)
                    mm.then_inc(s["out_ready"], 1)

        @block.scalar
        def _(e):
            norm.scalar(e)
            for i in range(8):
                e.wait_ge(s[("q_ready", "k_ready")[i // 4]], START + i % 4 + 1)
                for part in range(3):
                    if part > 0:
                        e.wait_ge(s["rest_made"], START + 2 * i + part)
                    e.copy(qk_parts[:, i // 4, part, i % 4 * BANK:(i % 4 + 1) * BANK], full[:, i % 4]).then_inc(s["part_made"], 1)
            for t in range(NT):
                e.wait_ge(s["vg_ready"], START + t + 1)
                nc.scalar.copy(vals[:, t, :], at.psO[:, t % 2, 0:D])
                nc.scalar.activation(gate[:, t, :], at.psO[:, t % 2, D:2 * D], ACT.Silu).then_inc(s["vg_used"], 1)
            e.wait_ge(s["consts_in"], 96)

            def make_decay(count, used):
                for half in range(2):
                    e.wait_ge(at.probsT_ready[half], START + used)
                e.wait_ge(s["log_gamma_ready"], START + count)
                e.activation(decay[:], dist[:], ACT.Exp, scale=log_gamma_head[:]).then_inc(s["decay_ready"], 1)

            def keep_queries(count, used):
                e.wait_ge(s["q_picked"], START + count)
                e.wait_ge(at.scores_ready, START + used)
                e.copy(q_head[:], at.psS[:, 0].rearrange("p a b -> p (a b)")).then_inc(s["q_kept"], 1)
            for b in range(B):
                make_decay(b * (H + 1) + 1, b * H * TB)
                keep_queries(b * (H + 1) + 1, b * (H * TB + 2))
                with e.Fori(0, H) as hh:
                    n = units(b, hh)
                    e.wait_ge(s["totals_kept"], START + n)
                    for i in range(TB):
                        at.exponentials(e, n, i, ahead=2 * b)
                    keep_queries(b * (H + 1) + hh + 2, n * TB + (2 * b + TB))
                    make_decay(b * (H + 1) + hh + 2, n * TB + TB)
                for half in range(2):
                    e.wait_ge(s["init_done"], START + 2 * b + half + 1)
                    e.copy(heads[:, half * BANK:(half + 1) * BANK], at.psO[:, half, :]).then_inc(s["heads_copied"], 1)
                for half in range(2):
                    e.wait_ge(s["y_turned"], START + 2 * b + half + 1)
                    e.copy(yt[:, 4 * half:4 * half + 4].rearrange("p t h e -> p (t h e)"),
                           at.psT[:, half, :]).then_inc(s["y_ready"], 1)
                e.wait_ge(s["gn_var"], START + b + 1)
                e.activation(gs[:, 3], gs[:, 2], ACT.Sqrt, bias=gn_eps[:], scale=1.0 / DH).then_inc(s["gn_root"], 1)
                for half in range(2):
                    e.wait_ge(s["g_turned"], START + 2 * b + half + 1)
                    e.copy(heads[:, half * BANK:(half + 1) * BANK], at.psT[:, half, :]).then_inc(s["gT_ready"], 1)


def experts(nc, io, keep):
    h, ident, xT = keep["h"], keep["ident"], keep["xT"]
    with ExitStack() as ctx:
        m = Core(nc, ctx, "moe")
        ps_t = m.ps("ps_t", [P, 2, BANK])
        ps_hid = m.ps("ps_hid", [P, 2, 2, BANK])
        ps_out = m.ps("ps_out", [P, 2, 4, D])
        norm = Norm(m, h, ident, xT, ps_t)
        wr = m.sb("wr", [P, E])
        br = m.sb("br", [P, E])
        w1 = m.sb("w1", [P, E, FH])
        b1 = m.sb("b1", [P, E, 2])
        w2 = m.sb("w2", [P, E, 2, D])
        b2 = m.sb("b2", [E, D])
        rank = m.sb("rank", [P, E])
        prob, left, hit, pick, comb = (m.sb(n, [P, NT, E]) for n in ("prob", "left", "hit", "pick", "comb"))
        best = m.sb("best", [P, NT])
        combT = m.sb("combT", [E, B * S])
        hid = m.sb("hid", [P, 2, 2, BANK])
        weights_in, logits_ready, chain, exp_asked, exp_out, comb_ready, combT_turned, combT_ready, bias_ready, bias_added = (
            m.sem(n) for n in "weights_in logits_ready chain exp_asked exp_out comb_ready combT_turned combT_ready bias_ready bias_added".split())
        hid_ready, hid_gelu, out_ready, out_added = (m.sem(n) for n in "hid_ready hid_gelu out_ready out_added".split())
        NC = B * S // BANK
        m.start()
        block = ctx.enter_context(nc.Block())

        @block.sync
        def _(e):
            for dst, src in ((wr, "Wr"), (w1, "W1"), (b1, "b1"), (w2, "W2"), (b2, "b2")):
                e.dma_start(dst[:], io[src]).then_inc(weights_in, 16)
            e.dma_start(br[:], io["br"].partition_broadcast(P)).then_inc(weights_in, 16)
            e.dma_start(rank[:], io["rank"].partition_broadcast(P)).then_inc(weights_in, 16)

        @block.tensor
        def _(e):
            norm.tensor(e)
            e.wait_ge(weights_in, 16 * 7)
            e.wait_ge(norm.xT_ready, START + NT // 4)
            for t in range(NT):
                mm = e.matmul(ps_out[:, 0, 0, t * E:(t + 1) * E], xT[:, t * P:(t + 1) * P], wr[:], start=True, stop=True)
            mm.then_inc(logits_ready, 1)
            e.wait_ge(comb_ready, START + 1)
            for c in range(NC):
                if c >= 2:
                    e.wait_ge(combT_ready, START + c - 1)
                for j in range(4):
                    mm = e.transpose(ps_t[0:E, c % 2, j * P:(j + 1) * P], comb[:, 4 * c + j, :], ident[:])
                mm.then_inc(combT_turned, 1)
            for c in range(NC):
                e.wait_ge(combT_ready, START + c + 1)
                if c >= 2:
                    e.wait_ge(bias_added, START + c - 1)
                for j in range(4):
                    t = 4 * c + j
                    mm = e.matmul(ps_out[:, c % 2, j, :], combT[:, t * P:(t + 1) * P], b2[:], start=True, stop=True)
                mm.then_inc(bias_ready, 1)
            with e.Fori(0, NC) as c:
                def out(x):
                    e.wait_ge(hid_gelu, START + c * E + (x + 1))
                    if x == 0:
                        e.wait_ge(bias_added, START + NC)
                    e.wait_ge(out_added, START + c * E + max(0, x - 1))
                    for j in range(4):
                        for k in range(2):
                            mm = e.matmul(ps_out[:, x % 2, j, :], hid[:, x % 2, k, j * P:(j + 1) * P], w2[:, x, k, :],
                                          start=(k == 0), stop=(k == 1))
                    mm.then_inc(out_ready, 1)
                for x in range(E):
                    e.wait_ge(hid_gelu, START + c * E + max(0, x - 1))
                    for k in range(2):
                        mm = e.matmul(ps_hid[:, x % 2, k, :], w1[:, x, k * P:(k + 1) * P], xT[:, bass.ds(c * BANK, BANK)],
                                      start=True, stop=True)
                    mm.then_inc(hid_ready, 1)
                    if x:
                        out(x - 1)
                out(E - 1)

        @block.scalar
        def _(e):
            norm.scalar(e)
            e.wait_ge(exp_asked, START + 1)
            e.activation(prob[:], prob[:], ACT.Exp).then_inc(exp_out, 1)
            for c in range(NC):
                e.wait_ge(combT_turned, START + c + 1)
                e.copy(combT[:, c * BANK:(c + 1) * BANK], ps_t[0:E, c % 2, :]).then_inc(combT_ready, 1)
            with e.Fori(0, NC) as c:
                for x in range(E):
                    e.wait_ge(hid_ready, START + c * E + (x + 1))
                    e.wait_ge(out_ready, START + c * E + max(0, x - 1))
                    for k in range(2):
                        act = e.activation(hid[:, x % 2, k, :], ps_hid[:, x % 2, k, :], ACT.Gelu, bias=b1[:, x, k:k + 1])
                    act.then_inc(hid_gelu, 1)

        @block.vector
        def _(e):
            norm.vector(e)
            c = Chain(e, chain)
            wide = lambda a: a.unsqueeze(2).to_broadcast([P, NT, E])
            row = lambda a: a[:].unsqueeze(1).to_broadcast([P, NT, E])
            e.wait_ge(logits_ready, START + 1)
            c.then(e.tensor_tensor(prob[:], ps_out[:, 0, 0, 0:NT * E].rearrange("p (t x) -> p t x", t=NT), row(br), ALU.add))
            c.then(e.tensor_reduce(best[:], prob[:], AX.X, ALU.max))
            e.tensor_tensor(prob[:], prob[:], wide(best[:]), ALU.subtract).then_inc(exp_asked, 1)
            e.wait_ge(exp_out, START + 1)
            c.then(e.tensor_reduce(best[:], prob[:], AX.X, ALU.add))
            c.then(e.reciprocal(best[:], best[:]))
            c.then(e.tensor_tensor(prob[:], prob[:], wide(best[:]), ALU.mult))
            c.then(e.tensor_copy(left[:], prob[:]))
            for n in range(2):
                c.then(e.tensor_reduce(best[:], left[:], AX.X, ALU.max))
                c.then(e.tensor_tensor(hit[:], left[:], wide(best[:]), ALU.is_equal))
                c.then(e.tensor_tensor(hit[:], hit[:], row(rank), ALU.mult))
                c.then(e.tensor_reduce(best[:], hit[:], AX.X, ALU.max))
                c.then(e.tensor_tensor(pick[:], hit[:], wide(best[:]), ALU.is_equal))
                if n == 0:
                    c.then(e.tensor_tensor(comb[:], pick[:], prob[:], ALU.mult))
                    c.then(e.tensor_scalar(pick[:], pick[:], 4.0, None, ALU.mult))
                    c.then(e.tensor_tensor(left[:], left[:], pick[:], ALU.subtract))
                else:
                    c.then(e.tensor_tensor(pick[:], pick[:], prob[:], ALU.mult))
                    e.tensor_tensor(comb[:], comb[:], pick[:], ALU.add).then_inc(comb_ready, 1)
            for q in range(NC):
                e.wait_ge(bias_ready, START + q + 1)
                hv = h[:, 4 * q:4 * q + 4, :]
                e.tensor_tensor(hv, ps_out[:, q % 2], hv, ALU.add).then_inc(bias_added, 1)
            e.wait_ge(bias_added, START + NC)
            e.wait_ge(comb_ready, START + 1)
            with e.Fori(0, NC) as q:
                for x in range(E):
                    e.wait_ge(out_ready, START + q * E + (x + 1))
                    e.wait_ge(out_added, START + q * E + x)
                    for j in range(4):
                        hv = h[:, bass.ds(q * 4 + j, 1), :].rearrange("p a d -> p (a d)")
                        add = e.scalar_tensor_tensor(hv, ps_out[:, x % 2, j, :],
                                                     comb[:, bass.ds(q * 4 + j, 1), x:x + 1].rearrange("p a x -> p (a x)"),
                                                     hv, ALU.mult, ALU.add)
                    add.then_inc(out_added, 1)


def attention(nc, io, keep):
    h, ident, xT = keep["h"], keep["ident"], keep["xT"]
    with ExitStack() as ctx:
        m = Core(nc, ctx, "mha")
        at = Attention(m, split=True)
        xr = m.sb("xr", [P, 2, NT * P], F32R)
        norm = Norm(m, h, ident, xT, at.psT, xr=xr)
        wqk = m.sb("wqk", [P, H + 1, 2, D])
        wqk_parts = m.sb("wqk_parts", [P, 2, H + 1, 2, D], F32R)
        wqk_head = m.sb("wqk_head", [P, 2, 2, D], F32R)
        wv, wo = m.sb("wv", [P, H + 1, D]), m.sb("wo", [P, H, D])
        bqk = m.sb("bqk", [P, 2, H + 1])
        bv = m.sb("bv", [P, H + 1, D])
        bqk_head = m.sb("bqk_head", [P, 2])
        q, k = m.sb("q", [P, 2, S], F32R), m.sb("k", [P, 2, S], F32R)
        v_full = m.sb("v_full", [P, TB * D])
        v = m.sb("v", [P, 2, TB, D], F32R)
        headT = m.sb("headT", [P, S])
        inv = m.sb("inv", [P, TB])
        (weights_in, pool_chain, split_ready, bias_ready, w_ready, q_ready, k_ready, v_ready, q_high, k_high, v_high,
         q_used, k_used, v_full_ready, v_used, headT_ready, out_ready, out_added, inv_ready) = (
             m.sem(n) for n in (
                 "weights_in pool_chain split_ready bias_ready w_ready q_ready k_ready v_ready q_high k_high v_high "
                 "q_used k_used v_full_ready v_used headT_ready out_ready out_added inv_ready").split())
        SCALE = float(D) ** -0.5
        m.start()
        block = ctx.enter_context(nc.Block())
        after = lambda hh, b: (hh + (b + 1) // B, (b + 1) % B)

        @block.sync
        def _(e):
            for dst, src in ((wqk, "Wqk"), (wv, "Wv"), (wo, "Wo"), (bqk, "bqk")):
                e.dma_start(dst[:], io[src]).then_inc(weights_in, 16)
            e.dma_start(bv[:], io["bv"].partition_broadcast(P)).then_inc(weights_in, 16)

        @block.gpsimd
        def _(e):
            c = Chain(e, pool_chain)
            e.wait_ge(weights_in, 80)
            c.then(nc.gpsimd.tensor_scalar(wqk[:, :, 0, :], wqk[:, :, 0, :], SCALE, None, ALU.mult))
            c.then(nc.gpsimd.tensor_scalar(bqk[:, 0, :], bqk[:, 0, :], SCALE, None, ALU.mult))
            c.then(nc.gpsimd.tensor_copy(wqk_parts[:, 0], wqk[:]))
            c.then(nc.gpsimd.tensor_tensor(wqk_parts[:, 1], wqk[:], wqk_parts[:, 0].bitcast(F32), ALU.subtract))

            def head_weights(j):
                for part in range(2):
                    cp = nc.gpsimd.tensor_copy(wqk_head[:, part], wqk_parts[:, part, bass.ds(j, 1)].rearrange("p a w d -> p (a w) d"))
                cp.then_inc(w_ready, 1)

            def low_values(n):
                e.wait_ge(v_high, START + n + 1)
                nc.gpsimd.tensor_tensor(v[:, 1].rearrange("p t d -> p (t d)"), v_full[:],
                                        v[:, 0].rearrange("p t d -> p (t d)").bitcast(F32), ALU.subtract).then_inc(v_used, 1)
            head_weights(0)
            low_values(0)
            with e.Fori(0, H) as hh:
                for b in range(B):
                    n = hh * B + b
                    if b == 1:
                        e.wait_ge(k_ready, START + n + 1)
                        head_weights(hh + 1)
                    low_values(n + 1)

        @block.tensor
        def _(e):
            cols = lambda b, c: slice(b * S + c * BANK, b * S + (c + 1) * BANK)

            def project(which, b, ready):
                for c in range(2):
                    for j, (w_part, x_part) in enumerate(PARTS):
                        mm = e.matmul(at.psS[:, which, c, :], wqk_head[:, w_part, which, :], xr[:, x_part, cols(b, c)],
                                      start=(j == 0), stop=(j == 2))
                mm.then_inc(ready, 1)

            def values(hh, b):
                for t in range(TB):
                    mm = e.matmul(at.psT[:, t // 4, t % 4 * P:(t % 4 + 1) * P], xT[:, (b * TB + t) * P:(b * TB + t + 1) * P],
                                  wv[:, bass.ds(hh, 1), :].rearrange("p a d -> p (a d)"), start=True, stop=True)
                mm.then_inc(v_ready, 1)

            def output(hh, n, half):
                e.wait_ge(headT_ready, START + n * 2 + (half + 1))
                for t in range(4 * half, 4 * half + 4):
                    mm = e.matmul(at.psO[:, half, t % 4 * P:(t % 4 + 1) * P], headT[:, t * P:(t + 1) * P],
                                  wo[:, bass.ds(hh, 1), :].rearrange("p a d -> p (a d)"), start=True, stop=True)
                mm.then_inc(out_ready, 1)

            def products(i, c):
                return [(q[:, q_part, i * P:(i + 1) * P], k[:, k_part, c * BANK:(c + 1) * BANK]) for q_part, k_part in PARTS]

            def first_scores(n):
                e.wait_ge(q_used, START + n + 1)
                e.wait_ge(k_used, START + n + 1)
                for i in range(2):
                    at.score(e, n, i, products)

            norm.tensor(e)
            e.wait_ge(norm.xT_ready, START + NT // 4)
            e.wait_ge(norm.xr_ready, START + NT // 4)
            e.wait_ge(weights_in, 80)
            e.wait_ge(w_ready, START + 1)
            project(0, 0, q_ready)
            project(1, 0, k_ready)
            values(0, 0)
            first_scores(0)
            with e.Fori(0, H) as hh:
                for b in range(B):
                    n = hh * B + b
                    hh1, b1 = after(hh, b)

                    def values_ready():
                        e.wait_ge(v_used, START + n + 1)
                        e.wait_ge(out_added, START + 2 * n)

                    def next_unit(i):
                        if i == TB - 2:
                            if b == 1:
                                e.wait_ge(w_ready, START + hh1 + 1)
                            project(0, b1, q_ready)
                        if i == TB - 1:
                            project(1, b1, k_ready)

                    e.wait_ge(v_full_ready, START + n + 1)
                    at.rest(e, n, products, v, ident[:], start=True, psO_free=values_ready, after_turn=next_unit)
                    values(hh1, b1)
                    first_scores(n + 1)
                    output(hh, n, 0)
                    output(hh, n, 1)

        @block.scalar
        def _(e):
            def high(n, which, dst, ready, high_sem):
                e.wait_ge(ready, START + n + 1)
                e.activation(dst[:, 0], at.psS[:, which].rearrange("p a b -> p (a b)"), ACT.Identity,
                             bias=bqk_head[:, which:which + 1]).then_inc(high_sem, 1)

            def turned_copy(n, i):
                for half in range(2):
                    (dst, _), src = at.turned_half(i, half)
                    e.wait_ge(at.turned, START + n * 2 * TB + (2 * i + half + 1))
                    e.copy(dst, src).then_inc(at.high_ready[half], 1)

            def high_values(n):
                e.wait_ge(v_full_ready, START + n + 1)
                e.copy(v[:, 0].rearrange("p t d -> p (t d)"), v_full[:]).then_inc(v_high, 1)

            norm.scalar(e)
            e.wait_ge(bias_ready, START + 1)
            high(0, 0, q, q_ready, q_high)
            high(0, 1, k, k_ready, k_high)
            high_values(0)
            with e.Fori(0, H) as hh:
                for b in range(B):
                    n = hh * B + b
                    e.wait_ge(inv_ready, START + n)
                    for i in range(TB):
                        at.exponentials(e, n, i)
                        if i >= 1:
                            turned_copy(n, i - 1)
                    if b == 1:
                        e.wait_ge(bias_ready, START + hh + 2)
                    high(n + 1, 0, q, q_ready, q_high)
                    turned_copy(n, TB - 1)
                    high(n + 1, 1, k, k_ready, k_high)
                    for c in range(2):
                        e.wait_ge(at.heads_ready, START + n * 2 + c + 1)
                        e.wait_ge(out_ready, START + n * 2)
                        e.copy(headT[:, c * BANK:(c + 1) * BANK], at.psO[:, c, :]).then_inc(headT_ready, 1)
                    high_values(n + 1)

        @block.vector
        def _(e):
            def biases(j):
                e.tensor_copy(bqk_head[:], bqk[:, :, bass.ds(j, 1)].rearrange("p w a -> p (w a)")).then_inc(bias_ready, 1)

            def low(n, which, dst, high_sem, used):
                e.wait_ge(high_sem, START + n + 1)
                e.scalar_tensor_tensor(dst[:, 1], at.psS[:, which].rearrange("p a b -> p (a b)"), bqk_head[:, which:which + 1],
                                       dst[:, 0].bitcast(F32), ALU.add, ALU.subtract).then_inc(used, 1)

            def values(j, n):
                e.wait_ge(v_ready, START + n + 1)
                e.tensor_tensor(v_full[:].rearrange("p (t d) -> p t d", t=TB), at.psT[:].rearrange("p a (j d) -> p (a j) d", j=4),
                                bv[:, bass.ds(j, 1), :].to_broadcast([P, TB, D]), ALU.add).then_inc(v_full_ready, 1)

            norm.vector(e)
            e.wait_ge(w_ready, START + 1)
            biases(0)
            e.wait_ge(bias_ready, START + 1)
            low(0, 0, q, q_high, q_used)
            low(0, 1, k, k_high, k_used)
            values(0, 0)
            at.maxima(e, 0, 0)
            at.maxima(e, 0, 1)
            with e.Fori(0, H) as hh:
                for b in range(B):
                    n = hh * B + b
                    hh1, b1 = after(hh, b)
                    for i in range(TB):
                        if i + 2 < TB:
                            at.maxima(e, n, i + 2)
                        if i == TB - 1:
                            if b == 1:
                                e.wait_ge(k_used, START + n + 1)
                                biases(hh1)
                                e.wait_ge(bias_ready, START + hh1 + 1)
                            low(n + 1, 0, q, q_high, q_used)
                        for half in range(2):
                            (high_part, low_part), src = at.turned_half(i, half)
                            e.wait_ge(at.high_ready[half], START + n * TB + (i + 1))
                            e.tensor_tensor(low_part, src, high_part.bitcast(F32), ALU.subtract).then_inc(at.probsT_ready[half], 1)
                    low(n + 1, 1, k, k_high, k_used)
                    e.wait_ge(at.probs_ready, START + n * TB + TB)
                    e.reciprocal(inv[:], at.total[:]).then_inc(inv_ready, 1)
                    values(hh1, n + 1)
                    at.maxima(e, n + 1, 0)
                    at.maxima(e, n + 1, 1)
                    e.wait_ge(inv_ready, START + n + 1)
                    for half in range(2):
                        e.wait_ge(out_ready, START + n * 2 + half + 1)
                        for j in range(4):
                            t = 4 * half + j
                            hv = h[:, b * TB + t, :]
                            add = e.scalar_tensor_tensor(hv, at.psO[:, half, j * P:(j + 1) * P], inv[:, t:t + 1], hv,
                                                         ALU.mult, ALU.add)
                        add.then_inc(out_added, 1)


def latent(nc, io, keep):
    h, ident, xT = keep["h"], keep["ident"], keep["xT"]
    HL = QH * L
    NS = NQ * TB
    with ExitStack() as ctx:
        m = Core(nc, ctx, "lat")
        ps_h = m.ps("ps_h", [P, TB, FF2])
        ps_s = m.ps("ps_s", [P, 2, BANK])
        ps_t = m.ps("ps_t", [P, BANK])
        ps_z = m.ps("ps_z", [P, BANK])
        gamma = m.sb("gamma", [P, 1])
        norm = Norm(m, h, ident, xT, ps_s, l2=gamma[:])
        xn = norm.xc
        kcT = m.sb("kcT", [P, B * G + 1, L])
        vcT = m.sb("vcT", [P, B * G + 1, L])
        vc = m.sb("vc", [L, 2, B * G, D], F32R)
        xr = m.sb("xr", [P, 2, NT * P], F32R)
        g1 = m.sb("g1", [P, NQ + 1, QH])
        qbias = m.sb("qbias", [P, B * G + 1, L])
        quad_mask = m.sb("quad_mask", [P, 4, QH])
        ones16 = m.sb("ones16", [P, P], mybir.dt.bfloat16)
        zero = m.sb("zero", [P, P])
        ones = m.sb("ones", [P, 1])
        zsq = m.sb("zsq", [P, 2, BANK])
        zz = m.sb("zz", [P, TB, BANK])
        b1, b2 = m.sb("b1", [P, FF2]), m.sb("b2", [P, D])
        w2 = m.sb("w2", [P, 2, D])
        g2 = m.sb("g2", [P, 2])
        consts_in, gamma_in, setup, setup_act, setup_pe, setup_pool, exp_asked, exp_out, tok_asked, tok_exped = (m.sem(n) for n in (
            "consts_in gamma_in setup setup_act setup_pe setup_pool exp_asked exp_out tok_asked tok_exped").split())

        with ExitStack() as early:
            m1 = Core(nc, early, "latw")
            wkv = m1.sb("wkv", [P, 2 * G * D])
            wkT = m1.sb("wkT", [P, G, D])
            aw1 = m1.sb("aw1", [P, G, L])
            bkv_row = m1.sb("bkv_row", [1, 2 * G * D])
            bk = m1.sb("bk", [P, G])
            aw1_b, aw2_b = m1.sb("aw1_b", [L, 1]), m1.sb("aw2_b", [L, 1])
            aw2 = m1.sb("aw2", [L, L])
            bq = m1.sb("bq", [P, G, P])
            wa = m1.sb("wa", [P, L])
            hb = m1.sb("hb", [L, 1])
            hidT = m1.sb("hidT", [L, B * S])
            wT = m1.sb("wT", [L, B * S])
            eT = m1.sb("eT", [L, B * S])
            vc_full = m1.sb("vc_full", [L, B * G * D])
            st = m1.sb("st", [L, 4, B])
            w_tok, e_tok = m1.sb("w_tok", [P, NT, L]), m1.sb("e_tok", [P, NT, L])
            tk = m1.sb("tk", [P, 2, NT])
            u = m1.sb("u", [P, B, L])
            wsum = m1.sb("wsum", [1, B, L])
            part = m1.sb("part", [P, 2], F32)
            part16 = m1.sb("part16", [P, B * G, L], mybir.dt.bfloat16)
            rest = m1.sb("rest", [P, B * G, L])
            ps_n = ps_h[:].rearrange("p a b -> p (a b)")
            bank = lambda i: ps_n[:, i * BANK:(i + 1) * BANK]
            dve_chain = m1.sem("dve_chain")
            x_high, v_high = m1.sem("x_high"), m1.sem("v_high")
            m.start()
            m1.start()
            block = early.enter_context(nc.Block())

            @block.sync
            def _(e):
                e.dma_start(gamma[:], io["gamma"]).then_inc(gamma_in, 16)
                for dst, src in ((wkT, "WkT"), (aw1, "aw1"), (bk, "bk"), (aw1_b, "aw1_b"), (aw2, "aw2"), (aw2_b, "aw2_b"),
                                 (wkv, "Wkv"), (bkv_row, "bkv"), (bq, "bq_parts"), (g1, "g1"), (quad_mask, "quad_mask"),
                                 (part, "part"), (w2, "w2"), (g2, "g2")):
                    e.dma_start(dst[:], io[src]).then_inc(consts_in, 16)
                e.dma_start(b1[:], io["wz_b1"].partition_broadcast(P)).then_inc(consts_in, 16)
                e.dma_start(b2[:], io["wz_b2"].partition_broadcast(P)).then_inc(consts_in, 16)

            @block.gpsimd
            def _(e):
                for dst in (zero[:], kcT[:, B * G:, :], vcT[:, B * G:, :], qbias[:, B * G:, :]):
                    nc.gpsimd.memset(dst, 0.0)
                nc.gpsimd.memset(ones[:], 1.0)
                nc.gpsimd.memset(zz[:], 0.0)
                nc.gpsimd.memset(zsq[:], 0.0)
                ms = nc.gpsimd.memset(ones16[:], 1.0)
                ms.then_inc(setup_pool, 1)

            @block.tensor
            def _(e):
                c = Chain(e, setup_pe)
                norm.tensor(e)
                e.wait_ge(consts_in, 256)
                for g in range(G):
                    e.matmul(bank(0)[:, 0:L], wkT[:, g, :], aw1[:, g, :], start=(g == 0), stop=(g == G - 1))
                for g in range(G):
                    mm = e.matmul(bank(1)[0:L, 0:1], aw1[:, g, :], bk[:, g:g + 1], start=(g == 0), stop=(g == G - 1))
                c.mark(mm)
                e.wait_ge(norm.xT_ready, START + NT // 4)
                e.wait_ge(setup, START + 1)
                for ch in range(4):
                    if ch >= 2:
                        e.wait_ge(setup_act, START + ch - 1)
                    c.mark(e.matmul(bank(2 + ch % 2)[0:L, :], wa[:], xT[:, ch * BANK:(ch + 1) * BANK], start=True, stop=True))
                for ch in range(4):
                    e.wait_ge(setup_act, START + (4 if ch < 2 else 4 + ch - 1))
                    c.mark(e.matmul(bank(ch % 2)[0:L, :], aw2[:], hidT[:, ch * BANK:(ch + 1) * BANK], start=True, stop=True))
                e.wait_ge(setup_act, START + 8)
                for t in range(NT):
                    mm = e.transpose(bank(2 + t // 4 % 2)[:, t % 4 * L:(t % 4 + 1) * L], wT[:, t * P:(t + 1) * P], ident[0:L, 0:L])
                    if t % 4 == 3:
                        c.mark(mm)
                        if t // 4 in (1, 2):
                            e.wait_ge(setup_act, START + 8 + t // 4)
                e.wait_ge(setup, START + 2)
                e.wait_ge(setup_act, START + 12)
                for t in range(NT):
                    mm = e.transpose(bank(2 + t // 4 % 2)[:, t % 4 * L:(t % 4 + 1) * L], eT[:, t * P:(t + 1) * P], ident[0:L, 0:L])
                    if t % 4 == 3:
                        c.mark(mm)
                        if t // 4 in (1, 2):
                            e.wait_ge(setup_act, START + 12 + t // 4)
                e.wait_ge(setup, START + 3)
                e.wait_ge(setup_pool, START + 1)
                for b in range(B):
                    for t in range(TB):
                        mm = e.matmul(bank(0)[:, b * L:(b + 1) * L], xn[:, b * TB + t, :], w_tok[:, b * TB + t, :],
                                      start=(t == 0), stop=(t == TB - 1))
                    for t in range(TB):
                        mm = e.matmul(bank(1)[0:1, b * L:(b + 1) * L], ones[:], w_tok[:, b * TB + t, :],
                                      start=(t == 0), stop=(t == TB - 1))
                c.mark(mm)
                e.wait_ge(setup_act, START + 18)
                for i in range(3 * B * G // 4):
                    if i >= 2:
                        e.wait_ge(setup_act, START + 18 + i - 1)
                    dst = bank(i % 2)
                    what, bg = divmod(i, B * G // 4)
                    b, g = divmod(4 * bg, G)
                    if what < 2:
                        for j in range(4):
                            cols = slice((what * G + g + j) * D, (what * G + g + j + 1) * D)
                            e.matmul(dst[:, j * L:(j + 1) * L], wkv[:, cols], u[:, b, :], start=True, stop=False)
                            mm = e.matmul(dst[:, j * L:(j + 1) * L], bkv_row[:, cols], wsum[:, b, :], start=False, stop=True)
                    else:
                        cols = slice((G + g) * D, (G + g + 4) * D)
                        e.matmul(dst[0:L, :], u[:, b, :], wkv[:, cols], start=True, stop=False)
                        mm = e.matmul(dst[0:L, :], wsum[:, b, :], bkv_row[:, cols], start=False, stop=True)
                    c.mark(mm)
                e.wait_ge(setup_act, START + 30)
                for bg in range(B * G):
                    mm = e.matmul(bank(bg // 4)[:, bg % 4 * L:(bg % 4 + 1) * L], bq[:, bg % G, :], kcT[:, bg, :], start=True, stop=True)
                c.mark(mm)

            @block.scalar
            def _(e):
                done = lambda ins: ins.then_inc(setup_act, 1)
                e.wait_ge(gamma_in, 16)
                norm.scalar(e)
                for ch in range(4):
                    e.wait_ge(setup_pe, START + 2 + ch)
                    done(e.activation(hidT[:, ch * BANK:(ch + 1) * BANK], bank(2 + ch % 2)[0:L, :], ACT.Silu, bias=hb[:]))
                for ch in range(4):
                    e.wait_ge(setup_pe, START + 6 + ch)
                    done(e.activation(wT[:, ch * BANK:(ch + 1) * BANK], bank(ch % 2)[0:L, :], ACT.Identity, bias=aw2_b[:]))
                e.copy(xr[:, 0], xT[:]).then_inc(x_high, 1)
                e.wait_ge(exp_asked, START + 1)
                e.activation(eT[:], eT[:], ACT.Exp).then_inc(exp_out, 1)
                for g in range(4):
                    e.wait_ge(setup_pe, START + 10 + g)
                    done(e.copy(w_tok[:, 4 * g:4 * g + 4, :].rearrange("p t l -> p (t l)"), bank(2 + g % 2)[:, 0:4 * L]))
                e.wait_ge(tok_asked, START + 1)
                e.activation(w_tok[:], w_tok[:], ACT.Exp).then_inc(tok_exped, 1)
                for g in range(4):
                    e.wait_ge(setup_pe, START + 14 + g)
                    done(e.copy(e_tok[:, 4 * g:4 * g + 4, :].rearrange("p t l -> p (t l)"), bank(2 + g % 2)[:, 0:4 * L]))
                e.wait_ge(setup_pe, START + 18)
                done(e.mul(u[:].rearrange("p b l -> p (b l)"), bank(0)[:, 0:B * L], gamma[:]))
                done(e.copy(wsum[:].rearrange("p b l -> p (b l)"), bank(1)[0:1, 0:B * L]))
                for i in range(3 * B * G // 4):
                    e.wait_ge(setup_pe, START + 19 + i)
                    what, bg = divmod(i, B * G // 4)
                    src = bank(i % 2)
                    if what == 0:
                        done(e.mul(kcT[:, 4 * bg:4 * bg + 4, :].rearrange("p g l -> p (g l)"), src[:, 0:4 * L], float(D) ** -0.5))
                    elif what == 1:
                        done(e.copy(vcT[:, 4 * bg:4 * bg + 4, :].rearrange("p g l -> p (g l)"), src[:, 0:4 * L]))
                    else:
                        done(e.copy(vc_full[:, 4 * bg * D:(4 * bg + 4) * D], src[0:L, :]))
                e.wait_ge(setup_act, START + 30)
                e.copy(vc[:, 0].rearrange("l g d -> l (g d)"), vc_full[:]).then_inc(v_high, 1)

            @block.vector
            def _(e):
                c = Chain(e, dve_chain)
                norm.vector(e)
                e.wait_ge(consts_in, 256)
                e.wait_ge(setup_pe, START + 1)
                c.then(e.tensor_copy(wa[:], bank(0)[:, 0:L]))
                e.tensor_tensor(hb[:], bank(1)[0:L, 0:1], aw1_b[:], ALU.add).then_inc(setup, 1)
                e.wait_ge(setup_act, START + 8)
                w3, e3 = (a[:].rearrange("l (b s) -> l b s", b=B) for a in (wT, eT))
                wide = lambda a: a.unsqueeze(2).to_broadcast([L, B, S])
                c.then(e.tensor_reduce(st[:, 0, :], w3, AX.X, ALU.max))
                c.then(e.tensor_tensor(e3, w3, wide(st[:, 0, :]), ALU.subtract))
                e.sem_inc(exp_asked, 1)
                e.wait_ge(exp_out, START + 1)
                c.then(e.tensor_reduce(st[:, 1, :], e3, AX.X, ALU.add))
                c.then(e.reciprocal(st[:, 2, :], st[:, 1, :]))
                c.then(e.tensor_scalar(st[:, 2, :], st[:, 2, :], 1.0 / (2 * L), None, ALU.mult))
                e.tensor_tensor(e3, e3, wide(st[:, 2, :]), ALU.mult).then_inc(setup, 1)
                wt = lambda a: a.unsqueeze(2).to_broadcast([P, NT, L])
                e.wait_ge(setup_act, START + 12)
                c.then(e.tensor_reduce(tk[:, 0, :], w_tok[:], AX.X, ALU.max))
                c.then(e.tensor_tensor(w_tok[:], w_tok[:], wt(tk[:, 0, :]), ALU.subtract))
                e.sem_inc(tok_asked, 1)
                e.wait_ge(tok_exped, START + 1)
                c.then(e.tensor_reduce(tk[:, 0, :], w_tok[:], AX.X, ALU.add))
                c.then(e.reciprocal(tk[:, 1, :], tk[:, 0, :]))
                c.then(e.tensor_scalar(tk[:, 1, :], tk[:, 1, :], 1.0 / (2 * S), None, ALU.mult))
                c.then(e.tensor_tensor(w_tok[:], w_tok[:], wt(tk[:, 1, :]), ALU.mult))
                e.wait_ge(setup_act, START + 16)
                e.tensor_tensor(w_tok[:], w_tok[:], e_tok[:], ALU.add).then_inc(setup, 1)
                e.wait_ge(x_high, START + 1)
                e.tensor_tensor(xr[:, 1], xT[:], xr[:, 0].bitcast(F32), ALU.subtract)
                e.wait_ge(setup_pe, START + 31)
                e.wait_ge(setup_pool, START + 1)
                four = lambda a: a.rearrange("p (k j) l -> p k (j l)", j=4)
                c.then(e.tensor_copy(four(rest[:]), ps_n.rearrange("p (k c) -> p k c", k=4)[:, :, 0:4 * L]))
                for k in range(2):
                    c.then(e.tensor_copy(part16[:], rest[:]))
                    c.then(e.scalar_tensor_tensor(rest[:], part16[:], part[:, k:k + 1], rest[:], ALU.mult, ALU.add))
                c.then(e.tensor_copy(part16[:], rest[:]))
                c.then(e.tensor_copy(qbias[:, 0:B * G, :], part16[:]))
                e.wait_ge(v_high, START + 1)
                e.tensor_tensor(vc[:, 1].rearrange("l g d -> l (g d)"), vc_full[:],
                                vc[:, 0].rearrange("l g d -> l (g d)").bitcast(F32), ALU.subtract)

        with ExitStack() as late:
            m2 = Core(nc, late, "latm")
            wq_in = m2.sb("wq_in", [P, 2, QH, P])
            w1_in = m2.sb("w1_in", [P, 2, QH, FF2])
            wk = m2.sb("wk", [P, 2, 2, HL], F32R)
            share = m2.sb("share", [L, 2, 2, QH * FF2], F32R)
            vcg = m2.sb("vcg", [P, 2, QH, L])
            qb = m2.sb("qb", [P, 2, QH, L], mybir.dt.bfloat16)
            top = m2.sb("top", [P, 2, QH])
            tot = m2.sb("tot", [P, 2, QH])
            sc = m2.sb("sc", [P, 2, HL])
            att = m2.sb("att", [P, 2, HL])
            vg = m2.sb("vg", [L, 2, D], F32R)
            attT = m2.sb("attT", [L, 2, 2, BANK], F32R)
            norm1 = m2.sb("norm1", [P, 2, TB])
            h1 = m2.sb("h1", [P, TB, FF2])
            h1sq = m2.sb("h1sq", [P, TB, FF2])
            h1T = m2.sb("h1T", [P, 2, S])
            res = m2.sb("res", [P, TB, D])
            names = ("wk_made wk_ready share_made share_ready vcg_ready qb_ready scores_ready topped shifted exped "
                     "vg_ready wk_high share_high attT_high "
                     "inv_ready weighted turned attT_ready z_ready squared added "
                     "top_chain zz_ready zz_zeroed z_root h1_affine h1_ready h1_sq h1_sum h1_root h1_inv h1_turned h1T_ready "
                     "closed zz_added res_ready res_affine res_out tail_chain stored g2_chain prep").split()
            s = {n: m2.sem(n) for n in names}
            wq_loaded = [m2.sem(f"wq_loaded{i}") for i in range(2)]
            w1_loaded = [m2.sem(f"w1_loaded{i}") for i in range(2)]
            m2.start()
            block = late.enter_context(nc.Block())
            z4 = ps_z[:, 0:HL]

            @block.sync
            def _(e):
                e.dma_start(wq_in[:, 0], io["wq_quads"][0]).then_inc(wq_loaded[0], 16)
                e.dma_start(w1_in[:, 0], io["w1_quads"][0]).then_inc(w1_loaded[0], 16)
                for b in range(B):
                    with e.Fori(0, G) as g:
                        for r in range(4):
                            m_, u1 = b * NQ + g * 4 + r, (r + 1) % 2
                            e.wait_ge(s["share_made"], START + m_ * 2)
                            e.dma_start(wq_in[:, u1], io["wq_quads"][bass.ds(g * 4 + r + 1, 1)].rearrange("a p j i -> (a p) j i")).then_inc(wq_loaded[u1], 16)
                            e.dma_start(w1_in[:, u1], io["w1_quads"][bass.ds(g * 4 + r + 1, 1)].rearrange("a p j f -> (a p) j f")).then_inc(w1_loaded[u1], 16)
                for b in range(B):
                    e.wait_ge(s["res_out"], START + b + 1)
                    e.dma_start(io["out"][b].rearrange("(t p) d -> p t d", p=P), res[:]).then_inc(s["stored"], 16)
                    e.wait_ge(s["stored"], 16 * (b + 1))

            def next_of(b, g, r):
                return b * NQ + g * 4 + (r + 1), g * 4 + (r + 1), b * G + g + (r + 1) // 4, (r + 1) % 4

            @block.gpsimd
            def _(e):
                def prepare(quad, row, quarter, u):
                    nc.gpsimd.tensor_tensor(vcg[:, u], vcT[:, bass.ds(row, 1), :].to_broadcast([P, QH, L]),
                                            g1[:, bass.ds(quad, 1), :].rearrange("p a j -> p (a j)").unsqueeze(2).to_broadcast([P, QH, L]),
                                            ALU.mult).then_inc(s["vcg_ready"], 1)
                    nc.gpsimd.tensor_tensor(qb[:, u], qbias[:, bass.ds(row, 1), :].to_broadcast([P, QH, L]),
                                            quad_mask[:, quarter, :].unsqueeze(2).to_broadcast([P, QH, L]),
                                            ALU.mult).then_inc(s["qb_ready"], 1)

                def weight(k, u, b, turned):
                    e.wait_ge(s["inv_ready"], START + b * (NS + 2) + k + 1)
                    e.wait_ge(s["turned"], START + turned)
                    nc.gpsimd.tensor_tensor(
                        att[:, u].rearrange("p (j l) -> p j l", j=QH), sc[:, u].rearrange("p (j l) -> p j l", j=QH),
                        tot[:, u].unsqueeze(2).to_broadcast([P, QH, L]), ALU.mult).then_inc(s["weighted"], 1)

                def add_squares(t, u, squares, added):
                    e.wait_ge(s["squared"], START + squares)
                    e.wait_ge(s["zz_added"], START + added)
                    nc.gpsimd.tensor_tensor(zz[:, t], zz[:, t], zsq[:, u], ALU.add).then_inc(s["zz_added"], 1)

                prepare(0, 0, 0, 0)
                for b in range(B):
                    for k in range(2):
                        weight(k, k, b, b * (NS + 1))
                    with e.Fori(0, G) as g:
                        for r in range(4):
                            for t in range(TB):
                                k = g * 4 * TB + (r * TB + t)
                                weight(k + 2, t % 2, b, b * (NS + 1) + k + 1)
                                add_squares((t - 1) % TB, (t - 1) % 2, b * NS + k, b * (NS + 1) + k)
                                if t == 0:
                                    m1_, quad, row, quarter = next_of(b, g, r)
                                    e.wait_ge(s["share_made"], START + m1_ * 2)
                                    e.wait_ge(s["scores_ready"], START + b * (NS + 2) + k + 1)
                                    prepare(quad, row, quarter, (r + 1) % 2)
                    add_squares(TB - 1, 1, (b + 1) * NS, b * (NS + 1) + NS)
                    if b < B - 1:
                        e.wait_ge(s["zz_ready"], START + b + 1)
                        nc.gpsimd.memset(zz[:], 0.0).then_inc(s["zz_zeroed"], 1)
                        nc.gpsimd.memset(zsq[:, 1], 0.0).then_inc(s["zz_zeroed"], 1)
                        e.wait_ge(s["zz_zeroed"], START + 2 * (b + 1))

            @block.vector
            def _(e):
                c = Chain(e, s["top_chain"])

                def shift(k, u, b, free):
                    done = b * (NS + 2) + k
                    e.wait_ge(s["scores_ready"], START + b * (NS + 2) + k + 1)
                    src = ps_s[:, u, 0:HL].rearrange("p (j l) -> p j l", j=QH)
                    e.tensor_reduce(top[:, u], src, AX.X, ALU.max).then_inc(s["topped"], 1)
                    e.wait_ge(s["topped"], START + done + 1)
                    e.wait_ge(s["weighted"], START + free)
                    e.tensor_tensor(sc[:, u].rearrange("p (j l) -> p j l", j=QH), src,
                                    top[:, u].unsqueeze(2).to_broadcast([P, QH, L]), ALU.subtract).then_inc(s["shifted"], 1)

                def total(k, u, b):
                    done = b * (NS + 2) + k
                    e.wait_ge(s["exped"], START + b * (NS + 2) + k + 1)
                    e.tensor_reduce(tot[:, u], sc[:, u].rearrange("p (j l) -> p j l", j=QH), AX.X, ALU.add).then_inc(s["prep"], 1)
                    e.wait_ge(s["prep"], START + done + 1)
                    e.reciprocal(tot[:, u], tot[:, u]).then_inc(s["inv_ready"], 1)

                def low(dst, src, high, made, high_sem, ready):
                    e.wait_ge(s[high_sem], START + made)
                    e.tensor_tensor(dst, src, high.bitcast(F32), ALU.subtract).then_inc(s[ready], 1)

                def low_wk(quads, u):
                    low(wk[:, u, 1], z4, wk[:, u, 0], quads, "wk_high", "wk_ready")

                def low_share(halves, half, u):
                    cols = slice(half * BANK, (half + 1) * BANK)
                    low(share[:, u, 1, cols], ps_z[0:L, :], share[:, u, 0, cols], halves, "share_high", "share_ready")

                low_wk(1, 0)
                for half in range(2):
                    low_share(half + 1, half, 0)
                for b in range(B):
                    for k in range(2):
                        shift(k, k, b, b * (NS + 2))
                        total(k, k, b)
                    low(attT[:, 0, 1], ps_t[0:L, :], attT[:, 0, 0], b * (NS + 1) + 1, "attT_high", "attT_ready")
                    with e.Fori(0, G) as g:
                        for r in range(4):
                            for t in range(TB):
                                k = g * 4 * TB + (r * TB + t)
                                m1_ = b * NQ + g * 4 + (r + 1)
                                shift(k + 2, t % 2, b, b * (NS + 2) + k + 1)
                                if t == 3:
                                    low_wk(m1_ + 1, (r + 1) % 2)
                                if t in (4, 5):
                                    low_share(m1_ * 2 + (t - 3), t - 4, (r + 1) % 2)
                                total(k + 2, t % 2, b)
                                low(attT[:, (t + 1) % 2, 1], ps_t[0:L, :], attT[:, (t + 1) % 2, 0],
                                    b * (NS + 1) + k + 2, "attT_high", "attT_ready")
                    e.wait_ge(s["z_root"], START + b + 1)
                    c.then(e.tensor_scalar(norm1[:, 1], norm1[:, 1], 1e-12, None, ALU.max))
                    c.then(e.reciprocal(norm1[:, 1], norm1[:, 1]))
                    c.then(e.tensor_scalar(norm1[:, 1], norm1[:, 1], float(G * GH * D) ** 0.5, None, ALU.mult))
                    e.wait_ge(s["h1_turned"], START + 4 * b)
                    e.wait_ge(s["closed"], START + TB // 2 * (b + 1))
                    for t in range(TB):
                        last = e.scalar_tensor_tensor(h1[:, t], ps_h[:, t], norm1[:, 1, t:t + 1], b1[:], ALU.mult, ALU.add)
                    last.then_inc(s["h1_affine"], 1)
                    e.wait_ge(s["h1_sq"], START + b + 1)
                    e.tensor_reduce(norm1[:, 0], h1sq[:], AX.X, ALU.add).then_inc(s["h1_sum"], 1)
                    if b == 0:
                        e.tensor_tensor(w2[:], w2[:], g2[:].unsqueeze(2).to_broadcast([P, 2, D]), ALU.mult).then_inc(s["g2_chain"], 1)
                    e.wait_ge(s["h1_root"], START + b + 1)
                    c.then(e.tensor_scalar(norm1[:, 1], norm1[:, 1], 1e-12, None, ALU.max))
                    c.then(e.reciprocal(norm1[:, 1], norm1[:, 1]))
                    c.then(e.tensor_scalar(norm1[:, 1], norm1[:, 1], float(FF2) ** 0.5, None, ALU.mult))
                    e.wait_ge(s["stored"], 16 * b)
                    e.wait_ge(s["res_ready"], START + b + 1)
                    for t in range(TB):
                        last = e.scalar_tensor_tensor(res[:, t], ps_s[:, t // 4, t % 4 * D:(t % 4 + 1) * D],
                                                      norm1[:, 1, t:t + 1], b2[:], ALU.mult, ALU.add)
                    last.then_inc(s["res_affine"], 1)
                    e.wait_ge(s["tail_chain"], START + b + 1)
                    e.tensor_tensor(res[:], res[:], h[:, b * TB:(b + 1) * TB, :], ALU.add).then_inc(s["res_out"], 1)

            @block.scalar
            def _(e):
                def exponentials(k, u, b):
                    e.wait_ge(s["shifted"], START + b * (NS + 2) + k + 1)
                    e.activation(sc[:, u], sc[:, u], ACT.Exp).then_inc(s["exped"], 1)

                def keep_wk(m1_, u, used):
                    e.wait_ge(s["wk_made"], START + m1_ + 1)
                    e.wait_ge(s["scores_ready"], START + used)
                    e.copy(wk[:, u, 0], z4).then_inc(s["wk_high"], 1)

                def keep_share(m1_, half, u, used):
                    e.wait_ge(s["share_made"], START + m1_ * 2 + (half + 1))
                    e.wait_ge(s["added"], START + used)
                    e.copy(share[:, u, 0, half * BANK:(half + 1) * BANK], ps_z[0:L, :]).then_inc(s["share_high"], 1)

                def high(k, u, b, used):
                    e.wait_ge(s["turned"], START + b * (NS + 1) + k + 1)
                    e.wait_ge(s["z_ready"], START + used)
                    e.copy(attT[:, u, 0], ps_t[0:L, :]).then_inc(s["attT_high"], 1)

                def square(k, u, b):
                    e.wait_ge(s["z_ready"], START + b * NS + k + 1)
                    e.wait_ge(s["zz_added"], START + b * (NS + 1) + k)
                    e.activation(zsq[:, u], ps_z[:], ACT.Square).then_inc(s["squared"], 1)

                keep_wk(0, 0, 0)
                for half in range(2):
                    keep_share(0, half, 0, 0)
                for b in range(B):
                    exponentials(0, 0, b)
                    exponentials(1, 1, b)
                    high(0, 0, b, b * NS)
                    with e.Fori(0, G) as g:
                        for r in range(4):
                            for t in range(TB):
                                k = g * 4 * TB + (r * TB + t)
                                n = b * NS + k
                                m1_ = b * NQ + g * 4 + (r + 1)
                                if r == 0 and t == 0:
                                    e.copy(vg[:], vc[:, :, bass.ds(b * G + g, 1), :].rearrange("l i a d -> l i (a d)")).then_inc(s["vg_ready"], 1)
                                if t == 3:
                                    keep_wk(m1_, (r + 1) % 2, b * (NS + 2) + k)
                                if t in (4, 5):
                                    keep_share(m1_, t - 4, (r + 1) % 2, n)
                                exponentials(k + 2, t % 2, b)
                                high(k + 1, (t + 1) % 2, b, n)
                                square(k, t % 2, b)
                    e.wait_ge(s["zz_ready"], START + b + 1)
                    e.activation(norm1[:, 1], ps_z[:, 0:TB], ACT.Sqrt).then_inc(s["z_root"], 1)
                    e.wait_ge(s["h1_affine"], START + b + 1)
                    e.activation(h1[:], h1[:], ACT.Silu).then_inc(s["h1_ready"], 1)
                    e.wait_ge(s["h1_ready"], START + b + 1)
                    e.activation(h1sq[:], h1[:], ACT.Square).then_inc(s["h1_sq"], 1)
                    e.wait_ge(s["h1_sum"], START + b + 1)
                    e.activation(norm1[:, 1], norm1[:, 0], ACT.Sqrt).then_inc(s["h1_root"], 1)
                    for i in range(4):
                        e.wait_ge(s["h1_turned"], START + 4 * b + i + 1)
                        e.wait_ge(s["res_ready"], START + b)
                        e.copy(h1T[:, i // 2, i % 2 * BANK:(i % 2 + 1) * BANK], ps_t[:] if i % 2 == 0 else ps_z[:]).then_inc(s["h1T_ready"], 1)
                    e.wait_ge(s["res_affine"], START + b + 1)
                    e.activation(res[:], res[:], ACT.Silu).then_inc(s["tail_chain"], 1)

            @block.tensor
            def _(e):
                def scores_of(dst, tile, u):
                    for i, (x_part, w_part) in enumerate(PARTS):
                        e.matmul(dst, xr[:, x_part, tile * P:(tile + 1) * P], wk[:, u, w_part], start=(i == 0), stop=False)

                def first_scores(t, b):
                    scores_of(ps_s[:, t % 2, 0:HL], b * TB + t, 0)
                    e.matmul(ps_s[:, t % 2, 0:HL], ones16[:], qb[:, 0].rearrange("p j l -> p (j l)"), start=False,
                             stop=True).then_inc(s["scores_ready"], 1)

                def make_wk(m1_, quarter_load, row, u):
                    e.wait_ge(wq_loaded[u], quarter_load)
                    for j in range(QH):
                        mm = e.matmul(ps_z[:, j * L:(j + 1) * L], wq_in[:, u, j, :], kcT[:, bass.ds(row, 1), :].rearrange("p a l -> p (a l)"),
                                      start=True, stop=True)
                    mm.then_inc(s["wk_made"], 1)

                def make_share(m1_, half, load, u):
                    e.wait_ge(w1_loaded[u], load)
                    e.wait_ge(s["vcg_ready"], START + m1_ + 1)
                    for j in range(2):
                        mm = e.matmul(ps_z[0:L, j * FF2:(j + 1) * FF2], vcg[:, u, 2 * half + j, :], w1_in[:, u, 2 * half + j, :],
                                      start=True, stop=True)
                    mm.then_inc(s["share_made"], 1)

                def turn(k, u, b):
                    e.wait_ge(s["weighted"], START + b * (NS + 2) + k + 1)
                    e.wait_ge(s["attT_ready"], START + b * (NS + 1) + k)
                    for j in range(QH):
                        mm = e.transpose(ps_t[0:L, j * P:(j + 1) * P], att[:, u, j * L:(j + 1) * L], ident[:])
                    mm.then_inc(s["turned"], 1)

                make_wk(0, 16, 0, 0)
                for half in range(2):
                    e.wait_ge(s["wk_ready"], START + 1)
                    e.wait_ge(s["share_ready"], START + half)
                    make_share(0, half, 16, 0)
                for b in range(B):
                    e.wait_ge(s["wk_ready"], START + b * NQ + 1)
                    e.wait_ge(s["qb_ready"], START + b * NQ + 1)
                    e.wait_ge(s["h1_affine"], START + b)
                    e.wait_ge(s["h1T_ready"], START + 4 * b)
                    e.wait_ge(s["res_affine"], START + b)
                    for i in range(TB // 2):
                        e.matmul(ps_h[:, 2 * i:2 * i + 2].rearrange("p t f -> p (t f)"), zero[:], xT[:, 0:BANK],
                                 start=True, stop=False, skip_group_check=True)
                    first_scores(0, b)
                    first_scores(1, b)
                    turn(0, 0, b)
                    with e.Fori(0, G) as g:
                        for r in range(4):
                            m1_, _, row, _ = next_of(b, g, r)
                            load = (g * 2 + (b * (NQ // 2) + (r + 1) // 2 + 1)) * 16
                            u, u1 = r % 2, (r + 1) % 2
                            for t in range(TB):
                                k = g * 4 * TB + (r * TB + t)
                                n = b * NS + k
                                if t == 6:
                                    e.wait_ge(s["wk_ready"], START + m1_ + 1)
                                    e.wait_ge(s["qb_ready"], START + m1_ + 1)
                                e.wait_ge(s["shifted"], START + b * (NS + 2) + k + 1)
                                t2, u2 = (t + 2) % TB, (u if t < 6 else u1)
                                scores_of(ps_s[:, t % 2, 0:HL], b * TB + t2, u2)
                                e.matmul(ps_s[:, t % 2, 0:HL], ones16[:], qb[:, u2].rearrange("p j l -> p (j l)"),
                                         start=False, stop=True).then_inc(s["scores_ready"], 1)
                                if t in (3, 4, 5):
                                    e.wait_ge(s["squared"], START + n)
                                if t == 3:
                                    make_wk(m1_, load, row, u1)
                                if t in (4, 5):
                                    make_share(m1_, t - 4, load, u1)
                                e.wait_ge(s["attT_high"], START + b * (NS + 1) + k + 1)
                                if t == 0:
                                    e.wait_ge(s["share_ready"], START + m1_ * 2)
                                for a_part, w_part in ((0, 0), (0, 1), (1, 0)):
                                    if a_part == 1:
                                        e.wait_ge(s["attT_ready"], START + b * (NS + 1) + k + 1)
                                    for j in range(QH):
                                        mm = e.matmul(ps_h[:, t, :], attT[:, t % 2, a_part, j * P:(j + 1) * P],
                                                      share[:, u, w_part, j * FF2:(j + 1) * FF2],
                                                      start=False, stop=False, skip_group_check=True)
                                mm.then_inc(s["added"], 1)
                                turn(k + 1, (t + 1) % 2, b)
                                e.wait_ge(s["squared"], START + n)
                                if t == 3:
                                    e.wait_ge(s["wk_ready"], START + m1_ + 1)
                                if t in (4, 5):
                                    e.wait_ge(s["share_ready"], START + m1_ * 2 + (t - 3))
                                if r == 0 and t == 0:
                                    e.wait_ge(s["vg_ready"], START + b * G + g + 1)
                                for i, (v_part, a_part) in enumerate(PARTS):
                                    mm = e.matmul(ps_z[:], vg[:, v_part], attT[:, t % 2, a_part], start=(i == 0), stop=(i == 2))
                                mm.then_inc(s["z_ready"], 1)
                    for i in range(TB // 2):
                        e.matmul(ps_h[:, 2 * i:2 * i + 2].rearrange("p t f -> p (t f)"), zero[:], xT[:, 0:BANK],
                                 start=False, stop=True, skip_group_check=True).then_inc(s["closed"], 1)
                    e.wait_ge(s["zz_added"], START + (b + 1) * (NS + 1))
                    e.wait_ge(s["squared"], START + (b + 1) * NS)
                    for t in range(TB):
                        for j in range(QH):
                            mm = e.matmul(ps_z[:, t:t + 1], zz[:, t, j * P:(j + 1) * P], ones[:], start=(j == 0), stop=(j == QH - 1))
                    mm.then_inc(s["zz_ready"], 1)
                    e.wait_ge(s["h1_ready"], START + b + 1)
                    e.wait_ge(s["attT_ready"], START + (b + 1) * (NS + 1))
                    for i in range(4):
                        dst = ps_t if i % 2 == 0 else ps_z
                        if i >= 2:
                            e.wait_ge(s["h1T_ready"], START + 4 * b + i - 1)
                        for j in range(4):
                            t = i % 2 * 4 + j
                            mm = e.transpose(dst[:, j * P:(j + 1) * P], h1[:, t, i // 2 * P:(i // 2 + 1) * P], ident[:])
                        mm.then_inc(s["h1_turned"], 1)
                    e.wait_ge(s["h1T_ready"], START + 4 * b + 4)
                    e.wait_ge(s["g2_chain"], START + 1)
                    e.wait_ge(s["shifted"], START + (b + 1) * (NS + 2))
                    for t in range(TB):
                        for i in range(2):
                            mm = e.matmul(ps_s[:, t // 4, t % 4 * D:(t % 4 + 1) * D], h1T[:, i, t * P:(t + 1) * P], w2[:, i, :],
                                          start=(i == 0), stop=(i == 1))
                    mm.then_inc(s["res_ready"], 1)


PHASES = [embed, retention, experts, attention, latent]


def build(nc, io, phases=PHASES):
    with ExitStack() as ctx:
        sb = lambda name, shape: ctx.enter_context(nc.sbuf_tensor(name, shape, F32))
        keep = {"h": sb("h", [P, NT, D]), "ident": sb("ident", [P, P]), "xT": sb("xT", [P, B * S])}
        for phase in phases:
            phase(nc, io, keep)


def layout(inputs):
    f = {k: np.ascontiguousarray(v) for k, v in inputs.items()}
    a = {}
    x = f["x"]
    pad = np.zeros((B, S + 3), x.dtype)
    pad[:, 2:S + 2] = x
    a["tok"] = np.stack([pad[:, k:k + S].reshape(NT, P).T for k in range(4)], axis=1)
    ok = np.ones((B, S, 3), np.float32)
    for n, (first, last) in enumerate(((1, 0), (1, 1), (2, 1))):
        ok[:, :first, n] = 0
        if last:
            ok[:, S - last:, n] = 0
    a["tok_mask"] = ok.reshape(NT, P, 3).transpose(1, 0, 2)
    a["ident"] = np.eye(P, dtype=np.float32)
    for n in (2, 3, 4):
        a[f"emb_{n}"] = f[f"L0_tok_emb_{n}"]
    a["proj_wT"] = f["L0_tok_proj_w"].T.reshape(3, P, D).transpose(1, 0, 2)
    a["proj_b"] = f["L0_tok_proj_b"]
    swap = np.arange(D) ^ 1
    for name, key in (("WQ", "L0_attn_W_Q"), ("WK", "L0_attn_W_K")):
        w = f[key].transpose(1, 0, 2).reshape(D, D)
        a[name], a[name + "_rot"] = w, w[:, swap]
    a["WVG"] = np.concatenate([f["L0_attn_W_V"].transpose(1, 0, 2).reshape(D, D), f["L0_attn_W_G"]], axis=1)
    a["WO_0"] = f["L0_attn_W_O"]
    a["gn_w"], a["gn_b"] = f["L0_attn_gn_weight"], f["L0_attn_gn_bias"]
    of_head = (np.arange(D)[:, None] // DH == np.arange(H)[None, :]).astype(np.float32)
    a["heads_mask"], a["heads_row"] = np.pad(of_head, ((0, 0), (0, 1))), of_head.T
    part_of = np.array(SCORE_PARTS)[np.arange(P) // DH]
    same = (np.arange(D)[:, None] % DH == np.arange(P)[None, :] % DH)
    a["pattern"] = np.stack([same & (part_of[None, :, which] == part) for which in range(2) for part in range(3)],
                            axis=1).astype(np.float32)
    a["log_gamma"] = np.log(np.append(GAMMAS, 1.0).astype(np.float64)).astype(np.float32)
    pos = np.arange(S, dtype=np.float32)
    pair = (np.arange(D) % DH) // 2
    base = (2.0 * pair + 0.4 * DH) / (1.4 * DH)
    power = base[:, None] ** (pos[None, :] / 128.0)
    inv_freq = (1.0 / 10000.0 ** (np.arange(DH // 2, dtype=np.float32) / np.float32(DH // 2))).astype(np.float32)
    angle = (pos[None, :] * inv_freq[pair][:, None]).astype(np.float32).astype(np.float64)
    sign = np.where(np.arange(D) % 2 == 0, -1.0, 1.0)[:, None]
    for name, scale in (("xpos_q", power), ("xpos_k", 1.0 / power)):
        a[name] = np.stack([np.cos(angle) * scale, sign * np.sin(angle) * scale], axis=1).astype(np.float32)
    a["Wr"], a["br"] = f["L0_ffn_Wr"].T, f["L0_ffn_br"]
    a["rank"] = (E - np.arange(E)).astype(np.float32)
    a["W1"] = f["L0_ffn_W1"].transpose(1, 0, 2)
    a["b1"] = f["L0_ffn_b1"].reshape(E, 2, P).transpose(2, 0, 1)
    a["W2"] = f["L0_ffn_W2"].reshape(E, 2, P, D).transpose(2, 0, 1, 3)
    a["b2"] = f["L0_ffn_b2"]
    wrap = lambda w: np.concatenate([w, w[:1]])
    a["Wqk"] = wrap(np.stack([f["L1_attn_Wq"], f["L1_attn_Wk"]], axis=1)).transpose(2, 0, 1, 3)
    a["Wv"] = wrap(f["L1_attn_Wv"]).transpose(1, 0, 2)
    a["Wo"] = f["L1_attn_Wo"].reshape(H, D, D).transpose(1, 0, 2)
    a["bqk"] = np.stack([wrap(f["L1_attn_bq"]).T, wrap(f["L1_attn_bk"]).T], axis=1)
    a["bv"] = wrap(f["L1_attn_bv"])
    a["gamma"] = f["L1_ffn_gamma_norm"].reshape(D, 1)
    wkv = f["L1_ffn_Wkv_w"]
    a["Wkv"], a["bkv"] = wkv, f["L1_ffn_Wkv_b"].reshape(1, -1)
    a["WkT"] = wkv[:, :G * D].T.reshape(G, D, D).transpose(1, 0, 2)
    a["aw1"] = f["L1_ffn_aw1_w"].reshape(G, D, L).transpose(1, 0, 2)
    a["bk"] = f["L1_ffn_Wkv_b"][:G * D].reshape(G, D).T
    a["aw1_b"], a["aw2"], a["aw2_b"] = f["L1_ffn_aw1_b"].reshape(L, 1), f["L1_ffn_aw2_w"], f["L1_ffn_aw2_b"].reshape(L, 1)
    bq = np.zeros((D, G, P), np.float32)
    for k in range(3):
        bq[:, :, 32 * k:32 * k + GH] = f["L1_ffn_Wq_b"].reshape(G, GH, D).transpose(2, 0, 1)
    a["bq_parts"] = bq
    a["g1"] = f["L1_ffn_wz_g1"].reshape(NQ, QH, D).transpose(2, 0, 1)
    a["g1"] = np.concatenate([a["g1"], a["g1"][:, :1]], axis=1)
    row = np.arange(P)
    a["quad_mask"] = ((row[:, None, None] % 32 == 4 * np.arange(4)[None, :, None] + np.arange(QH)[None, None, :])
                      & (row[:, None, None] < 96)).astype(np.float32)
    a["part"] = -np.stack([(row >= 32).astype(np.float32), (row >= 64).astype(np.float32)], axis=1)
    quads = f["L1_ffn_Wq_w"].T.reshape(NQ, QH, D, D).transpose(0, 2, 1, 3)
    a["wq_quads"] = np.concatenate([quads, quads[:1]])
    quads = f["L1_ffn_wz_w1"].reshape(NQ, QH, D, FF2).transpose(0, 2, 1, 3)
    a["w1_quads"] = np.concatenate([quads, quads[:1]])
    a["wz_b1"], a["wz_b2"] = f["L1_ffn_wz_b1"], f["L1_ffn_wz_b2"]
    a["w2"] = f["L1_ffn_wz_w2"].reshape(2, P, D).transpose(1, 0, 2)
    a["g2"] = f["L1_ffn_wz_g2"].reshape(2, P).T
    return {k: np.ascontiguousarray(v) for k, v in a.items()}


def kernel(**inputs):
    import concourse.bacc as bacc
    from concourse.bass_utils import run_bass_kernel_spmd

    nc = bacc.Bacc("TRN2", target_bir_lowering=False, num_devices=1)
    arrays = layout(inputs)
    io = {name: nc.dram_tensor(f"in_{name}", a.shape, mybir.dt.from_np(a.dtype), kind="ExternalInput").ap()
          for name, a in arrays.items()}
    io["out"] = nc.dram_tensor("out", (B, S, D), F32, kind="ExternalOutput").ap()
    build(nc, io)
    r = run_bass_kernel_spmd(nc, [{f"in_{name}": a for name, a in arrays.items()}], core_ids=[0])
    return r.results[0]["out"]
```

```python
from contextlib import ExitStack

import numpy as np

import concourse.bass as bass
from concourse import mybir

F32 = mybir.dt.float32
F32R = mybir.dt.float32r
PARTS = ((0, 0), (0, 1), (1, 0))
BF16 = mybir.dt.bfloat16
I32 = mybir.dt.int32
U32 = mybir.dt.uint32
ALU = mybir.AluOpType
ACT = mybir.ActivationFunctionType
AX = mybir.AxisListType

P = 128
B, S, D = 2, 1024, 128
NT = B * S // P
TB = S // P
BANK = 512
H = 8
DH = D // H
VOCAB = 25000
E, FH = 8, 256
G, GH = 8, 16
L = 100
QH = 4
NQ = G * GH // QH
FF2 = 2 * D
START = 1
SCORE_PARTS = ((0, 0), (0, 1), (1, 0), (1, 1), (0, 2), (2, 0), (1, 2), (2, 1))
DMA_SEMS = ("_in", "_loaded", "gathered", "stored")
GAMMAS = (1.0 - np.exp(np.linspace(np.log(1.0 / 32), np.log(1.0 / 128), H))).astype(np.float32)


class Chain:

    def __init__(self, eng, sem, base=0):
        self.eng, self.sem, self.base, self.n = eng, sem, base, 0

    def mark(self, ins):
        self.n += 1
        ins.then_inc(self.sem, 1)

    def then(self, ins):
        self.n += 1
        ins.then_inc(self.sem, 1)
        self.eng.wait_ge(self.sem, START + self.base + self.n)


class Core:

    def __init__(self, nc, ctx, tag):
        self.nc, self.ctx, self.tag, self.sems, self.primed = nc, ctx, tag, [], []

    def sb(self, name, shape, dt=F32):
        return self.ctx.enter_context(self.nc.sbuf_tensor(f"{self.tag}_{name}", shape, dt))

    def ps(self, name, shape):
        return self.ctx.enter_context(self.nc.psum_tensor(f"{self.tag}_{name}", shape, F32))

    def sem(self, name):
        if not self.sems:
            self.ctx.callback(self.clear)
        self.sems.append(self.nc.alloc_semaphore(f"{self.tag}_{name}"))
        if not name.rstrip("0123456789").endswith(DMA_SEMS):
            self.primed.append(self.sems[-1])
        return self.sems[-1]

    def start(self):
        engines = (self.nc.sync, self.nc.gpsimd, self.nc.vector, self.nc.tensor, self.nc.scalar)
        for n, sem in enumerate(self.primed):
            engines[n % len(engines)].sem_inc(sem, START)
        self.nc.all_engine_barrier()

    def clear(self):
        self.nc.clear_and_free_semaphores(self.sems)
        self.nc.all_engine_barrier()


class Norm:

    def __init__(self, core, h, ident, xT, psT, l2=None, xr=None):
        self.nc, self.h, self.ident, self.xT, self.psT, self.l2 = core.nc, h, ident, xT, psT, l2
        self.xr = xr
        self.xc = core.sb("xc", [P, NT, D])
        self.sq = core.sb("sq", [P, NT, D])
        self.stat = core.sb("stat", [P, 6, NT])
        self.eps = core.sb("eps", [P, 1])
        self.chain = core.sem("norm_chain")
        self.squares = core.sem("norm_squares")
        self.var_ready = core.sem("norm_var_ready")
        self.root = core.sem("norm_root")
        self.centred = core.sem("norm_centred")
        self.scaled = core.sem("norm_scaled")
        self.turned = core.sem("norm_turned")
        self.xT_ready = core.sem("norm_xT_ready")
        self.xr_ready = core.sem("norm_xr_ready")
        self.high = core.sem("norm_high")

    def vector(self, e):
        nc, c = self.nc, Chain(e, self.chain)
        tot, mean, var, root, inv = (self.stat[:, i, :] for i in range(5))
        halves = [slice(i * NT // 2, (i + 1) * NT // 2) for i in range(2)]
        quarters = [slice(i * NT // 4, (i + 1) * NT // 4) for i in range(4)]

        def rows(dst, src, column, op, tiles, done):
            n = tiles.stop - tiles.start
            nc.vector.tensor_tensor(dst[:, tiles], src[:, tiles], column[:, tiles].unsqueeze(2).to_broadcast([P, n, D]),
                                    op).then_inc(done, 1)

        def sum_squares(rounds):
            for i, tiles in enumerate(halves):
                e.wait_ge(self.squares, START + 2 * rounds + i + 1)
                nc.vector.tensor_reduce(var[:, tiles], self.sq[:, tiles], AX.X, ALU.add).then_inc(self.var_ready, 1)
            e.wait_ge(self.root, START + rounds + 1)

        c.then(nc.vector.memset(self.eps[:], 1e-5))
        c.then(nc.vector.tensor_reduce(tot, self.h[:], AX.X, ALU.add))
        c.then(nc.vector.tensor_scalar(mean, tot, 1.0 / D, None, ALU.mult))
        for tiles in halves:
            rows(self.xc, self.h, mean, ALU.subtract, tiles, self.centred)
        sum_squares(0)
        c.then(nc.vector.reciprocal(inv, root))
        e.wait_ge(self.centred, START + 2)
        if self.l2 is not None:
            for tiles in halves:
                rows(self.xc, self.xc, inv, ALU.mult, tiles, self.centred)
            sum_squares(1)
            c.then(nc.vector.tensor_scalar(root, root, 1e-12, None, ALU.max))
            c.then(nc.vector.reciprocal(inv, root))
            c.then(nc.vector.tensor_scalar(inv, inv, float(D) ** 0.5, None, ALU.mult))
            e.wait_ge(self.centred, START + 4)
        for tiles in quarters:
            rows(self.xc, self.xc, inv, ALU.mult, tiles, self.scaled)
        if self.xr is not None:
            for g in range(NT // 4):
                cols = slice(g * BANK, (g + 1) * BANK)
                e.wait_ge(self.high, START + g + 1)
                e.wait_ge(self.xT_ready, START + g + 1)
                nc.vector.tensor_tensor(self.xr[:, 1, cols], self.xT[:, cols], self.xr[:, 0, cols].bitcast(F32),
                                        ALU.subtract).then_inc(self.xr_ready, 1)

    def scalar(self, e):
        nc = self.nc
        var, root = self.stat[:, 2, :], self.stat[:, 3, :]
        for n in range(1 if self.l2 is None else 2):
            for i in range(2):
                tiles = slice(i * NT // 2, (i + 1) * NT // 2)
                e.wait_ge(self.centred, START + 2 * n + i + 1)
                if n > 0:
                    e.wait_ge(self.var_ready, START + 2)
                nc.scalar.activation(self.sq[:, tiles], self.xc[:, tiles], ACT.Square).then_inc(self.squares, 1)
            e.wait_ge(self.var_ready, START + 2 * n + 2)
            if n == 0:
                nc.scalar.activation(root, var, ACT.Sqrt, bias=self.eps[:], scale=1.0 / D).then_inc(self.root, 1)
            else:
                nc.scalar.activation(root, var, ACT.Sqrt).then_inc(self.root, 1)
        for g in range(NT // 4):
            e.wait_ge(self.turned, START + g + 1)
            dst, src = self.xT[:, g * BANK:(g + 1) * BANK], self.psT[:, g % 2, :]
            if self.xr is not None:
                nc.scalar.copy(self.xr[:, 0, g * BANK:(g + 1) * BANK], src).then_inc(self.high, 1)
            if self.l2 is None:
                nc.scalar.copy(dst, src).then_inc(self.xT_ready, 1)
            else:
                nc.scalar.mul(dst, src, self.l2).then_inc(self.xT_ready, 1)

    def tensor(self, e):
        for g in range(NT // 4):
            e.wait_ge(self.scaled, START + g + 1)
            if g >= 2:
                e.wait_ge(self.xT_ready, START + g - 1)
            for k in range(4):
                mm = e.transpose(self.psT[:, g % 2, k * P:(k + 1) * P], self.xc[:, 4 * g + k, :], self.ident[:])
            mm.then_inc(self.turned, 1)


def embed(nc, io, keep):
    GT = 4
    with ExitStack() as ctx:
        m = Core(nc, ctx, "emb")
        tok_i = m.sb("tok_i", [P, 4, NT], I32)
        tok = m.sb("tok", [P, 4, NT])
        hash_f = m.sb("hash_f", [P, 3, NT])
        quot = m.sb("quot", [P, NT])
        quot_i = m.sb("quot_i", [P, NT], I32)
        fix = m.sb("fix", [P, NT])
        ids = m.sb("ids", [P, 3 * NT], U32)
        mask = m.sb("mask", [P, NT, 3])
        proj = m.sb("proj", [P, 3, D])
        bias = m.sb("bias", [P, D])
        rows = m.sb("rows", [P, NT, 3, D])
        rowsM = m.sb("rowsM", [P, 2, 3, D])
        rowsT = m.sb("rowsT", [P, 2, 3, D])
        ps_t = m.ps("ps_t", [P, 2, BANK])
        ps_h = m.ps("ps_h", [P, 2, BANK])
        tok_in, proj_in, ident_in = m.sem("tok_in"), m.sem("proj_in"), m.sem("ident_in")
        chain, ids_ready = m.sem("chain"), m.sem("ids_ready")
        gathered = [m.sem(f"gathered{g}") for g in range(NT // GT)]
        masked, turned, rows_ready, projected, h_ready = (
            m.sem(n) for n in ("masked", "turned", "rows_ready", "projected", "h_ready"))
        m.start()
        block = ctx.enter_context(nc.Block())

        @block.sync
        def _(e):
            e.dma_start(tok_i[:], io["tok"]).then_inc(tok_in, 16)
            e.dma_start(mask[:], io["tok_mask"]).then_inc(proj_in, 16)
            e.dma_start(keep["ident"][:], io["ident"]).then_inc(ident_in, 16)
            e.dma_start(proj[:], io["proj_wT"]).then_inc(proj_in, 16)
            e.dma_start(bias[:], io["proj_b"].partition_broadcast(P)).then_inc(proj_in, 16)

        @block.gpsimd
        def _(e):
            e.wait_ge(ids_ready, START + 1)
            for t in range(NT):
                for n in range(3):
                    nc.gpsimd.indirect_dma_start(
                        out=rows[:, t, n, :], out_offset=None, in_=io[f"emb_{n + 2}"],
                        in_offset=bass.IndirectOffsetOnAxis(ap=ids[:, n * NT + t:n * NT + t + 1], axis=0),
                    ).then_inc(gathered[t // GT], 16)

        @block.vector
        def _(e):
            c = Chain(e, chain)

            def push(dst, src, nxt):
                c.then(nc.vector.tensor_scalar(dst, src, 64.0, None, ALU.mult))
                c.then(nc.vector.tensor_tensor(dst, dst, nxt, ALU.add))
                c.then(nc.vector.tensor_scalar(quot_i[:], dst, 1.0 / VOCAB, None, ALU.mult))
                c.then(nc.vector.tensor_copy(quot[:], quot_i[:]))
                c.then(nc.vector.tensor_scalar(quot[:], quot[:], float(VOCAB), None, ALU.mult))
                c.then(nc.vector.tensor_tensor(dst, dst, quot[:], ALU.subtract))
                c.then(nc.vector.tensor_scalar(fix[:], dst, 0.0, float(VOCAB), ALU.is_lt, ALU.mult))
                c.then(nc.vector.tensor_tensor(dst, dst, fix[:], ALU.add))
                c.then(nc.vector.tensor_scalar(fix[:], dst, float(VOCAB), float(VOCAB), ALU.is_ge, ALU.mult))
                c.then(nc.vector.tensor_tensor(dst, dst, fix[:], ALU.subtract))

            e.wait_ge(tok_in, 16)
            c.then(nc.vector.tensor_copy(tok[:], tok_i[:]))
            push(hash_f[:, 0, :], tok[:, 1, :], tok[:, 2, :])
            push(hash_f[:, 1, :], hash_f[:, 0, :], tok[:, 3, :])
            push(hash_f[:, 2, :], tok[:, 0, :], tok[:, 1, :])
            push(hash_f[:, 2, :], hash_f[:, 2, :], tok[:, 2, :])
            push(hash_f[:, 2, :], hash_f[:, 2, :], tok[:, 3, :])
            nc.vector.tensor_copy(ids[:], hash_f[:].rearrange("p n t -> p (n t)")).then_inc(ids_ready, 1)
            e.wait_ge(proj_in, 48)

            def add_bias(t, u, count):
                e.wait_ge(projected, START + count + 1)
                nc.vector.tensor_tensor(keep["h"][:, t, :],
                                        ps_h[:, u, 0:D], bias[:], ALU.add).then_inc(h_ready, 1)
            for g in range(NT // GT):
                e.wait_ge(gathered[g], 16 * 3 * GT)
                for i in range(GT):
                    t, u = g * GT + i, i % 2
                    if t >= 2:
                        e.wait_ge(turned, START + t - 1)
                    nc.vector.tensor_tensor(rowsM[:, u], rows[:, t], mask[:, t, :].unsqueeze(2).to_broadcast([P, 3, D]),
                                            ALU.mult).then_inc(masked, 1)
                    if t >= 1:
                        add_bias(t - 1, 1 - u, t - 1)
            add_bias(NT - 1, 1, NT - 1)

        @block.tensor
        def _(e):
            def turn(t, u):
                e.wait_ge(masked, START + t + 1)
                e.wait_ge(rows_ready, START + max(0, t - 1))
                for n in range(3):
                    mm = e.transpose(ps_t[:, u, n * D:(n + 1) * D], rowsM[:, u, n, :], keep["ident"][:])
                mm.then_inc(turned, 1)

            def project(t, u):
                e.wait_ge(rows_ready, START + t + 1)
                e.wait_ge(h_ready, START + max(0, t - 1))
                for n in range(3):
                    mm = e.matmul(ps_h[:, u, 0:D], rowsT[:, u, n, :], proj[:, n, :], start=(n == 0), stop=(n == 2))
                mm.then_inc(projected, 1)

            e.wait_ge(ident_in, 16)
            e.wait_ge(proj_in, 48)
            for t in range(NT):
                turn(t, t % 2)
                if t >= 1:
                    project(t - 1, (t - 1) % 2)
            project(NT - 1, 1)

        @block.scalar
        def _(e):
            for t in range(NT):
                e.wait_ge(turned, START + t + 1)
                e.wait_ge(projected, START + max(0, t - 1))
                nc.scalar.copy(rowsT[:, t % 2].rearrange("p n d -> p (n d)"), ps_t[:, t % 2, 0:3 * D]).then_inc(rows_ready, 1)


class Attention:

    def __init__(self, m, split):
        self.parts = PARTS if split else ((0, 0),)
        count = 2 if split else 1
        self.psS = m.ps("psS", [P, 2, 2, BANK])
        self.psT = m.ps("psT", [P, 2, BANK])
        self.psO = m.ps("psO", [P, 2, BANK])
        self.probs = m.sb("probs", [P, 3, S])
        self.probsT = m.sb("probsT", [P, count, TB, S], F32R if split else F32)
        self.negmax = m.sb("negmax", [P, TB])
        self.total = m.sb("total", [P, TB])
        self.scores_ready = m.sem("scores_ready")
        self.max_ready = m.sem("max_ready")
        self.probs_ready = m.sem("probs_ready")
        self.turned = m.sem("turned")
        self.high_ready = [m.sem(f"high_ready{q}") for q in range(2)]
        self.probsT_ready = [m.sem(f"probsT_ready{q}") for q in range(2)]
        self.heads_ready = [m.sem(f"heads_ready{c}") for c in range(2)]

    def score(self, e, n, i, products):
        e.wait_ge(self.probs_ready, START + n * TB + max(0, i - 1))
        for c in range(2):
            pairs = products(i, c)
            for j, (lhsT, rhs) in enumerate(pairs):
                mm = e.matmul(self.psS[:, i % 2, c, :], lhsT, rhs, start=(j == 0), stop=(j == len(pairs) - 1))
        mm.then_inc(self.scores_ready, 1)

    def turn(self, e, n, i, ident):
        e.wait_ge(self.probs_ready, START + n * TB + (i + 1))
        for half in range(2):
            e.wait_ge(self.probsT_ready[half], START + n * TB + i)
            for j in range(4):
                mm = e.transpose(self.psT[:, half, j * P:(j + 1) * P],
                                 self.probs[:, i % 3, (4 * half + j) * P:(4 * half + j + 1) * P], ident)
            mm.then_inc(self.turned, 1)

    def gather(self, e, v, c, t, start):
        last = len(self.parts) - 1
        for j, (v_part, p_part) in enumerate(self.parts):
            mm = e.matmul(self.psO[:, c, :], v[:, v_part, t, :], self.probsT[:, p_part, t, c * BANK:(c + 1) * BANK],
                          start=(start and t == 0 and j == 0), stop=(start and t == TB - 1 and j == last),
                          skip_group_check=not start)
        if t == TB - 1:
            mm.then_inc(self.heads_ready[c], 1)

    def rest(self, e, n, products, v, ident, start, psO_free, after_turn):
        for i in range(TB):
            if i + 2 < TB:
                self.score(e, n, i + 2, products)
            self.turn(e, n, i, ident)
            after_turn(i)
            if i >= 4:
                if i == 4:
                    for half in range(2):
                        e.wait_ge(self.probsT_ready[half], START + n * TB + 4)
                    psO_free()
                self.gather(e, v, 0, 2 * (i - 4), start)
                self.gather(e, v, 0, 2 * (i - 4) + 1, start)
        for half in range(2):
            e.wait_ge(self.probsT_ready[half], START + n * TB + TB)
        for t in range(TB):
            self.gather(e, v, 1, t, start)

    def maxima(self, e, n, i, ahead=0):
        if i == 0:
            e.wait_ge(self.probs_ready, START + n * TB)
        e.wait_ge(self.scores_ready, START + n * TB + (ahead + i + 1))
        e.tensor_reduce(self.negmax[:, i:i + 1], self.psS[:, i % 2].rearrange("p a b -> p (a b)"),
                        AX.X, ALU.max, negate=True).then_inc(self.max_ready, 1)

    def exponentials(self, e, n, i, ahead=0):
        e.wait_ge(self.turned, START + n * 2 * TB + max(0, 2 * (i - 2)))
        e.wait_ge(self.max_ready, START + n * TB + (ahead + i + 1))
        e.activation(self.probs[:, i % 3, :], self.psS[:, i % 2].rearrange("p a b -> p (a b)"), ACT.Exp,
                     bias=self.negmax[:, i:i + 1],
                     accum_out=self.total[:, i:i + 1]).then_inc(self.probs_ready, 1)

    def turned_half(self, i, half):
        return ([self.probsT[:, part, 4 * half:4 * half + 4, i * P:(i + 1) * P] for part in range(len(self.parts[:2]))],
                self.psT[:, half, :].rearrange("p (j s) -> p j s", j=4))


def retention(nc, io, keep):
    h, ident, xT = keep["h"], keep["ident"], keep["xT"]
    with ExitStack() as ctx:
        m = Core(nc, ctx, "ret")
        at = Attention(m, split=False)
        norm = Norm(m, h, ident, xT, at.psT)
        wq, wqr, wk, wkr, wo = (m.sb(n, [P, D]) for n in ("wq", "wqr", "wk", "wkr", "wo"))
        wvg = m.sb("wvg", [P, 2 * D])
        heads_mask = m.sb("heads_mask", [P, H + 1])
        heads_row = m.sb("heads_row", [P, H, D])
        gn_w, gn_b = m.sb("gn_w", [P, D]), m.sb("gn_b", [P, D])
        log_gamma = m.sb("log_gamma", [P, H + 1])
        log_gamma_head = m.sb("log_gamma_head", [P, 1])
        xpos = m.sb("xpos", [P, 2, S])
        full = m.sb("full", [P, 4, BANK])
        qk_parts = m.sb("qk_parts", [P, 2, 3, B * S], BF16)
        pattern = m.sb("pattern", [P, 2 * 3, P])
        pick = m.sb("pick", [P, 2 * 3, P], BF16)
        q_head, k_head = m.sb("q_head", [P, S], BF16), m.sb("k_head", [P, S], BF16)
        vals = m.sb("vals", [P, NT, D])
        gate = m.sb("gate", [P, NT, D])
        v_head = m.sb("v_head", [P, 2, 1, TB, D])
        dist = m.sb("dist", [P, 2 * TB - 1, P])
        decay = m.sb("decay", [P, 2 * TB - 1, P])
        heads = m.sb("heads", [P, S])
        zeros = m.sb("zeros", [P, BANK], BF16)
        yt = m.sb("yt", [P, TB, H, DH])
        totals = m.sb("totals", [P, B, H, TB])
        gs = m.sb("gs", [P, 4, TB, H])
        gn_eps = m.sb("gn_eps", [P, 1])
        names = ("log_gamma_ready weights_in consts_in xpos_q_in xpos_k_in pool_chain dist_ready proj_ready proj_used q_ready k_ready "
                 "vg_ready vg_used v_head_ready decay_ready init_done heads_copied "
                 "part_made rest_made pick_ready q_picked k_picked q_kept k_kept y_turned y_ready gn_var gn_root gated g_turned gT_ready out_ready totals_kept out_added dve_chain").split()
        s = {n: m.sem(n) for n in names}
        sq = norm.sq
        m.start()
        block = ctx.enter_context(nc.Block())
        units = lambda b, hh: hh + b * H
        chunks = range(8)
        part_order = [(r - part, part) for r in range(10) for part in range(3) if r - part in chunks]
        part_count = lambda i, part: part_order.index((i, part)) + 1
        rest_order = [(i, part) for i, part in part_order if part < 2]
        rest_count = lambda i, part: rest_order.index((i, part)) + 1

        @block.sync
        def _(e):
            for dst, src in ((wq, "WQ"), (wqr, "WQ_rot"), (wk, "WK"), (wkr, "WK_rot"), (wvg, "WVG"), (wo, "WO_0")):
                e.dma_start(dst[:], io[src]).then_inc(s["weights_in"], 16)
            e.dma_start(xpos[:], io["xpos_q"]).then_inc(s["xpos_q_in"], 16)
            e.dma_start(heads_mask[:], io["heads_mask"]).then_inc(s["consts_in"], 16)
            e.dma_start(pattern[:], io["pattern"]).then_inc(s["consts_in"], 16)
            e.dma_start(heads_row[:], io["heads_row"].partition_broadcast(P)).then_inc(s["consts_in"], 16)
            e.dma_start(log_gamma[:], io["log_gamma"].partition_broadcast(P)).then_inc(s["consts_in"], 16)
            e.dma_start(gn_w[:], io["gn_w"].partition_broadcast(P)).then_inc(s["consts_in"], 16)
            e.dma_start(gn_b[:], io["gn_b"].partition_broadcast(P)).then_inc(s["consts_in"], 16)
            e.wait_ge(s["q_ready"], START + 4)
            e.dma_start(xpos[:], io["xpos_k"]).then_inc(s["xpos_k_in"], 16)

        @block.gpsimd
        def _(e):
            c = Chain(e, s["pool_chain"])
            c.then(nc.gpsimd.iota(decay[:].bitcast(I32), [[P, 2 * TB - 1], [-1, P]], base=-(TB - 1) * P,
                                  channel_multiplier=1))
            c.then(nc.gpsimd.tensor_copy(dist[:], decay[:].bitcast(I32)))
            c.then(nc.gpsimd.tensor_scalar(decay[:], dist[:], -1.0, None, ALU.mult))
            nc.gpsimd.memset(zeros[:], 0.0).then_inc(s["dist_ready"], 1)
            nc.gpsimd.memset(at.probsT[:, 0, :, BANK:], 0.0)
            for i, part in rest_order:
                e.wait_ge(s["part_made"], START + part_count(i, part))
                nc.gpsimd.tensor_tensor(full[:, i % 4], full[:, i % 4], qk_parts[:, i // 4, part, i % 4 * BANK:(i % 4 + 1) * BANK],
                                        ALU.subtract).then_inc(s["rest_made"], 1)
            e.wait_ge(s["consts_in"], 96)

            def make_pick(hh):
                nc.gpsimd.tensor_tensor(pick[:].rearrange("p m r -> p (m r)"), pattern[:].rearrange("p m r -> p (m r)"),
                                        heads_mask[:, bass.ds(hh, 1)].to_broadcast([P, 6 * P]), ALU.mult).then_inc(s["pick_ready"], 1)
            for b in range(B):
                e.wait_ge(s["vg_used"], START + NT)
                if b > 0:
                    e.wait_ge(s["k_picked"], START + b * (H + 1))
                make_pick(0)
                e.wait_ge(at.heads_ready[1], START + b * (H + 1))
                nc.gpsimd.memset(v_head[:, 1], 0.0).then_inc(s["v_head_ready"], 1)
                with e.Fori(0, H // 2) as pair:
                    for u in range(2):
                        hh = pair * 2 + u
                        e.wait_ge(at.heads_ready[1], START + b * (H + 1) + hh)
                        nc.gpsimd.tensor_tensor(v_head[:, u, 0], vals[:, b * TB:(b + 1) * TB, :],
                                                heads_row[:, bass.ds(hh, 1), :].to_broadcast([P, TB, D]),
                                                ALU.mult).then_inc(s["v_head_ready"], 1)
                        e.wait_ge(s["k_picked"], START + b * (H + 1) + hh + 1)
                        make_pick(hh + 1)

        @block.vector
        def _(e):
            c = Chain(e, s["dve_chain"])
            norm.vector(e)
            for n, (ready, tables) in enumerate((("q_ready", "xpos_q_in"), ("k_ready", "xpos_k_in"))):
                e.wait_ge(s[tables], 16)
                for ch in range(4):
                    i, dst, pos = 4 * n + ch, full[:, ch], slice(ch % 2 * BANK, (ch % 2 + 1) * BANK)
                    e.wait_ge(s["proj_ready"], START + i + 1)
                    if i >= 4:
                        e.wait_ge(s["part_made"], START + part_count(i - 4, 2))
                    c.then(nc.vector.tensor_tensor(dst, at.psS[:, i % 2, 0, :], xpos[:, 0, pos], ALU.mult))
                    nc.vector.tensor_tensor(heads[:, 0:BANK], at.psS[:, i % 2, 1, :], xpos[:, 1, pos],
                                            ALU.mult).then_inc(s["proj_used"], 1)
                    e.wait_ge(s["proj_used"], START + i + 1)
                    nc.vector.tensor_tensor(dst, dst, heads[:, 0:BANK], ALU.add).then_inc(s[ready], 1)
                    e.wait_ge(s[ready], START + ch + 1)
            e.wait_ge(s["consts_in"], 96)
            e.wait_ge(s["dist_ready"], START + 1)
            c.then(nc.vector.tensor_tensor(dist[:], dist[:], decay[:], ALU.max))
            c.then(nc.vector.memset(gn_eps[:], 1e-5))

            def choose_decay(hh, count):
                e.wait_ge(s["decay_ready"], START + count)
                e.tensor_scalar(log_gamma_head[:], log_gamma[:, bass.ds(hh, 1)], 1.0, None, ALU.mult).then_inc(
                    s["log_gamma_ready"], 1)

            def keep_keys(count, used):
                e.wait_ge(s["k_picked"], START + count)
                e.wait_ge(at.scores_ready, START + used)
                e.tensor_copy(k_head[:], at.psS[:, 1].rearrange("p a b -> p (a b)")).then_inc(s["k_kept"], 1)

            def begin(b):
                choose_decay(0, b * (H + 1))
                keep_keys(b * (H + 1) + 1, b * (H * TB + 2))
                at.maxima(e, b * H, 0, ahead=2 * b)
                at.maxima(e, b * H, 1, ahead=2 * b)
            begin(0)
            for b in range(B):
                with e.Fori(0, H) as hh:
                    n = units(b, hh)
                    for i in range(TB):
                        if i + 2 < TB:
                            at.maxima(e, n, i + 2, ahead=2 * b)
                        for half in range(2):
                            (dst,), src = at.turned_half(i, half)
                            first = 4 * half - i + TB - 1
                            e.wait_ge(s["decay_ready"], START + b * (H + 1) + hh + 1)
                            e.wait_ge(at.turned, START + n * 2 * TB + (2 * i + half + 1))
                            e.tensor_tensor(dst, src, decay[:, first:first + 4, :], ALU.mult).then_inc(
                                at.probsT_ready[half], 1)
                    e.wait_ge(at.probs_ready, START + n * TB + TB)
                    e.tensor_copy(totals[:, b, bass.ds(hh, 1), :], at.total[:].unsqueeze(1)).then_inc(s["totals_kept"], 1)
                    choose_decay(hh + 1, b * (H + 1) + hh + 1)
                    keep_keys(b * (H + 1) + hh + 2, n * TB + (2 * b + TB))
                    at.maxima(e, n + 1, 0, ahead=2 * b)
                    at.maxima(e, n + 1, 1, ahead=2 * b)
                if b < B - 1:
                    begin(b + 1)
                wide = lambda a: a.unsqueeze(3).to_broadcast([P, TB, H, DH])
                e.wait_ge(s["totals_kept"], START + (b + 1) * H)
                e.wait_ge(s["y_ready"], START + 2 * b + 2)
                c.then(e.reciprocal(gs[:, 0], totals[:, b].rearrange("p h t -> p t h")))
                c.then(e.tensor_tensor(yt[:], yt[:], wide(gs[:, 0]), ALU.mult))
                c.then(e.tensor_reduce(gs[:, 1], yt[:], AX.X, ALU.add))
                c.then(e.tensor_scalar(gs[:, 1], gs[:, 1], 1.0 / DH, None, ALU.mult))
                c.then(e.tensor_tensor(yt[:], yt[:], wide(gs[:, 1]), ALU.subtract))
                sq4 = sq[:, 0:TB, :].rearrange("p t (h e) -> p t h e", h=H)
                c.then(e.tensor_tensor(sq4, yt[:], yt[:], ALU.mult))
                e.tensor_reduce(gs[:, 2], sq4, AX.X, ALU.add).then_inc(s["gn_var"], 1)
                e.wait_ge(s["gn_root"], START + b + 1)
                c.then(e.reciprocal(gs[:, 0], gs[:, 3]))
                c.then(e.tensor_tensor(yt[:], yt[:], wide(gs[:, 0]), ALU.mult))
                y3 = yt[:].rearrange("p t h e -> p t (h e)")
                row = lambda a: a[:].unsqueeze(1).to_broadcast([P, TB, D])
                c.then(e.tensor_tensor(y3, y3, row(gn_w), ALU.mult))
                c.then(e.tensor_tensor(y3, y3, row(gn_b), ALU.add))
                e.tensor_tensor(y3, y3, gate[:, b * TB:(b + 1) * TB, :], ALU.mult).then_inc(s["gated"], 1)
                for half in range(2):
                    e.wait_ge(s["out_ready"], START + 2 * b + half + 1)
                    hv = h[:, b * TB + 4 * half:b * TB + 4 * half + 4, :]
                    e.tensor_tensor(hv, at.psO[:, half, :].rearrange("p (t d) -> p t d", t=4), hv,
                                    ALU.add).then_inc(s["out_added"], 1)

        @block.tensor
        def _(e):
            norm.tensor(e)
            e.wait_ge(s["weights_in"], 96)
            for n, (w, wr) in enumerate(((wq, wqr), (wk, wkr))):
                for ch in range(4):
                    i, cols = 4 * n + ch, slice(ch * BANK, (ch + 1) * BANK)
                    e.wait_ge(norm.xT_ready, START + min(4, max(ch, i // 2) + 1))
                    if i >= 2:
                        e.wait_ge(s["proj_used"], START + i - 1)
                    e.matmul(at.psS[:, i % 2, 0, :], w[:], xT[:, cols], start=True, stop=True)
                    e.matmul(at.psS[:, i % 2, 1, :], wr[:], xT[:, cols], start=True, stop=True).then_inc(s["proj_ready"], 1)
                    for t in (2 * i, 2 * i + 1):
                        if t >= 2:
                            e.wait_ge(s["vg_used"], START + t - 1)
                        e.matmul(at.psO[:, t % 2, 0:2 * D], xT[:, t * P:(t + 1) * P], wvg[:], start=True,
                                 stop=True).then_inc(s["vg_ready"], 1)
            e.wait_ge(s["proj_used"], START + 8)
            e.wait_ge(s["vg_used"], START + NT)
            e.wait_ge(s["dist_ready"], START + 1)

            def pick_head(which, b, picked):
                for c in range(2):
                    for part in range(3):
                        mm = e.matmul(at.psS[:, which, c, :], pick[:, 3 * which + part, :],
                                      qk_parts[:, which, part, b * S + c * BANK:b * S + (c + 1) * BANK],
                                      start=(part == 0), stop=(part == 2))
                mm.then_inc(picked, 1)

            def products(i, c):
                return [(q_head[:, i * P:(i + 1) * P], k_head[:, c * BANK:(c + 1) * BANK])]

            def first_scores(n, count):
                e.wait_ge(s["q_kept"], START + count)
                e.wait_ge(s["k_kept"], START + count)
                for i in range(2):
                    at.score(e, n, i, products)

            e.wait_ge(s["part_made"], START + 24)

            def begin(b):
                e.wait_ge(s["pick_ready"], START + b * (H + 1) + 1)
                if b > 0:
                    e.wait_ge(at.max_ready, START + b * (H * TB + 2))
                pick_head(0, b, s["q_picked"])
                pick_head(1, b, s["k_picked"])
                first_scores(b * H, b * (H + 1) + 1)
            begin(0)
            for b in range(B):
                e.wait_ge(s["out_added"], START + 2 * b)
                for c in range(2):
                    e.matmul(at.psO[:, c, :], zeros[:, 0:P], zeros[:], start=True, stop=False, skip_group_check=True)
                e.wait_ge(s["v_head_ready"], START + b * (H + 1) + 1)
                with e.Fori(0, H // 2) as pair:
                    for u in range(2):
                        hh = pair * 2 + u
                        n = units(b, hh)
                        for i in range(TB):
                            if i < 4:
                                if i == 0:
                                    for half in range(2):
                                        e.wait_ge(at.probsT_ready[half], START + n * TB)
                                for t in (2 * i, 2 * i + 1):
                                    at.gather(e, v_head[:, 1 - u], 1, t, start=False)
                            if i + 2 < TB:
                                at.score(e, n, i + 2, products)
                            at.turn(e, n, i, ident[:])
                            if i == TB - 2:
                                e.wait_ge(s["pick_ready"], START + b * (H + 1) + hh + 2)
                                pick_head(0, b, s["q_picked"])
                            if i == TB - 1:
                                pick_head(1, b, s["k_picked"])
                            if i >= 4:
                                if i == 4:
                                    for half in range(2):
                                        e.wait_ge(at.probsT_ready[half], START + n * TB + 4)
                                    e.wait_ge(s["v_head_ready"], START + b * (H + 1) + hh + 2)
                                for t in (2 * i - 8, 2 * i - 7):
                                    at.gather(e, v_head[:, u], 0, t, start=False)
                        first_scores(n + 1, b * (H + 1) + hh + 2)
                for half in range(2):
                    e.wait_ge(at.probsT_ready[half], START + (b + 1) * H * TB)
                for t in range(TB):
                    at.gather(e, v_head[:, 1], 1, t, start=False)
                for c in range(2):
                    e.matmul(at.psO[:, c, :], zeros[:, 0:P], zeros[:], start=False, stop=True,
                             skip_group_check=True).then_inc(s["init_done"], 1)
                if b < B - 1:
                    begin(b + 1)
                for half in range(2):
                    e.wait_ge(s["heads_copied"], START + 2 * b + half + 1)
                    for j in range(4):
                        t = 4 * half + j
                        mm = e.transpose(at.psT[:, half, j * P:(j + 1) * P], heads[:, t * P:(t + 1) * P], ident[:])
                    mm.then_inc(s["y_turned"], 1)
                e.wait_ge(s["gated"], START + b + 1)
                for half in range(2):
                    for j in range(4):
                        mm = e.transpose(at.psT[:, half, j * P:(j + 1) * P],
                                         yt[:, 4 * half + j].rearrange("p h e -> p (h e)"), ident[:])
                    mm.then_inc(s["g_turned"], 1)
                for half in range(2):
                    e.wait_ge(s["gT_ready"], START + 2 * b + half + 1)
                    for j in range(4):
                        t = 4 * half + j
                        mm = e.matmul(at.psO[:, half, j * P:(j + 1) * P], heads[:, t * P:(t + 1) * P], wo[:],
                                      start=True, stop=True)
                    mm.then_inc(s["out_ready"], 1)

        @block.scalar
        def _(e):
            norm.scalar(e)
            for i, part in part_order:
                if part == 0:
                    e.wait_ge(s[("q_ready", "k_ready")[i // 4]], START + i % 4 + 1)
                else:
                    e.wait_ge(s["rest_made"], START + rest_count(i, part - 1))
                e.copy(qk_parts[:, i // 4, part, i % 4 * BANK:(i % 4 + 1) * BANK], full[:, i % 4]).then_inc(s["part_made"], 1)
                if part == 0:
                    for t in (2 * i, 2 * i + 1):
                        e.wait_ge(s["vg_ready"], START + t + 1)
                        nc.scalar.copy(vals[:, t, :], at.psO[:, t % 2, 0:D])
                        nc.scalar.activation(gate[:, t, :], at.psO[:, t % 2, D:2 * D], ACT.Silu).then_inc(s["vg_used"], 1)
            e.wait_ge(s["consts_in"], 96)

            def make_decay(count, used):
                for half in range(2):
                    e.wait_ge(at.probsT_ready[half], START + used)
                e.wait_ge(s["log_gamma_ready"], START + count)
                e.activation(decay[:], dist[:], ACT.Exp, scale=log_gamma_head[:]).then_inc(s["decay_ready"], 1)

            def keep_queries(count, used):
                e.wait_ge(s["q_picked"], START + count)
                e.wait_ge(at.scores_ready, START + used)
                e.copy(q_head[:], at.psS[:, 0].rearrange("p a b -> p (a b)")).then_inc(s["q_kept"], 1)

            def begin(b):
                make_decay(b * (H + 1) + 1, b * H * TB)
                keep_queries(b * (H + 1) + 1, b * (H * TB + 2))
            begin(0)
            for b in range(B):
                with e.Fori(0, H) as hh:
                    n = units(b, hh)
                    e.wait_ge(s["totals_kept"], START + n)
                    for i in range(TB):
                        at.exponentials(e, n, i, ahead=2 * b)
                    keep_queries(b * (H + 1) + hh + 2, n * TB + (2 * b + TB))
                    make_decay(b * (H + 1) + hh + 2, n * TB + TB)
                for half in range(2):
                    e.wait_ge(s["init_done"], START + 2 * b + half + 1)
                    e.copy(heads[:, half * BANK:(half + 1) * BANK], at.psO[:, half, :]).then_inc(s["heads_copied"], 1)
                if b < B - 1:
                    begin(b + 1)
                for half in range(2):
                    e.wait_ge(s["y_turned"], START + 2 * b + half + 1)
                    e.copy(yt[:, 4 * half:4 * half + 4].rearrange("p t h e -> p (t h e)"),
                           at.psT[:, half, :]).then_inc(s["y_ready"], 1)
                e.wait_ge(s["gn_var"], START + b + 1)
                e.activation(gs[:, 3], gs[:, 2], ACT.Sqrt, bias=gn_eps[:], scale=1.0 / DH).then_inc(s["gn_root"], 1)
                for half in range(2):
                    e.wait_ge(s["g_turned"], START + 2 * b + half + 1)
                    e.copy(heads[:, half * BANK:(half + 1) * BANK], at.psT[:, half, :]).then_inc(s["gT_ready"], 1)


def experts(nc, io, keep):
    h, ident, xT = keep["h"], keep["ident"], keep["xT"]
    with ExitStack() as ctx:
        m = Core(nc, ctx, "moe")
        ps_t = m.ps("ps_t", [P, 2, BANK])
        ps_hid = m.ps("ps_hid", [P, 2, 2, BANK])
        ps_out = m.ps("ps_out", [P, 2, 4, D])
        xr = m.sb("xr", [P, 2, B * S], F32R)
        norm = Norm(m, h, ident, xT, ps_t, xr=xr)
        wr = m.sb("wr", [P, E])
        br = m.sb("br", [P, E])
        w1 = m.sb("w1", [P, E, FH])
        w1_parts = m.sb("w1_parts", [P, 2, E, FH], F32R)
        b1 = m.sb("b1", [P, E, 2])
        w2 = m.sb("w2", [P, E, 2, D])
        b2 = m.sb("b2", [E, D])
        rank = m.sb("rank", [P, E])
        prob, left, hit, pick, comb = (m.sb(n, [P, NT, E]) for n in ("prob", "left", "hit", "pick", "comb"))
        best = m.sb("best", [P, NT])
        combT = m.sb("combT", [E, B * S])
        hid = m.sb("hid", [P, 2, 2, BANK])
        w1_high, w1_ready = m.sem("w1_high"), m.sem("w1_ready")
        weights_in, logits_ready, chain, exp_asked, exp_out, comb_ready, combT_turned, combT_ready, bias_ready, bias_added = (
            m.sem(n) for n in "weights_in logits_ready chain exp_asked exp_out comb_ready combT_turned combT_ready bias_ready bias_added".split())
        hid_ready, hid_gelu, out_ready, out_added = (m.sem(n) for n in "hid_ready hid_gelu out_ready out_added".split())
        NC = B * S // BANK
        m.start()
        block = ctx.enter_context(nc.Block())

        @block.sync
        def _(e):
            for dst, src in ((wr, "Wr"), (w1, "W1"), (b1, "b1"), (w2, "W2"), (b2, "b2")):
                e.dma_start(dst[:], io[src]).then_inc(weights_in, 16)
            e.dma_start(br[:], io["br"].partition_broadcast(P)).then_inc(weights_in, 16)
            e.dma_start(rank[:], io["rank"].partition_broadcast(P)).then_inc(weights_in, 16)

        @block.gpsimd
        def _(e):
            e.wait_ge(weights_in, 16 * 7)
            nc.gpsimd.tensor_copy(w1_parts[:, 0], w1[:]).then_inc(w1_high, 1)
            e.wait_ge(w1_high, START + 1)
            nc.gpsimd.tensor_tensor(w1_parts[:, 1], w1[:], w1_parts[:, 0].bitcast(F32), ALU.subtract).then_inc(w1_ready, 1)

        @block.tensor
        def _(e):
            norm.tensor(e)
            e.wait_ge(weights_in, 16 * 7)
            e.wait_ge(norm.xT_ready, START + NT // 4)
            for t in range(NT):
                mm = e.matmul(ps_out[:, 0, 0, t * E:(t + 1) * E], xT[:, t * P:(t + 1) * P], wr[:], start=True, stop=True)
            mm.then_inc(logits_ready, 1)
            e.wait_ge(comb_ready, START + 1)
            for c in range(NC):
                if c >= 2:
                    e.wait_ge(combT_ready, START + c - 1)
                for j in range(4):
                    mm = e.transpose(ps_t[0:E, c % 2, j * P:(j + 1) * P], comb[:, 4 * c + j, :], ident[:])
                mm.then_inc(combT_turned, 1)
            for c in range(NC):
                e.wait_ge(combT_ready, START + c + 1)
                if c >= 2:
                    e.wait_ge(bias_added, START + c - 1)
                for j in range(4):
                    t = 4 * c + j
                    mm = e.matmul(ps_out[:, c % 2, j, :], combT[:, t * P:(t + 1) * P], b2[:], start=True, stop=True)
                mm.then_inc(bias_ready, 1)
            e.wait_ge(w1_ready, START + 1)
            e.wait_ge(norm.xr_ready, START + NT // 4)
            with e.Fori(0, NC) as c:
                def out(x):
                    e.wait_ge(hid_gelu, START + c * E + (x + 1))
                    if x == 0:
                        e.wait_ge(bias_added, START + NC)
                    e.wait_ge(out_added, START + c * E + max(0, x - 1))
                    for j in range(4):
                        for k in range(2):
                            mm = e.matmul(ps_out[:, x % 2, j, :], hid[:, x % 2, k, j * P:(j + 1) * P], w2[:, x, k, :],
                                          start=(k == 0), stop=(k == 1))
                    mm.then_inc(out_ready, 1)
                for x in range(E):
                    e.wait_ge(hid_gelu, START + c * E + max(0, x - 1))
                    for k in range(2):
                        for j, (w_part, x_part) in enumerate(PARTS):
                            mm = e.matmul(ps_hid[:, x % 2, k, :], w1_parts[:, w_part, x, k * P:(k + 1) * P],
                                          xr[:, x_part, bass.ds(c * BANK, BANK)], start=(j == 0), stop=(j == 2))
                    mm.then_inc(hid_ready, 1)
                    if x:
                        out(x - 1)
                out(E - 1)

        @block.scalar
        def _(e):
            norm.scalar(e)
            e.wait_ge(exp_asked, START + 1)
            e.activation(prob[:], prob[:], ACT.Exp).then_inc(exp_out, 1)
            for c in range(NC):
                e.wait_ge(combT_turned, START + c + 1)
                e.copy(combT[:, c * BANK:(c + 1) * BANK], ps_t[0:E, c % 2, :]).then_inc(combT_ready, 1)
            with e.Fori(0, NC) as c:
                for x in range(E):
                    e.wait_ge(hid_ready, START + c * E + (x + 1))
                    e.wait_ge(out_ready, START + c * E + max(0, x - 1))
                    for k in range(2):
                        act = e.activation(hid[:, x % 2, k, :], ps_hid[:, x % 2, k, :], ACT.Gelu, bias=b1[:, x, k:k + 1])
                    act.then_inc(hid_gelu, 1)

        @block.vector
        def _(e):
            norm.vector(e)
            c = Chain(e, chain)
            wide = lambda a: a.unsqueeze(2).to_broadcast([P, NT, E])
            row = lambda a: a[:].unsqueeze(1).to_broadcast([P, NT, E])
            e.wait_ge(logits_ready, START + 1)
            c.then(e.tensor_tensor(prob[:], ps_out[:, 0, 0, 0:NT * E].rearrange("p (t x) -> p t x", t=NT), row(br), ALU.add))
            c.then(e.tensor_reduce(best[:], prob[:], AX.X, ALU.max))
            e.tensor_tensor(prob[:], prob[:], wide(best[:]), ALU.subtract).then_inc(exp_asked, 1)
            e.wait_ge(exp_out, START + 1)
            c.then(e.tensor_reduce(best[:], prob[:], AX.X, ALU.add))
            c.then(e.reciprocal(best[:], best[:]))
            c.then(e.tensor_tensor(prob[:], prob[:], wide(best[:]), ALU.mult))
            c.then(e.tensor_copy(left[:], prob[:]))
            for n in range(2):
                c.then(e.tensor_reduce(best[:], left[:], AX.X, ALU.max))
                c.then(e.tensor_tensor(hit[:], left[:], wide(best[:]), ALU.is_equal))
                c.then(e.tensor_tensor(hit[:], hit[:], row(rank), ALU.mult))
                c.then(e.tensor_reduce(best[:], hit[:], AX.X, ALU.max))
                c.then(e.tensor_tensor(pick[:], hit[:], wide(best[:]), ALU.is_equal))
                if n == 0:
                    c.then(e.tensor_tensor(comb[:], pick[:], prob[:], ALU.mult))
                    c.then(e.tensor_scalar(pick[:], pick[:], 4.0, None, ALU.mult))
                    c.then(e.tensor_tensor(left[:], left[:], pick[:], ALU.subtract))
                else:
                    c.then(e.tensor_tensor(pick[:], pick[:], prob[:], ALU.mult))
                    e.tensor_tensor(comb[:], comb[:], pick[:], ALU.add).then_inc(comb_ready, 1)
            for q in range(NC):
                e.wait_ge(bias_ready, START + q + 1)
                hv = h[:, 4 * q:4 * q + 4, :]
                e.tensor_tensor(hv, ps_out[:, q % 2], hv, ALU.add).then_inc(bias_added, 1)
            e.wait_ge(bias_added, START + NC)
            e.wait_ge(comb_ready, START + 1)
            with e.Fori(0, NC) as q:
                for x in range(E):
                    e.wait_ge(out_ready, START + q * E + (x + 1))
                    e.wait_ge(out_added, START + q * E + x)
                    for j in range(4):
                        hv = h[:, bass.ds(q * 4 + j, 1), :].rearrange("p a d -> p (a d)")
                        add = e.scalar_tensor_tensor(hv, ps_out[:, x % 2, j, :],
                                                     comb[:, bass.ds(q * 4 + j, 1), x:x + 1].rearrange("p a x -> p (a x)"),
                                                     hv, ALU.mult, ALU.add)
                    add.then_inc(out_added, 1)


def attention(nc, io, keep):
    h, ident, xT = keep["h"], keep["ident"], keep["xT"]
    with ExitStack() as ctx:
        m = Core(nc, ctx, "mha")
        at = Attention(m, split=True)
        xr = m.sb("xr", [P, 2, NT * P], F32R)
        norm = Norm(m, h, ident, xT, at.psT, xr=xr)
        wqk = m.sb("wqk", [P, H + 1, 2, D])
        wqk_parts = m.sb("wqk_parts", [P, 2, H + 1, 2, D], F32R)
        wqk_head = m.sb("wqk_head", [P, 2, 2, D], F32R)
        wv, wo = m.sb("wv", [P, H + 1, D]), m.sb("wo", [P, H, D])
        bqk = m.sb("bqk", [P, 2, H + 1])
        bv = m.sb("bv", [P, H + 1, D])
        bqk_head = m.sb("bqk_head", [P, 2])
        q, k = m.sb("q", [P, 2, S], F32R), m.sb("k", [P, 2, S], F32R)
        v_full = m.sb("v_full", [P, TB * D])
        v = m.sb("v", [P, 2, TB, D], F32R)
        headT = m.sb("headT", [P, S])
        inv = m.sb("inv", [P, TB])
        (weights_in, pool_chain, bias_ready, w_ready, q_ready, k_ready, v_ready, q_high, k_high, v_high,
         q_used, k_used, v_full_ready, v_used, headT_ready, out_ready, out_added, inv_ready) = (
             m.sem(n) for n in (
                 "weights_in pool_chain bias_ready w_ready q_ready k_ready v_ready q_high k_high v_high "
                 "q_used k_used v_full_ready v_used headT_ready out_ready out_added inv_ready").split())
        SCALE = float(D) ** -0.5
        m.start()
        block = ctx.enter_context(nc.Block())
        after = lambda hh, b: (hh + (b + 1) // B, (b + 1) % B)

        @block.sync
        def _(e):
            for dst, src in ((wqk, "Wqk"), (wv, "Wv"), (wo, "Wo"), (bqk, "bqk")):
                e.dma_start(dst[:], io[src]).then_inc(weights_in, 16)
            e.dma_start(bv[:], io["bv"].partition_broadcast(P)).then_inc(weights_in, 16)

        @block.gpsimd
        def _(e):
            c = Chain(e, pool_chain)
            e.wait_ge(weights_in, 80)
            c.then(nc.gpsimd.tensor_scalar(bqk[:, 0, :], bqk[:, 0, :], SCALE, None, ALU.mult))

            def split(heads):
                full, high, low = wqk[:, heads], wqk_parts[:, 0, heads], wqk_parts[:, 1, heads]
                c.then(nc.gpsimd.tensor_scalar(full[:, :, 0, :], full[:, :, 0, :], SCALE, None, ALU.mult))
                c.then(nc.gpsimd.tensor_copy(high, full))
                c.then(nc.gpsimd.tensor_tensor(low, full, high.bitcast(F32), ALU.subtract))

            def head_weights(j):
                for part in range(2):
                    cp = nc.gpsimd.tensor_copy(wqk_head[:, part], wqk_parts[:, part, bass.ds(j, 1)].rearrange("p a w d -> p (a w) d"))
                cp.then_inc(w_ready, 1)

            def low_values(n):
                e.wait_ge(v_high, START + n + 1)
                nc.gpsimd.tensor_tensor(v[:, 1].rearrange("p t d -> p (t d)"), v_full[:],
                                        v[:, 0].rearrange("p t d -> p (t d)").bitcast(F32), ALU.subtract).then_inc(v_used, 1)
            split(slice(0, 1))
            head_weights(0)
            split(slice(1, H + 1))
            low_values(0)
            with e.Fori(0, H) as hh:
                for b in range(B):
                    n = hh * B + b
                    if b == 1:
                        e.wait_ge(k_ready, START + n + 1)
                        head_weights(hh + 1)
                    low_values(n + 1)

        @block.tensor
        def _(e):
            cols = lambda b, c: slice(b * S + c * BANK, b * S + (c + 1) * BANK)

            def project(which, b, ready):
                for c in range(2):
                    for j, (w_part, x_part) in enumerate(PARTS):
                        mm = e.matmul(at.psS[:, which, c, :], wqk_head[:, w_part, which, :], xr[:, x_part, cols(b, c)],
                                      start=(j == 0), stop=(j == 2))
                mm.then_inc(ready, 1)

            def values(hh, b):
                for t in range(TB):
                    mm = e.matmul(at.psT[:, t // 4, t % 4 * P:(t % 4 + 1) * P], xT[:, (b * TB + t) * P:(b * TB + t + 1) * P],
                                  wv[:, bass.ds(hh, 1), :].rearrange("p a d -> p (a d)"), start=True, stop=True)
                mm.then_inc(v_ready, 1)

            def output(hh, n, half):
                e.wait_ge(headT_ready, START + n * 2 + (half + 1))
                for t in range(4 * half, 4 * half + 4):
                    mm = e.matmul(at.psO[:, half, t % 4 * P:(t % 4 + 1) * P], headT[:, t * P:(t + 1) * P],
                                  wo[:, bass.ds(hh, 1), :].rearrange("p a d -> p (a d)"), start=True, stop=True)
                mm.then_inc(out_ready, 1)

            def products(i, c):
                return [(q[:, q_part, i * P:(i + 1) * P], k[:, k_part, c * BANK:(c + 1) * BANK]) for q_part, k_part in PARTS]

            def first_scores(n):
                e.wait_ge(q_used, START + n + 1)
                e.wait_ge(k_used, START + n + 1)
                for i in range(2):
                    at.score(e, n, i, products)

            norm.tensor(e)
            e.wait_ge(norm.xT_ready, START + NT // 4)
            e.wait_ge(norm.xr_ready, START + NT // 4)
            e.wait_ge(weights_in, 80)
            e.wait_ge(w_ready, START + 1)
            project(0, 0, q_ready)
            project(1, 0, k_ready)
            values(0, 0)
            first_scores(0)
            with e.Fori(0, H) as hh:
                for b in range(B):
                    n = hh * B + b
                    hh1, b1 = after(hh, b)

                    def values_ready():
                        e.wait_ge(v_used, START + n + 1)
                        e.wait_ge(out_added, START + 2 * n)

                    def next_unit(i):
                        if i == TB - 2:
                            if b == 1:
                                e.wait_ge(w_ready, START + hh1 + 1)
                            project(0, b1, q_ready)
                        if i == TB - 1:
                            project(1, b1, k_ready)

                    e.wait_ge(v_full_ready, START + n + 1)
                    at.rest(e, n, products, v, ident[:], start=True, psO_free=values_ready, after_turn=next_unit)
                    values(hh1, b1)
                    first_scores(n + 1)
                    output(hh, n, 0)
                    output(hh, n, 1)

        @block.scalar
        def _(e):
            def high(n, which, dst, ready, high_sem):
                e.wait_ge(ready, START + n + 1)
                e.activation(dst[:, 0], at.psS[:, which].rearrange("p a b -> p (a b)"), ACT.Identity,
                             bias=bqk_head[:, which:which + 1]).then_inc(high_sem, 1)

            def turned_copy(n, i):
                for half in range(2):
                    (dst, _), src = at.turned_half(i, half)
                    e.wait_ge(at.turned, START + n * 2 * TB + (2 * i + half + 1))
                    e.copy(dst, src).then_inc(at.high_ready[half], 1)

            def high_values(n):
                e.wait_ge(v_full_ready, START + n + 1)
                e.copy(v[:, 0].rearrange("p t d -> p (t d)"), v_full[:]).then_inc(v_high, 1)

            norm.scalar(e)
            e.wait_ge(bias_ready, START + 1)
            high(0, 0, q, q_ready, q_high)
            high(0, 1, k, k_ready, k_high)
            high_values(0)
            with e.Fori(0, H) as hh:
                for b in range(B):
                    n = hh * B + b
                    e.wait_ge(inv_ready, START + n)
                    for i in range(TB):
                        at.exponentials(e, n, i)
                        if i >= 1:
                            turned_copy(n, i - 1)
                    if b == 1:
                        e.wait_ge(bias_ready, START + hh + 2)
                    high(n + 1, 0, q, q_ready, q_high)
                    turned_copy(n, TB - 1)
                    high(n + 1, 1, k, k_ready, k_high)
                    for c in range(2):
                        e.wait_ge(at.heads_ready[c], START + n + 1)
                        e.wait_ge(out_ready, START + n * 2)
                        e.copy(headT[:, c * BANK:(c + 1) * BANK], at.psO[:, c, :]).then_inc(headT_ready, 1)
                    high_values(n + 1)

        @block.vector
        def _(e):
            def biases(j):
                e.tensor_copy(bqk_head[:], bqk[:, :, bass.ds(j, 1)].rearrange("p w a -> p (w a)")).then_inc(bias_ready, 1)

            def low(n, which, dst, high_sem, used):
                e.wait_ge(high_sem, START + n + 1)
                e.scalar_tensor_tensor(dst[:, 1], at.psS[:, which].rearrange("p a b -> p (a b)"), bqk_head[:, which:which + 1],
                                       dst[:, 0].bitcast(F32), ALU.add, ALU.subtract).then_inc(used, 1)

            def values(j, n):
                e.wait_ge(v_ready, START + n + 1)
                e.tensor_tensor(v_full[:].rearrange("p (t d) -> p t d", t=TB), at.psT[:].rearrange("p a (j d) -> p (a j) d", j=4),
                                bv[:, bass.ds(j, 1), :].to_broadcast([P, TB, D]), ALU.add).then_inc(v_full_ready, 1)

            norm.vector(e)
            e.wait_ge(w_ready, START + 1)
            biases(0)
            e.wait_ge(bias_ready, START + 1)
            low(0, 0, q, q_high, q_used)
            low(0, 1, k, k_high, k_used)
            values(0, 0)
            at.maxima(e, 0, 0)
            at.maxima(e, 0, 1)
            with e.Fori(0, H) as hh:
                for b in range(B):
                    n = hh * B + b
                    hh1, b1 = after(hh, b)
                    for i in range(TB):
                        if i + 2 < TB:
                            at.maxima(e, n, i + 2)
                        if i == TB - 1:
                            if b == 1:
                                e.wait_ge(k_used, START + n + 1)
                                biases(hh1)
                                e.wait_ge(bias_ready, START + hh1 + 1)
                            low(n + 1, 0, q, q_high, q_used)
                        for half in range(2):
                            (high_part, low_part), src = at.turned_half(i, half)
                            e.wait_ge(at.high_ready[half], START + n * TB + (i + 1))
                            e.tensor_tensor(low_part, src, high_part.bitcast(F32), ALU.subtract).then_inc(at.probsT_ready[half], 1)
                    low(n + 1, 1, k, k_high, k_used)
                    e.wait_ge(at.probs_ready, START + n * TB + TB)
                    e.reciprocal(inv[:], at.total[:]).then_inc(inv_ready, 1)
                    values(hh1, n + 1)
                    at.maxima(e, n + 1, 0)
                    at.maxima(e, n + 1, 1)
                    e.wait_ge(inv_ready, START + n + 1)
                    for half in range(2):
                        e.wait_ge(out_ready, START + n * 2 + half + 1)
                        for j in range(4):
                            t = 4 * half + j
                            hv = h[:, b * TB + t, :]
                            add = e.scalar_tensor_tensor(hv, at.psO[:, half, j * P:(j + 1) * P], inv[:, t:t + 1], hv,
                                                         ALU.mult, ALU.add)
                        add.then_inc(out_added, 1)


def latent(nc, io, keep):
    h, ident, xT = keep["h"], keep["ident"], keep["xT"]
    HL = QH * L
    NS = NQ * TB
    with ExitStack() as ctx:
        m = Core(nc, ctx, "lat")
        ps_h = m.ps("ps_h", [P, TB, FF2])
        ps_s = m.ps("ps_s", [P, 2, BANK])
        ps_t = m.ps("ps_t", [P, BANK])
        ps_z = m.ps("ps_z", [P, BANK])
        gamma = m.sb("gamma", [P, 1])
        norm = Norm(m, h, ident, xT, ps_s, l2=gamma[:])
        xn = norm.xc
        kcT = m.sb("kcT", [P, B * G + 1, L])
        vcT = m.sb("vcT", [P, B * G + 1, L])
        vc = m.sb("vc", [L, 2, B * G, D], F32R)
        xr = m.sb("xr", [P, 2, NT * P], F32R)
        g1 = m.sb("g1", [P, NQ + 1, QH])
        qbias = m.sb("qbias", [P, B * G + 1, L])
        quad_mask = m.sb("quad_mask", [P, 4, QH])
        ones16 = m.sb("ones16", [P, P], BF16)
        zero = m.sb("zero", [P, BANK], BF16)
        ones = m.sb("ones", [P, 1])
        zsq = m.sb("zsq", [P, 2, BANK])
        zz = m.sb("zz", [P, TB, BANK])
        b1, b2 = m.sb("b1", [P, FF2]), m.sb("b2", [P, D])
        w2 = m.sb("w2", [P, 2, D])
        g2 = m.sb("g2", [P, 2])
        consts_in, gamma_in, setup, setup_act, setup_pe, setup_pool, exp_asked, exp_out, tok_asked, tok_exped = (m.sem(n) for n in (
            "consts_in gamma_in setup setup_act setup_pe setup_pool exp_asked exp_out tok_asked tok_exped").split())

        with ExitStack() as early:
            m1 = Core(nc, early, "latw")
            wkv = m1.sb("wkv", [P, 2 * G * D])
            wkT = m1.sb("wkT", [P, G, D])
            aw1 = m1.sb("aw1", [P, G, L])
            bkv_row = m1.sb("bkv_row", [1, 2 * G * D])
            bk = m1.sb("bk", [P, G])
            aw1_b, aw2_b = m1.sb("aw1_b", [L, 1]), m1.sb("aw2_b", [L, 1])
            aw2 = m1.sb("aw2", [L, L])
            bq = m1.sb("bq", [P, G, P])
            wa = m1.sb("wa", [P, L])
            hb = m1.sb("hb", [L, 1])
            hidT = m1.sb("hidT", [L, B * S])
            wT = m1.sb("wT", [L, B * S])
            eT = m1.sb("eT", [L, B * S])
            vc_full = m1.sb("vc_full", [L, B * G * D])
            st = m1.sb("st", [L, 4, B])
            w_tok, e_tok = m1.sb("w_tok", [P, NT, L]), m1.sb("e_tok", [P, NT, L])
            tk = m1.sb("tk", [P, 2, NT])
            u = m1.sb("u", [P, B, L])
            wsum = m1.sb("wsum", [1, B, L])
            part = m1.sb("part", [P, 2], F32)
            part16 = m1.sb("part16", [P, B * G, L], BF16)
            rest = m1.sb("rest", [P, B * G, L])
            ps_n = ps_h[:].rearrange("p a b -> p (a b)")
            bank = lambda i: ps_n[:, i * BANK:(i + 1) * BANK]
            dve_chain = m1.sem("dve_chain")
            spare = (ps_s[:, 0, :], ps_s[:, 1, :], ps_t[:], ps_z[:])
            bias_made = m1.sem("bias_made")
            x_high, v_high = m1.sem("x_high"), m1.sem("v_high")
            m.start()
            m1.start()
            block = early.enter_context(nc.Block())

            @block.sync
            def _(e):
                e.dma_start(gamma[:], io["gamma"]).then_inc(gamma_in, 16)
                for dst, src in ((wkT, "WkT"), (aw1, "aw1"), (bk, "bk"), (aw1_b, "aw1_b"), (aw2, "aw2"), (aw2_b, "aw2_b"),
                                 (wkv, "Wkv"), (bkv_row, "bkv"), (bq, "bq_parts"), (g1, "g1"), (quad_mask, "quad_mask"),
                                 (part, "part"), (w2, "w2"), (g2, "g2")):
                    e.dma_start(dst[:], io[src]).then_inc(consts_in, 16)
                e.dma_start(b1[:], io["wz_b1"].partition_broadcast(P)).then_inc(consts_in, 16)
                e.dma_start(b2[:], io["wz_b2"].partition_broadcast(P)).then_inc(consts_in, 16)

            @block.gpsimd
            def _(e):
                for dst in (zero[:], kcT[:, B * G:, :], vcT[:, B * G:, :], qbias[:, B * G:, :]):
                    nc.gpsimd.memset(dst, 0.0)
                nc.gpsimd.memset(ones[:], 1.0)
                nc.gpsimd.memset(zz[:], 0.0)
                nc.gpsimd.memset(zsq[:], 0.0)
                ms = nc.gpsimd.memset(ones16[:], 1.0)
                ms.then_inc(setup_pool, 1)

            @block.tensor
            def _(e):
                c = Chain(e, setup_pe)
                norm.tensor(e)
                e.wait_ge(consts_in, 256)
                for g in range(G):
                    e.matmul(bank(0)[:, 0:L], wkT[:, g, :], aw1[:, g, :], start=(g == 0), stop=(g == G - 1))
                for g in range(G):
                    mm = e.matmul(bank(1)[0:L, 0:1], aw1[:, g, :], bk[:, g:g + 1], start=(g == 0), stop=(g == G - 1))
                c.mark(mm)
                e.wait_ge(norm.xT_ready, START + NT // 4)
                e.wait_ge(setup, START + 1)
                for ch in range(4):
                    if ch >= 2:
                        e.wait_ge(setup_act, START + ch - 1)
                    c.mark(e.matmul(bank(2 + ch % 2)[0:L, :], wa[:], xT[:, ch * BANK:(ch + 1) * BANK], start=True, stop=True))
                for ch in range(4):
                    e.wait_ge(setup_act, START + (4 if ch < 2 else 4 + ch - 1))
                    c.mark(e.matmul(bank(ch % 2)[0:L, :], aw2[:], hidT[:, ch * BANK:(ch + 1) * BANK], start=True, stop=True))
                e.wait_ge(setup_act, START + 8)
                for t in range(NT):
                    mm = e.transpose(bank(2 + t // 4 % 2)[:, t % 4 * L:(t % 4 + 1) * L], wT[:, t * P:(t + 1) * P], ident[0:L, 0:L])
                    if t % 4 == 3:
                        c.mark(mm)
                        if t // 4 in (1, 2):
                            e.wait_ge(setup_act, START + 8 + t // 4)
                e.wait_ge(setup, START + 2)
                e.wait_ge(setup_act, START + 12)
                for t in range(NT):
                    mm = e.transpose(bank(2 + t // 4 % 2)[:, t % 4 * L:(t % 4 + 1) * L], eT[:, t * P:(t + 1) * P], ident[0:L, 0:L])
                    if t % 4 == 3:
                        c.mark(mm)
                        if t // 4 in (1, 2):
                            e.wait_ge(setup_act, START + 12 + t // 4)
                e.wait_ge(setup, START + 3)
                e.wait_ge(setup_pool, START + 1)
                for b in range(B):
                    for t in range(TB):
                        mm = e.matmul(bank(0)[:, b * L:(b + 1) * L], xn[:, b * TB + t, :], w_tok[:, b * TB + t, :],
                                      start=(t == 0), stop=(t == TB - 1))
                    for t in range(TB):
                        mm = e.matmul(bank(1)[0:1, b * L:(b + 1) * L], ones[:], w_tok[:, b * TB + t, :],
                                      start=(t == 0), stop=(t == TB - 1))
                c.mark(mm)
                e.wait_ge(setup_act, START + 18)
                for i in range(3 * B * G // 4):
                    if i >= 2:
                        e.wait_ge(setup_act, START + 18 + i - 1)
                    dst = bank(i % 2)
                    what, bg = divmod(i, B * G // 4)
                    b, g = divmod(4 * bg, G)
                    if what < 2:
                        for j in range(4):
                            cols = slice((what * G + g + j) * D, (what * G + g + j + 1) * D)
                            e.matmul(dst[:, j * L:(j + 1) * L], wkv[:, cols], u[:, b, :], start=True, stop=False)
                            mm = e.matmul(dst[:, j * L:(j + 1) * L], bkv_row[:, cols], wsum[:, b, :], start=False, stop=True)
                    else:
                        cols = slice((G + g) * D, (G + g + 4) * D)
                        e.matmul(dst[0:L, :], u[:, b, :], wkv[:, cols], start=True, stop=False)
                        mm = e.matmul(dst[0:L, :], wsum[:, b, :], bkv_row[:, cols], start=False, stop=True)
                    c.mark(mm)
                    if i == 5:
                        e.wait_ge(setup_act, START + 18 + B * G // 4)
                        for bg in range(B * G):
                            mm = e.matmul(spare[bg // 4][:, bg % 4 * L:(bg % 4 + 1) * L], bq[:, bg % G, :], kcT[:, bg, :],
                                          start=True, stop=True)
                        mm.then_inc(bias_made, 1)

            @block.scalar
            def _(e):
                done = lambda ins: ins.then_inc(setup_act, 1)
                e.wait_ge(gamma_in, 16)
                norm.scalar(e)
                for ch in range(4):
                    e.wait_ge(setup_pe, START + 2 + ch)
                    done(e.activation(hidT[:, ch * BANK:(ch + 1) * BANK], bank(2 + ch % 2)[0:L, :], ACT.Silu, bias=hb[:]))
                for ch in range(4):
                    e.wait_ge(setup_pe, START + 6 + ch)
                    done(e.activation(wT[:, ch * BANK:(ch + 1) * BANK], bank(ch % 2)[0:L, :], ACT.Identity, bias=aw2_b[:]))
                e.copy(xr[:, 0], xT[:]).then_inc(x_high, 1)
                e.wait_ge(exp_asked, START + 1)
                e.activation(eT[:], eT[:], ACT.Exp).then_inc(exp_out, 1)
                for g in range(4):
                    e.wait_ge(setup_pe, START + 10 + g)
                    done(e.copy(w_tok[:, 4 * g:4 * g + 4, :].rearrange("p t l -> p (t l)"), bank(2 + g % 2)[:, 0:4 * L]))
                e.wait_ge(tok_asked, START + 1)
                e.activation(w_tok[:], w_tok[:], ACT.Exp).then_inc(tok_exped, 1)
                for g in range(4):
                    e.wait_ge(setup_pe, START + 14 + g)
                    done(e.copy(e_tok[:, 4 * g:4 * g + 4, :].rearrange("p t l -> p (t l)"), bank(2 + g % 2)[:, 0:4 * L]))
                e.wait_ge(setup_pe, START + 18)
                done(e.mul(u[:].rearrange("p b l -> p (b l)"), bank(0)[:, 0:B * L], gamma[:]))
                done(e.copy(wsum[:].rearrange("p b l -> p (b l)"), bank(1)[0:1, 0:B * L]))
                for i in range(3 * B * G // 4):
                    e.wait_ge(setup_pe, START + 19 + i)
                    what, bg = divmod(i, B * G // 4)
                    src = bank(i % 2)
                    if what == 0:
                        done(e.mul(kcT[:, 4 * bg:4 * bg + 4, :].rearrange("p g l -> p (g l)"), src[:, 0:4 * L], float(D) ** -0.5))
                    elif what == 1:
                        done(e.copy(vcT[:, 4 * bg:4 * bg + 4, :].rearrange("p g l -> p (g l)"), src[:, 0:4 * L]))
                    else:
                        done(e.copy(vc_full[:, 4 * bg * D:(4 * bg + 4) * D], src[0:L, :]))
                e.wait_ge(setup_act, START + 30)
                e.copy(vc[:, 0].rearrange("l g d -> l (g d)"), vc_full[:]).then_inc(v_high, 1)

            @block.vector
            def _(e):
                c = Chain(e, dve_chain)
                norm.vector(e)
                e.wait_ge(consts_in, 256)
                e.wait_ge(setup_pe, START + 1)
                c.then(e.tensor_copy(wa[:], bank(0)[:, 0:L]))
                e.tensor_tensor(hb[:], bank(1)[0:L, 0:1], aw1_b[:], ALU.add).then_inc(setup, 1)
                e.wait_ge(setup_act, START + 8)
                w3, e3 = (a[:].rearrange("l (b s) -> l b s", b=B) for a in (wT, eT))
                wide = lambda a: a.unsqueeze(2).to_broadcast([L, B, S])
                c.then(e.tensor_reduce(st[:, 0, :], w3, AX.X, ALU.max))
                c.then(e.tensor_tensor(e3, w3, wide(st[:, 0, :]), ALU.subtract))
                e.sem_inc(exp_asked, 1)
                e.wait_ge(exp_out, START + 1)
                c.then(e.tensor_reduce(st[:, 1, :], e3, AX.X, ALU.add))
                c.then(e.reciprocal(st[:, 2, :], st[:, 1, :]))
                c.then(e.tensor_scalar(st[:, 2, :], st[:, 2, :], 1.0 / (2 * L), None, ALU.mult))
                e.tensor_tensor(e3, e3, wide(st[:, 2, :]), ALU.mult).then_inc(setup, 1)
                wt = lambda a: a.unsqueeze(2).to_broadcast([P, NT, L])
                e.wait_ge(setup_act, START + 12)
                c.then(e.tensor_reduce(tk[:, 0, :], w_tok[:], AX.X, ALU.max))
                c.then(e.tensor_tensor(w_tok[:], w_tok[:], wt(tk[:, 0, :]), ALU.subtract))
                e.sem_inc(tok_asked, 1)
                e.wait_ge(tok_exped, START + 1)
                c.then(e.tensor_reduce(tk[:, 0, :], w_tok[:], AX.X, ALU.add))
                c.then(e.reciprocal(tk[:, 1, :], tk[:, 0, :]))
                c.then(e.tensor_scalar(tk[:, 1, :], tk[:, 1, :], 1.0 / (2 * S), None, ALU.mult))
                c.then(e.tensor_tensor(w_tok[:], w_tok[:], wt(tk[:, 1, :]), ALU.mult))
                e.wait_ge(setup_act, START + 16)
                e.tensor_tensor(w_tok[:], w_tok[:], e_tok[:], ALU.add).then_inc(setup, 1)
                e.wait_ge(x_high, START + 1)
                e.tensor_tensor(xr[:, 1], xT[:], xr[:, 0].bitcast(F32), ALU.subtract)
                e.wait_ge(bias_made, START + 1)
                e.wait_ge(setup_pool, START + 1)
                for i in range(4):
                    c.then(e.tensor_copy(rest[:, 4 * i:4 * i + 4, :].rearrange("p j l -> p (j l)"), spare[i][:, 0:4 * L]))
                for k in range(2):
                    c.then(e.tensor_copy(part16[:], rest[:]))
                    c.then(e.scalar_tensor_tensor(rest[:], part16[:], part[:, k:k + 1], rest[:], ALU.mult, ALU.add))
                c.then(e.tensor_copy(part16[:], rest[:]))
                c.then(e.tensor_copy(qbias[:, 0:B * G, :], part16[:]))
                e.wait_ge(v_high, START + 1)
                e.tensor_tensor(vc[:, 1].rearrange("l g d -> l (g d)"), vc_full[:],
                                vc[:, 0].rearrange("l g d -> l (g d)").bitcast(F32), ALU.subtract)

        with ExitStack() as late:
            m2 = Core(nc, late, "latm")
            wq_in = m2.sb("wq_in", [P, 2, QH, P])
            w1_in = m2.sb("w1_in", [P, 2, QH, FF2])
            wk = m2.sb("wk", [P, 2, 2, HL], F32R)
            share = m2.sb("share", [L, 2, 2, QH * FF2], F32R)
            vcg = m2.sb("vcg", [P, 2, QH, L])
            qb = m2.sb("qb", [P, 2, QH, L], BF16)
            top = m2.sb("top", [P, 2, QH])
            tot = m2.sb("tot", [P, 2, QH])
            sc = m2.sb("sc", [P, 2, HL])
            att = m2.sb("att", [P, 2, HL])
            vg = m2.sb("vg", [L, 2, D], F32R)
            attT = m2.sb("attT", [L, 2, 2, BANK], F32R)
            norm1 = m2.sb("norm1", [P, 2, TB])
            h1 = m2.sb("h1", [P, TB, FF2])
            h1sq = m2.sb("h1sq", [P, TB, FF2])
            h1T = m2.sb("h1T", [P, 2, S])
            res = m2.sb("res", [P, TB, D])
            names = ("wk_made wk_ready share_made share_ready vcg_ready qb_ready scores_ready topped shifted exped "
                     "vg_ready wk_high share_high attT_high "
                     "inv_ready weighted turned attT_ready z_ready squared added "
                     "tail_scale zz_ready zz_zeroed z_root h1_affine h1_ready h1_sq h1_sum h1_root h1_turned h1T_ready "
                     "closed zz_added res_ready res_affine res_out res_silu stored g2_scaled summed").split()
            s = {n: m2.sem(n) for n in names}
            wq_loaded = [m2.sem(f"wq_loaded{i}") for i in range(2)]
            w1_loaded = [m2.sem(f"w1_loaded{i}") for i in range(2)]
            m2.start()
            block = late.enter_context(nc.Block())
            z4 = ps_z[:, 0:HL]

            @block.sync
            def _(e):
                e.dma_start(wq_in[:, 0], io["wq_quads"][0]).then_inc(wq_loaded[0], 16)
                e.dma_start(w1_in[:, 0], io["w1_quads"][0]).then_inc(w1_loaded[0], 16)
                for b in range(B):
                    with e.Fori(0, G) as g:
                        for r in range(4):
                            quad_now, u1 = b * NQ + g * 4 + r, (r + 1) % 2
                            e.wait_ge(s["share_made"], START + quad_now * 2)
                            e.dma_start(wq_in[:, u1], io["wq_quads"][bass.ds(g * 4 + r + 1, 1)].rearrange("a p j i -> (a p) j i")).then_inc(wq_loaded[u1], 16)
                            e.dma_start(w1_in[:, u1], io["w1_quads"][bass.ds(g * 4 + r + 1, 1)].rearrange("a p j f -> (a p) j f")).then_inc(w1_loaded[u1], 16)
                for b in range(B):
                    e.wait_ge(s["res_out"], START + b + 1)
                    e.dma_start(io["out"][b].rearrange("(t p) d -> p t d", p=P), res[:]).then_inc(s["stored"], 16)
                    e.wait_ge(s["stored"], 16 * (b + 1))

            def next_of(b, g, r):
                return b * NQ + g * 4 + (r + 1), g * 4 + (r + 1), b * G + g + (r + 1) // 4, (r + 1) % 4

            @block.gpsimd
            def _(e):
                def prepare(quad, row, quarter, u):
                    nc.gpsimd.tensor_tensor(vcg[:, u], vcT[:, bass.ds(row, 1), :].to_broadcast([P, QH, L]),
                                            g1[:, bass.ds(quad, 1), :].rearrange("p a j -> p (a j)").unsqueeze(2).to_broadcast([P, QH, L]),
                                            ALU.mult).then_inc(s["vcg_ready"], 1)
                    nc.gpsimd.tensor_tensor(qb[:, u], qbias[:, bass.ds(row, 1), :].to_broadcast([P, QH, L]),
                                            quad_mask[:, quarter, :].unsqueeze(2).to_broadcast([P, QH, L]),
                                            ALU.mult).then_inc(s["qb_ready"], 1)

                def weight(k, u, b, turned):
                    e.wait_ge(s["inv_ready"], START + b * (NS + 2) + k + 1)
                    e.wait_ge(s["turned"], START + turned)
                    nc.gpsimd.tensor_tensor(
                        att[:, u].rearrange("p (j l) -> p j l", j=QH), sc[:, u].rearrange("p (j l) -> p j l", j=QH),
                        tot[:, u].unsqueeze(2).to_broadcast([P, QH, L]), ALU.mult).then_inc(s["weighted"], 1)

                def add_squares(t, u, squares, added):
                    e.wait_ge(s["squared"], START + squares)
                    e.wait_ge(s["zz_added"], START + added)
                    nc.gpsimd.tensor_tensor(zz[:, t], zz[:, t], zsq[:, u], ALU.add).then_inc(s["zz_added"], 1)

                prepare(0, 0, 0, 0)
                for b in range(B):
                    for k in range(2):
                        weight(k, k, b, b * (NS + 1))
                    with e.Fori(0, G) as g:
                        for r in range(4):
                            for t in range(TB):
                                k = g * 4 * TB + (r * TB + t)
                                weight(k + 2, t % 2, b, b * (NS + 1) + k + 1)
                                add_squares((t - 1) % TB, (t - 1) % 2, b * NS + k, b * (NS + 1) + k)
                                if t == 0:
                                    quad_next, quad, row, quarter = next_of(b, g, r)
                                    e.wait_ge(s["share_made"], START + quad_next * 2)
                                    e.wait_ge(s["scores_ready"], START + b * (NS + 2) + k + 1)
                                    prepare(quad, row, quarter, (r + 1) % 2)
                    add_squares(TB - 1, 1, (b + 1) * NS, b * (NS + 1) + NS)
                    if b < B - 1:
                        e.wait_ge(s["zz_ready"], START + b + 1)
                        nc.gpsimd.memset(zz[:], 0.0).then_inc(s["zz_zeroed"], 1)
                        nc.gpsimd.memset(zsq[:, 1], 0.0).then_inc(s["zz_zeroed"], 1)
                        e.wait_ge(s["zz_zeroed"], START + 2 * (b + 1))

            @block.vector
            def _(e):
                c = Chain(e, s["tail_scale"])

                def shift(k, u, b, free):
                    done = b * (NS + 2) + k
                    e.wait_ge(s["scores_ready"], START + b * (NS + 2) + k + 1)
                    src = ps_s[:, u, 0:HL].rearrange("p (j l) -> p j l", j=QH)
                    e.tensor_reduce(top[:, u], src, AX.X, ALU.max).then_inc(s["topped"], 1)
                    e.wait_ge(s["topped"], START + done + 1)
                    e.wait_ge(s["weighted"], START + free)
                    e.tensor_tensor(sc[:, u].rearrange("p (j l) -> p j l", j=QH), src,
                                    top[:, u].unsqueeze(2).to_broadcast([P, QH, L]), ALU.subtract).then_inc(s["shifted"], 1)

                def total(k, u, b):
                    done = b * (NS + 2) + k
                    e.wait_ge(s["exped"], START + b * (NS + 2) + k + 1)
                    e.tensor_reduce(tot[:, u], sc[:, u].rearrange("p (j l) -> p j l", j=QH), AX.X, ALU.add).then_inc(s["summed"], 1)
                    e.wait_ge(s["summed"], START + done + 1)
                    e.reciprocal(tot[:, u], tot[:, u]).then_inc(s["inv_ready"], 1)

                def low(dst, src, high, made, high_sem, ready):
                    e.wait_ge(s[high_sem], START + made)
                    e.tensor_tensor(dst, src, high.bitcast(F32), ALU.subtract).then_inc(s[ready], 1)

                def low_wk(quads, u):
                    low(wk[:, u, 1], z4, wk[:, u, 0], quads, "wk_high", "wk_ready")

                def low_share(halves, half, u):
                    cols = slice(half * BANK, (half + 1) * BANK)
                    low(share[:, u, 1, cols], ps_z[0:L, :], share[:, u, 0, cols], halves, "share_high", "share_ready")

                low_wk(1, 0)
                for half in range(2):
                    low_share(half + 1, half, 0)
                for b in range(B):
                    for k in range(2):
                        shift(k, k, b, b * (NS + 2))
                        total(k, k, b)
                    low(attT[:, 0, 1], ps_t[0:L, :], attT[:, 0, 0], b * (NS + 1) + 1, "attT_high", "attT_ready")
                    with e.Fori(0, G) as g:
                        for r in range(4):
                            for t in range(TB):
                                k = g * 4 * TB + (r * TB + t)
                                quad_next = b * NQ + g * 4 + (r + 1)
                                shift(k + 2, t % 2, b, b * (NS + 2) + k + 1)
                                if t == 3:
                                    low_wk(quad_next + 1, (r + 1) % 2)
                                if t in (4, 5):
                                    low_share(quad_next * 2 + (t - 3), t - 4, (r + 1) % 2)
                                total(k + 2, t % 2, b)
                                low(attT[:, (t + 1) % 2, 1], ps_t[0:L, :], attT[:, (t + 1) % 2, 0],
                                    b * (NS + 1) + k + 2, "attT_high", "attT_ready")
                    e.wait_ge(s["z_root"], START + b + 1)
                    c.then(e.tensor_scalar(norm1[:, 1], norm1[:, 1], 1e-12, None, ALU.max))
                    c.then(e.reciprocal(norm1[:, 1], norm1[:, 1]))
                    c.then(e.tensor_scalar(norm1[:, 1], norm1[:, 1], float(G * GH * D) ** 0.5, None, ALU.mult))
                    e.wait_ge(s["h1_turned"], START + 4 * b)
                    e.wait_ge(s["closed"], START + TB // 2 * (b + 1))
                    for t in range(TB):
                        last = e.scalar_tensor_tensor(h1[:, t], ps_h[:, t], norm1[:, 1, t:t + 1], b1[:], ALU.mult, ALU.add)
                    last.then_inc(s["h1_affine"], 1)
                    e.wait_ge(s["h1_sq"], START + b + 1)
                    e.tensor_reduce(norm1[:, 0], h1sq[:], AX.X, ALU.add).then_inc(s["h1_sum"], 1)
                    if b == 0:
                        e.tensor_tensor(w2[:], w2[:], g2[:].unsqueeze(2).to_broadcast([P, 2, D]), ALU.mult).then_inc(s["g2_scaled"], 1)
                    e.wait_ge(s["h1_root"], START + b + 1)
                    c.then(e.tensor_scalar(norm1[:, 1], norm1[:, 1], 1e-12, None, ALU.max))
                    c.then(e.reciprocal(norm1[:, 1], norm1[:, 1]))
                    c.then(e.tensor_scalar(norm1[:, 1], norm1[:, 1], float(FF2) ** 0.5, None, ALU.mult))
                    e.wait_ge(s["stored"], 16 * b)
                    e.wait_ge(s["res_ready"], START + b + 1)
                    for t in range(TB):
                        last = e.scalar_tensor_tensor(res[:, t], ps_s[:, t // 4, t % 4 * D:(t % 4 + 1) * D],
                                                      norm1[:, 1, t:t + 1], b2[:], ALU.mult, ALU.add)
                    last.then_inc(s["res_affine"], 1)
                    e.wait_ge(s["res_silu"], START + b + 1)
                    e.tensor_tensor(res[:], res[:], h[:, b * TB:(b + 1) * TB, :], ALU.add).then_inc(s["res_out"], 1)

            @block.scalar
            def _(e):
                def exponentials(k, u, b):
                    e.wait_ge(s["shifted"], START + b * (NS + 2) + k + 1)
                    e.activation(sc[:, u], sc[:, u], ACT.Exp).then_inc(s["exped"], 1)

                def keep_wk(quad_next, u, used):
                    e.wait_ge(s["wk_made"], START + quad_next + 1)
                    e.wait_ge(s["scores_ready"], START + used)
                    e.copy(wk[:, u, 0], z4).then_inc(s["wk_high"], 1)

                def keep_share(quad_next, half, u, used):
                    e.wait_ge(s["share_made"], START + quad_next * 2 + (half + 1))
                    e.wait_ge(s["added"], START + used)
                    e.copy(share[:, u, 0, half * BANK:(half + 1) * BANK], ps_z[0:L, :]).then_inc(s["share_high"], 1)

                def high(k, u, b, used):
                    e.wait_ge(s["turned"], START + b * (NS + 1) + k + 1)
                    e.wait_ge(s["z_ready"], START + used)
                    e.copy(attT[:, u, 0], ps_t[0:L, :]).then_inc(s["attT_high"], 1)

                def square(k, u, b):
                    e.wait_ge(s["z_ready"], START + b * NS + k + 1)
                    e.wait_ge(s["zz_added"], START + b * (NS + 1) + k)
                    e.activation(zsq[:, u], ps_z[:], ACT.Square).then_inc(s["squared"], 1)

                keep_wk(0, 0, 0)
                for half in range(2):
                    keep_share(0, half, 0, 0)
                for b in range(B):
                    exponentials(0, 0, b)
                    exponentials(1, 1, b)
                    high(0, 0, b, b * NS)
                    with e.Fori(0, G) as g:
                        for r in range(4):
                            for t in range(TB):
                                k = g * 4 * TB + (r * TB + t)
                                n = b * NS + k
                                quad_next = b * NQ + g * 4 + (r + 1)
                                if r == 0 and t == 0:
                                    e.copy(vg[:], vc[:, :, bass.ds(b * G + g, 1), :].rearrange("l i a d -> l i (a d)")).then_inc(s["vg_ready"], 1)
                                if t == 3:
                                    keep_wk(quad_next, (r + 1) % 2, b * (NS + 2) + k)
                                if t in (4, 5):
                                    keep_share(quad_next, t - 4, (r + 1) % 2, n)
                                exponentials(k + 2, t % 2, b)
                                high(k + 1, (t + 1) % 2, b, n)
                                square(k, t % 2, b)
                    e.wait_ge(s["zz_ready"], START + b + 1)
                    e.activation(norm1[:, 1], ps_z[:, 0:TB], ACT.Sqrt).then_inc(s["z_root"], 1)
                    e.wait_ge(s["h1_affine"], START + b + 1)
                    e.activation(h1[:], h1[:], ACT.Silu).then_inc(s["h1_ready"], 1)
                    e.wait_ge(s["h1_ready"], START + b + 1)
                    e.activation(h1sq[:], h1[:], ACT.Square).then_inc(s["h1_sq"], 1)
                    e.wait_ge(s["h1_sum"], START + b + 1)
                    e.activation(norm1[:, 1], norm1[:, 0], ACT.Sqrt).then_inc(s["h1_root"], 1)
                    for i in range(4):
                        e.wait_ge(s["h1_turned"], START + 4 * b + i + 1)
                        e.wait_ge(s["res_ready"], START + b)
                        e.copy(h1T[:, i // 2, i % 2 * BANK:(i % 2 + 1) * BANK], ps_t[:] if i % 2 == 0 else ps_z[:]).then_inc(s["h1T_ready"], 1)
                    e.wait_ge(s["res_affine"], START + b + 1)
                    e.activation(res[:], res[:], ACT.Silu).then_inc(s["res_silu"], 1)

            @block.tensor
            def _(e):
                def scores_of(dst, tile, u):
                    for i, (x_part, w_part) in enumerate(PARTS):
                        e.matmul(dst, xr[:, x_part, tile * P:(tile + 1) * P], wk[:, u, w_part], start=(i == 0), stop=False)

                def first_scores(t, b):
                    scores_of(ps_s[:, t % 2, 0:HL], b * TB + t, 0)
                    e.matmul(ps_s[:, t % 2, 0:HL], ones16[:], qb[:, 0].rearrange("p j l -> p (j l)"), start=False,
                             stop=True).then_inc(s["scores_ready"], 1)

                def make_wk(quad_next, quarter_load, row, u):
                    e.wait_ge(wq_loaded[u], quarter_load)
                    for j in range(QH):
                        mm = e.matmul(ps_z[:, j * L:(j + 1) * L], wq_in[:, u, j, :], kcT[:, bass.ds(row, 1), :].rearrange("p a l -> p (a l)"),
                                      start=True, stop=True)
                    mm.then_inc(s["wk_made"], 1)

                def make_share(quad_next, half, load, u):
                    e.wait_ge(w1_loaded[u], load)
                    e.wait_ge(s["vcg_ready"], START + quad_next + 1)
                    for j in range(2):
                        mm = e.matmul(ps_z[0:L, j * FF2:(j + 1) * FF2], vcg[:, u, 2 * half + j, :], w1_in[:, u, 2 * half + j, :],
                                      start=True, stop=True)
                    mm.then_inc(s["share_made"], 1)

                def turn(k, u, b):
                    e.wait_ge(s["weighted"], START + b * (NS + 2) + k + 1)
                    e.wait_ge(s["attT_ready"], START + b * (NS + 1) + k)
                    for j in range(QH):
                        mm = e.transpose(ps_t[0:L, j * P:(j + 1) * P], att[:, u, j * L:(j + 1) * L], ident[:])
                    mm.then_inc(s["turned"], 1)

                make_wk(0, 16, 0, 0)
                for half in range(2):
                    e.wait_ge(s["wk_ready"], START + 1)
                    e.wait_ge(s["share_ready"], START + half)
                    make_share(0, half, 16, 0)
                for b in range(B):
                    e.wait_ge(s["wk_ready"], START + b * NQ + 1)
                    e.wait_ge(s["qb_ready"], START + b * NQ + 1)
                    e.wait_ge(s["h1_affine"], START + b)
                    e.wait_ge(s["h1T_ready"], START + 4 * b)
                    e.wait_ge(s["res_affine"], START + b)
                    for i in range(TB // 2):
                        e.matmul(ps_h[:, 2 * i:2 * i + 2].rearrange("p t f -> p (t f)"), zero[:, 0:P], zero[:],
                                 start=True, stop=False, skip_group_check=True)
                    first_scores(0, b)
                    first_scores(1, b)
                    turn(0, 0, b)
                    with e.Fori(0, G) as g:
                        for r in range(4):
                            quad_next, _, row, _ = next_of(b, g, r)
                            load = (g * 2 + (b * (NQ // 2) + (r + 1) // 2 + 1)) * 16
                            u, u1 = r % 2, (r + 1) % 2
                            for t in range(TB):
                                k = g * 4 * TB + (r * TB + t)
                                n = b * NS + k
                                if t == 6:
                                    e.wait_ge(s["wk_ready"], START + quad_next + 1)
                                    e.wait_ge(s["qb_ready"], START + quad_next + 1)
                                e.wait_ge(s["shifted"], START + b * (NS + 2) + k + 1)
                                t2, u2 = (t + 2) % TB, (u if t < 6 else u1)
                                scores_of(ps_s[:, t % 2, 0:HL], b * TB + t2, u2)
                                e.matmul(ps_s[:, t % 2, 0:HL], ones16[:], qb[:, u2].rearrange("p j l -> p (j l)"),
                                         start=False, stop=True).then_inc(s["scores_ready"], 1)
                                e.wait_ge(s["attT_high"], START + b * (NS + 1) + k + 1)
                                if t == 0:
                                    e.wait_ge(s["share_ready"], START + quad_next * 2)
                                for a_part, w_part in ((0, 0), (0, 1), (1, 0)):
                                    if a_part == 1:
                                        e.wait_ge(s["attT_ready"], START + b * (NS + 1) + k + 1)
                                    for j in range(QH):
                                        if (a_part, w_part, j) == (0, 0, 2) and t in (3, 4, 5):
                                            e.wait_ge(s["squared"], START + n)
                                            if t == 3:
                                                make_wk(quad_next, load, row, u1)
                                            else:
                                                make_share(quad_next, t - 4, load, u1)
                                        mm = e.matmul(ps_h[:, t, :], attT[:, t % 2, a_part, j * P:(j + 1) * P],
                                                      share[:, u, w_part, j * FF2:(j + 1) * FF2],
                                                      start=False, stop=False, skip_group_check=True)
                                mm.then_inc(s["added"], 1)
                                turn(k + 1, (t + 1) % 2, b)
                                e.wait_ge(s["squared"], START + n)
                                if t == 3:
                                    e.wait_ge(s["wk_ready"], START + quad_next + 1)
                                if t in (4, 5):
                                    e.wait_ge(s["share_ready"], START + quad_next * 2 + (t - 3))
                                if r == 0 and t == 0:
                                    e.wait_ge(s["vg_ready"], START + b * G + g + 1)
                                for i, (v_part, a_part) in enumerate(PARTS):
                                    mm = e.matmul(ps_z[:], vg[:, v_part], attT[:, t % 2, a_part], start=(i == 0), stop=(i == 2))
                                mm.then_inc(s["z_ready"], 1)
                    for i in range(TB // 2):
                        e.matmul(ps_h[:, 2 * i:2 * i + 2].rearrange("p t f -> p (t f)"), zero[:, 0:P], zero[:],
                                 start=False, stop=True, skip_group_check=True).then_inc(s["closed"], 1)
                    e.wait_ge(s["zz_added"], START + (b + 1) * (NS + 1))
                    e.wait_ge(s["squared"], START + (b + 1) * NS)
                    for t in range(TB):
                        for j in range(QH):
                            mm = e.matmul(ps_z[:, t:t + 1], zz[:, t, j * P:(j + 1) * P], ones[:], start=(j == 0), stop=(j == QH - 1))
                    mm.then_inc(s["zz_ready"], 1)
                    e.wait_ge(s["h1_ready"], START + b + 1)
                    e.wait_ge(s["attT_ready"], START + (b + 1) * (NS + 1))
                    for i in range(4):
                        dst = ps_t if i % 2 == 0 else ps_z
                        if i >= 2:
                            e.wait_ge(s["h1T_ready"], START + 4 * b + i - 1)
                        for j in range(4):
                            t = i % 2 * 4 + j
                            mm = e.transpose(dst[:, j * P:(j + 1) * P], h1[:, t, i // 2 * P:(i // 2 + 1) * P], ident[:])
                        mm.then_inc(s["h1_turned"], 1)
                    e.wait_ge(s["h1T_ready"], START + 4 * b + 4)
                    e.wait_ge(s["g2_scaled"], START + 1)
                    e.wait_ge(s["shifted"], START + (b + 1) * (NS + 2))
                    for t in range(TB):
                        for i in range(2):
                            mm = e.matmul(ps_s[:, t // 4, t % 4 * D:(t % 4 + 1) * D], h1T[:, i, t * P:(t + 1) * P], w2[:, i, :],
                                          start=(i == 0), stop=(i == 1))
                    mm.then_inc(s["res_ready"], 1)


PHASES = [embed, retention, experts, attention, latent]


def build(nc, io, phases=PHASES):
    with ExitStack() as ctx:
        sb = lambda name, shape: ctx.enter_context(nc.sbuf_tensor(name, shape, F32))
        keep = {"h": sb("h", [P, NT, D]), "ident": sb("ident", [P, P]), "xT": sb("xT", [P, B * S])}
        for phase in phases:
            phase(nc, io, keep)


def layout(inputs):
    f = {k: np.ascontiguousarray(v) for k, v in inputs.items()}
    a = {}
    x = f["x"]
    pad = np.zeros((B, S + 3), x.dtype)
    pad[:, 2:S + 2] = x
    a["tok"] = np.stack([pad[:, k:k + S].reshape(NT, P).T for k in range(4)], axis=1)
    ok = np.ones((B, S, 3), np.float32)
    for n, (first, last) in enumerate(((1, 0), (1, 1), (2, 1))):
        ok[:, :first, n] = 0
        if last:
            ok[:, S - last:, n] = 0
    a["tok_mask"] = ok.reshape(NT, P, 3).transpose(1, 0, 2)
    a["ident"] = np.eye(P, dtype=np.float32)
    for n in (2, 3, 4):
        a[f"emb_{n}"] = f[f"L0_tok_emb_{n}"]
    a["proj_wT"] = f["L0_tok_proj_w"].T.reshape(3, P, D).transpose(1, 0, 2)
    a["proj_b"] = f["L0_tok_proj_b"]
    swap = np.arange(D) ^ 1
    for name, key in (("WQ", "L0_attn_W_Q"), ("WK", "L0_attn_W_K")):
        w = f[key].transpose(1, 0, 2).reshape(D, D)
        a[name], a[name + "_rot"] = w, w[:, swap]
    a["WVG"] = np.concatenate([f["L0_attn_W_V"].transpose(1, 0, 2).reshape(D, D), f["L0_attn_W_G"]], axis=1)
    a["WO_0"] = f["L0_attn_W_O"]
    a["gn_w"], a["gn_b"] = f["L0_attn_gn_weight"], f["L0_attn_gn_bias"]
    of_head = (np.arange(D)[:, None] // DH == np.arange(H)[None, :]).astype(np.float32)
    a["heads_mask"], a["heads_row"] = np.pad(of_head, ((0, 0), (0, 1))), of_head.T
    part_of = np.array(SCORE_PARTS)[np.arange(P) // DH]
    same = (np.arange(D)[:, None] % DH == np.arange(P)[None, :] % DH)
    a["pattern"] = np.stack([same & (part_of[None, :, which] == part) for which in range(2) for part in range(3)],
                            axis=1).astype(np.float32)
    a["log_gamma"] = np.log(np.append(GAMMAS, 1.0).astype(np.float64)).astype(np.float32)
    pos = np.arange(S, dtype=np.float32)
    pair = (np.arange(D) % DH) // 2
    base = (2.0 * pair + 0.4 * DH) / (1.4 * DH)
    power = base[:, None] ** (pos[None, :] / 128.0)
    inv_freq = (1.0 / 10000.0 ** (np.arange(DH // 2, dtype=np.float32) / np.float32(DH // 2))).astype(np.float32)
    angle = (pos[None, :] * inv_freq[pair][:, None]).astype(np.float32).astype(np.float64)
    sign = np.where(np.arange(D) % 2 == 0, -1.0, 1.0)[:, None]
    for name, scale in (("xpos_q", power), ("xpos_k", 1.0 / power)):
        a[name] = np.stack([np.cos(angle) * scale, sign * np.sin(angle) * scale], axis=1).astype(np.float32)
    a["Wr"], a["br"] = f["L0_ffn_Wr"].T, f["L0_ffn_br"]
    a["rank"] = (E - np.arange(E)).astype(np.float32)
    a["W1"] = f["L0_ffn_W1"].transpose(1, 0, 2)
    a["b1"] = f["L0_ffn_b1"].reshape(E, 2, P).transpose(2, 0, 1)
    a["W2"] = f["L0_ffn_W2"].reshape(E, 2, P, D).transpose(2, 0, 1, 3)
    a["b2"] = f["L0_ffn_b2"]
    wrap = lambda w: np.concatenate([w, w[:1]])
    a["Wqk"] = wrap(np.stack([f["L1_attn_Wq"], f["L1_attn_Wk"]], axis=1)).transpose(2, 0, 1, 3)
    a["Wv"] = wrap(f["L1_attn_Wv"]).transpose(1, 0, 2)
    a["Wo"] = f["L1_attn_Wo"].reshape(H, D, D).transpose(1, 0, 2)
    a["bqk"] = np.stack([wrap(f["L1_attn_bq"]).T, wrap(f["L1_attn_bk"]).T], axis=1)
    a["bv"] = wrap(f["L1_attn_bv"])
    a["gamma"] = f["L1_ffn_gamma_norm"].reshape(D, 1)
    wkv = f["L1_ffn_Wkv_w"]
    a["Wkv"], a["bkv"] = wkv, f["L1_ffn_Wkv_b"].reshape(1, -1)
    a["WkT"] = wkv[:, :G * D].T.reshape(G, D, D).transpose(1, 0, 2)
    a["aw1"] = f["L1_ffn_aw1_w"].reshape(G, D, L).transpose(1, 0, 2)
    a["bk"] = f["L1_ffn_Wkv_b"][:G * D].reshape(G, D).T
    a["aw1_b"], a["aw2"], a["aw2_b"] = f["L1_ffn_aw1_b"].reshape(L, 1), f["L1_ffn_aw2_w"], f["L1_ffn_aw2_b"].reshape(L, 1)
    bq = np.zeros((D, G, P), np.float32)
    for k in range(3):
        bq[:, :, 32 * k:32 * k + GH] = f["L1_ffn_Wq_b"].reshape(G, GH, D).transpose(2, 0, 1)
    a["bq_parts"] = bq
    a["g1"] = f["L1_ffn_wz_g1"].reshape(NQ, QH, D).transpose(2, 0, 1)
    a["g1"] = np.concatenate([a["g1"], a["g1"][:, :1]], axis=1)
    row = np.arange(P)
    a["quad_mask"] = ((row[:, None, None] % 32 == 4 * np.arange(4)[None, :, None] + np.arange(QH)[None, None, :])
                      & (row[:, None, None] < 96)).astype(np.float32)
    a["part"] = -np.stack([(row >= 32).astype(np.float32), (row >= 64).astype(np.float32)], axis=1)
    quads = f["L1_ffn_Wq_w"].T.reshape(NQ, QH, D, D).transpose(0, 2, 1, 3)
    a["wq_quads"] = np.concatenate([quads, quads[:1]])
    quads = f["L1_ffn_wz_w1"].reshape(NQ, QH, D, FF2).transpose(0, 2, 1, 3)
    a["w1_quads"] = np.concatenate([quads, quads[:1]])
    a["wz_b1"], a["wz_b2"] = f["L1_ffn_wz_b1"], f["L1_ffn_wz_b2"]
    a["w2"] = f["L1_ffn_wz_w2"].reshape(2, P, D).transpose(1, 0, 2)
    a["g2"] = f["L1_ffn_wz_g2"].reshape(2, P).T
    return {k: np.ascontiguousarray(v) for k, v in a.items()}


def kernel(**inputs):
    import concourse.bacc as bacc
    from concourse.bass_utils import run_bass_kernel_spmd

    nc = bacc.Bacc("TRN2", target_bir_lowering=False, num_devices=1)
    arrays = layout(inputs)
    io = {name: nc.dram_tensor(f"in_{name}", a.shape, mybir.dt.from_np(a.dtype), kind="ExternalInput").ap()
          for name, a in arrays.items()}
    io["out"] = nc.dram_tensor("out", (B, S, D), F32, kind="ExternalOutput").ap()
    build(nc, io)
    r = run_bass_kernel_spmd(nc, [{f"in_{name}": a for name, a in arrays.items()}], core_ids=[0])
    return r.results[0]["out"]
```
